# Optimizing a Trainium2 kernel written in Bass

```python
import numpy as np
import jax
import jax.numpy as jnp

def _softmax(x, axis=-1):
    return jax.nn.softmax(x, axis=axis)

def _gelu(x):
    return jax.nn.gelu(x, approximate=True)

def _silu(x):
    return jax.nn.silu(x)

def _sigmoid(x):
    return jax.nn.sigmoid(x)

def _layernorm(x, axis=-1, eps=1e-05):
    m = jnp.mean(x, axis=axis, keepdims=True)
    v = jnp.var(x, axis=axis, keepdims=True)
    return (x - m) / jnp.sqrt(v + eps)

def _scatter_add(tgt, idx, src, axis=0):
    return tgt.at[idx].add(src)

def _segment_sum(src, seg, n):
    return jax.ops.segment_sum(src, seg, n)
kernel_name = 'mk_adaln_attn_ffn_d2_seqx_r8_703072'

def setup_inputs(seed: int=0):
    np.random.seed(seed)
    _w = jnp.asarray

    def _rec_inputs():
        import jax
        import jax.numpy as jnp
        _rk = jax.random.key(seed)
        x = -0.000125 + 0.9999 * jax.random.normal(jax.random.fold_in(_rk, 1), (32, 128, 128), jnp.float32)
        _lenS = 128 - jax.random.randint(jax.random.fold_in(_rk, 7), (32,), 0, max(1, 128 // 4) + 1, jnp.int32)
        _lenS2 = 128 - jax.random.randint(jax.random.fold_in(_rk, 8), (32,), 0, max(1, 128 // 4) + 1, jnp.int32)
        cond_1024 = 0.00513981 + 1.0024 * jax.random.normal(jax.random.fold_in(_rk, 11), (32, 128), jnp.float32)
        return (x, cond_1024)
    x, cond_1024 = _rec_inputs()

    def _L0_cond_setup():
        import jax, jax.numpy as jnp
        import numpy as np
        IN_FEATURES = 128
        OUT_FEATURES = 128
        BATCH = 32
        SEQ = 128
        EPS = 1e-08
        key = jax.random.key(seed)
        k1, k2, k3 = jax.random.split(key, 3)
        Efou = jax.random.normal(k1, (BATCH, SEQ, IN_FEATURES), dtype=jnp.float32)
        y = jax.random.normal(k2, (BATCH, IN_FEATURES), dtype=jnp.float32)
        weight = jax.random.normal(k3, (IN_FEATURES, OUT_FEATURES), dtype=jnp.float32)
        return {'Efou': Efou, 'y': y, 'weight': weight}
    _L0_cond_all = _L0_cond_setup()
    _L0_cond_in = {k: v for k, v in _L0_cond_all.items() if k in ('weight',)}
    del _L0_cond_all

    def _L0_attn_setup():
        import jax, jax.numpy as jnp
        import numpy as np
        B, L, IN_DIM = (4, 256, 128)
        H, D = (16, 64)
        OUT_DIM = 128
        key = jax.random.key(seed)
        k1, k2, k3 = jax.random.split(key, 3)
        inputs = jax.random.normal(k1, (B, L, IN_DIM), dtype=jnp.float32)
        W_qkv = jax.random.normal(k2, (IN_DIM, 3 * H * D), dtype=jnp.float32) * IN_DIM ** (-0.5)
        W_out = jax.random.normal(k3, (H * D, OUT_DIM), dtype=jnp.float32) * (H * D) ** (-0.5)
        return {'inputs': inputs, 'W_qkv': W_qkv, 'W_out': W_out}
    _L0_attn_all = _L0_attn_setup()
    _L0_attn_in = {k: v for k, v in _L0_attn_all.items() if k in ('W_qkv', 'W_out')}
    del _L0_attn_all

    def _L0_cond2_setup():
        import jax, jax.numpy as jnp
        import numpy as np
        EPS = 1e-08
        key = jax.random.key(seed)
        ks = jax.random.split(key, 8)
        B, S, D, H = (8, 256, 128, 128)
        scale = 1.0 / np.sqrt(D)
        return {'input_seq': jax.random.normal(ks[0], (B, S, D), dtype=jnp.float32), 'initial_hidden': jax.random.normal(ks[1], (B, H), dtype=jnp.float32), 'W_f': jax.random.normal(ks[2], (H, D), dtype=jnp.float32) * scale, 'b_f': jnp.zeros((H,), dtype=jnp.float32), 'W_i': jax.random.normal(ks[3], (H, D), dtype=jnp.float32) * scale, 'b_i': jnp.zeros((H,), dtype=jnp.float32), 'W_h': jax.random.normal(ks[4], (H, D), dtype=jnp.float32) * scale, 'b_h': jnp.zeros((H,), dtype=jnp.float32)}
    _L0_cond2_all = _L0_cond2_setup()
    _L0_cond2_in = {k: v for k, v in _L0_cond2_all.items() if k in ('W_f', 'b_f', 'W_i', 'b_i', 'W_h', 'b_h')}
    del _L0_cond2_all

    def _L0_ffn_setup():
        import jax, jax.numpy as jnp
        import numpy as np
        B, S, DIM = (4, 512, 128)
        BASE_COUPLING = 0.1
        NUM_CYCLES = 3

        def _gelu(x):
            return jax.nn.gelu(x, approximate=False)

        def _coupling_net(h, w1, b1, w2, b2, w3, b3, w4, b4):
            h = _gelu(h @ w1 + b1)
            h = _gelu(h @ w2 + b2)
            h = _gelu(h @ w3 + b3)
            return jax.nn.sigmoid(h @ w4 + b4)

        def _global_net(h, w1, b1, w2, b2, w3, b3):
            h = _gelu(h @ w1 + b1)
            h = _gelu(h @ w2 + b2)
            return jax.nn.sigmoid(h @ w3 + b3)

        def _twist(x):
            o_r, o_i, p_r, p_i = jnp.split(x, 4, axis=-1)
            return jnp.concatenate([p_r, -p_i, -o_r, o_i], axis=-1)
        key = jax.random.key(seed)
        ks = jax.random.split(key, 9)
        d = DIM

        def w(k, fan_in, fan_out):
            return jax.random.normal(k, (fan_in, fan_out), dtype=jnp.float32) / np.sqrt(fan_in).astype(np.float32)
        inp = {'x': jax.random.normal(ks[0], (B, S, d), dtype=jnp.float32)}
        cn_dims = [(d, d), (d, d // 2), (d // 2, d // 4), (d // 4, 1)]
        for i, (a, b) in enumerate(cn_dims):
            inp[f'cn_w{i + 1}'] = w(ks[1 + i], a, b)
            inp[f'cn_b{i + 1}'] = jnp.zeros((b,), dtype=jnp.float32)
        gc_dims = [(d, d // 2), (d // 2, d // 4), (d // 4, 1)]
        for i, (a, b) in enumerate(gc_dims):
            inp[f'gc_w{i + 1}'] = w(ks[5 + i], a, b)
            inp[f'gc_b{i + 1}'] = jnp.zeros((b,), dtype=jnp.float32)
        inp['adaptive_range'] = jnp.full((1,), 0.2, dtype=jnp.float32)
        return inp
    _L0_ffn_all = _L0_ffn_setup()
    _L0_ffn_in = {k: v for k, v in _L0_ffn_all.items() if k in ('cn_w1', 'cn_b1', 'cn_w2', 'cn_b2', 'cn_w3', 'cn_b3', 'cn_w4', 'cn_b4', 'gc_w1', 'gc_b1', 'gc_w2', 'gc_b2', 'gc_w3', 'gc_b3', 'adaptive_range')}
    del _L0_ffn_all

    def _L1_cond_setup():
        import jax, jax.numpy as jnp
        import numpy as np
        NUM_EXPERTS = 4
        TOP_K = 2
        key = jax.random.key(seed)
        ks = jax.random.split(key, 16)
        B, L, D, E, H = (8, 96, 128, NUM_EXPERTS, 512)
        s = 0.02
        return {'context_c': jax.random.normal(ks[0], (B, L, D), jnp.float32), 'time_cond': jax.random.normal(ks[1], (B, D), jnp.float32), 'gate_w': jax.random.normal(ks[2], (3 * D, E), jnp.float32) * s, 'gate_b': jnp.zeros((E,), jnp.float32), 'time_w': jax.random.normal(ks[3], (D, 2 * E), jnp.float32) * s, 'time_b': jnp.zeros((2 * E,), jnp.float32), 'ew1': jax.random.normal(ks[4], (E, D, H), jnp.float32) * s, 'eb1': jnp.zeros((E, H), jnp.float32), 'ew2': jax.random.normal(ks[5], (E, H, D), jnp.float32) * s, 'eb2': jnp.zeros((E, D), jnp.float32), 'sw1': jax.random.normal(ks[6], (D, H), jnp.float32) * s, 'sb1': jnp.zeros((H,), jnp.float32), 'sw2': jax.random.normal(ks[7], (H, D), jnp.float32) * s, 'sb2': jnp.zeros((D,), jnp.float32)}
    _L1_cond_all = _L1_cond_setup()
    _L1_cond_in = {k: v for k, v in _L1_cond_all.items() if k in ('gate_w', 'gate_b', 'time_w', 'time_b', 'ew1', 'eb1', 'ew2', 'eb2', 'sw1', 'sb1', 'sw2', 'sb2')}
    del _L1_cond_all

    def _L1_attn_setup():
        import jax, jax.numpy as jnp
        import numpy as np
        NUM_HEADS = 16
        NUM_UNITS = 128
        NEG = -2.0 ** 32 + 1.0
        EPS = 1e-08

        def _attention(x, Wq, bq, Wk, bk, Wv, bv, gamma, beta):
            B, T, C = x.shape
            H = NUM_HEADS
            U = NUM_UNITS
            dh = U // H
            Q = jax.nn.relu(x @ Wq + bq)
            K = jax.nn.relu(x @ Wk + bk)
            V = jax.nn.relu(x @ Wv + bv)
            Qh = Q.reshape(B, T, H, dh)
            Kh = K.reshape(B, T, H, dh)
            Vh = V.reshape(B, T, H, dh)
            scores = jnp.einsum('bqhd,bkhd->bhqk', Qh, Kh) / np.sqrt(dh)
            key_mask = jnp.sign(jnp.abs(jnp.sum(x, axis=-1)))
            scores = jnp.where(key_mask[:, None, None, :] == 0, NEG, scores)
            tril = jnp.tril(jnp.ones((T, T), dtype=scores.dtype))
            scores = jnp.where(tril[None, None, :, :] == 0, NEG, scores)
            attn = jax.nn.softmax(scores, axis=-1)
            query_mask = jnp.sign(jnp.abs(jnp.sum(x, axis=-1)))
            attn = attn * query_mask[:, None, :, None]
            out = jnp.einsum('bhqk,bkhd->bqhd', attn, Vh).reshape(B, T, U)
            out = out + x
            mean = jnp.mean(out, axis=-1, keepdims=True)
            var = jnp.mean((out - mean) ** 2, axis=-1, keepdims=True)
            normalized = (out - mean) / jnp.sqrt(var + EPS)
            return gamma * normalized + beta
        key = jax.random.key(seed)
        ks = jax.random.split(key, 8)
        B, T, C = (2, 256, 128)
        U = NUM_UNITS
        x = jax.random.normal(ks[0], (B, T, C), dtype=jnp.float32)
        s = 1.0 / np.sqrt(C)
        Wq = jax.random.normal(ks[1], (C, U), dtype=jnp.float32) * s
        Wk = jax.random.normal(ks[2], (C, U), dtype=jnp.float32) * s
        Wv = jax.random.normal(ks[3], (C, U), dtype=jnp.float32) * s
        bq = jnp.zeros((U,), dtype=jnp.float32)
        bk = jnp.zeros((U,), dtype=jnp.float32)
        bv = jnp.zeros((U,), dtype=jnp.float32)
        gamma = jnp.ones((U,), dtype=jnp.float32)
        beta = jnp.zeros((U,), dtype=jnp.float32)
        return {'x': x, 'Wq': Wq, 'bq': bq, 'Wk': Wk, 'bk': bk, 'Wv': Wv, 'bv': bv, 'gamma': gamma, 'beta': beta}
    _L1_attn_all = _L1_attn_setup()
    _L1_attn_in = {k: v for k, v in _L1_attn_all.items() if k in ('Wq', 'bq', 'Wk', 'bk', 'Wv', 'bv', 'gamma', 'beta')}
    del _L1_attn_all

    def _L1_cond2_setup():
        import jax, jax.numpy as jnp
        import numpy as np
        B, T, D = (128, 32, 128)
        ADA, INTER, RANK = (128, 128, 8)
        LN_EPS = 1e-05

        def _layernorm(x, g, b):
            mu = jnp.mean(x, axis=-1, keepdims=True)
            var = jnp.var(x, axis=-1, keepdims=True)
            return (x - mu) * jax.lax.rsqrt(var + LN_EPS) * g + b
        key = jax.random.key(seed)
        ks = jax.random.split(key, 9)
        return {'x': jax.random.normal(ks[0], (B, T, D), dtype=jnp.float32), 'ada_emb': jax.random.normal(ks[1], (B, ADA), dtype=jnp.float32), 'base_layer': jax.random.normal(ks[2], (D, D), dtype=jnp.float32), 'w1': jax.random.normal(ks[3], (ADA, INTER), dtype=jnp.float32) * 0.02, 'b1': jnp.zeros((INTER,), dtype=jnp.float32), 'w2': jax.random.normal(ks[4], (INTER, 2 * D * RANK), dtype=jnp.float32) * 0.02, 'b2': jnp.zeros((2 * D * RANK,), dtype=jnp.float32), 'ln_g': jnp.ones((ADA,), dtype=jnp.float32), 'ln_b': jnp.zeros((ADA,), dtype=jnp.float32)}
    _L1_cond2_all = _L1_cond2_setup()
    _L1_cond2_in = {k: v for k, v in _L1_cond2_all.items() if k in ('base_layer', 'w1', 'b1', 'w2', 'b2', 'ln_g', 'ln_b')}
    del _L1_cond2_all

    def _L1_ffn_setup():
        import jax, jax.numpy as jnp
        import numpy as np
        B, T, D = (8, 512, 128)
        NUM_SLOTS = 64
        TOP_K = 8
        DQ = D // 4
        DH = D // 2

        def _forward(x, slot_init, w1, b1, w2, b2, tau, Wih, Whh, bih, bhh, wq, bq, wk, bk, wv, bv, ln_g, ln_b, wvp, bvp, wo, bo):
            Bx, Tx, Dx = x.shape
            S = jnp.broadcast_to(slot_init[None], (Bx, NUM_SLOTS, Dx)).astype(x.dtype)
            slot_mean = jnp.broadcast_to(S.mean(axis=1, keepdims=True), (Bx, Tx, Dx))
            ctx = jnp.concatenate([x, slot_mean], axis=-1)
            h = jax.nn.gelu(ctx @ w1 + b1, approximate=False)
            route_logits = (h @ w2 + b2) / (jnp.abs(tau) + 0.1)
            topk_vals, topk_idx = jax.lax.top_k(route_logits, TOP_K)
            topk_w = jax.nn.softmax(topk_vals, axis=-1)
            alpha = (jax.nn.one_hot(topk_idx, NUM_SLOTS, dtype=x.dtype) * topk_w[..., None]).sum(axis=-2)
            slot_input = jnp.einsum('bts,btd->bsd', alpha, x)
            denom = alpha.sum(axis=1) + 1e-08
            si = slot_input / denom[..., None]
            gi = si @ Wih.T + bih
            gh = S @ Whh.T + bhh
            i_r, i_z, i_n = jnp.split(gi, 3, axis=-1)
            h_r, h_z, h_n = jnp.split(gh, 3, axis=-1)
            r = jax.nn.sigmoid(i_r + h_r)
            z = jax.nn.sigmoid(i_z + h_z)
            n = jnp.tanh(i_n + r * h_n)
            S_new = (1.0 - z) * n + z * S
            q = S_new @ wq + bq
            k = S_new @ wk + bk
            v = S_new @ wv + bv
            scale = DQ ** (-0.5)
            attn = jax.nn.softmax(jnp.einsum('bsq,btq->bst', q, k) * scale, axis=-1)
            S_comm = jnp.einsum('bst,btd->bsd', attn, v)
            y = S_new + S_comm
            mu = y.mean(axis=-1, keepdims=True)
            var = y.var(axis=-1, keepdims=True)
            y = (y - mu) * jax.lax.rsqrt(var + 1e-05) * ln_g + ln_b
            slot_values = y @ wvp + bvp
            out = jnp.einsum('bts,bsd->btd', alpha, slot_values)
            return out @ wo + bo
        key = jax.random.key(seed)
        ks = jax.random.split(key, 24)
        n = lambda k, shp, s=0.02: jax.random.normal(k, shp, dtype=jnp.float32) * s
        return {'x': jax.random.normal(ks[0], (B, T, D), dtype=jnp.float32), 'slot_init': n(ks[1], (NUM_SLOTS, D)), 'w1': n(ks[2], (2 * D, DH)), 'b1': jnp.zeros((DH,)), 'w2': n(ks[3], (DH, NUM_SLOTS)), 'b2': jnp.zeros((NUM_SLOTS,)), 'tau': jnp.ones((1,)), 'Wih': n(ks[4], (3 * D, D)), 'Whh': n(ks[5], (3 * D, D)), 'bih': jnp.zeros((3 * D,)), 'bhh': jnp.zeros((3 * D,)), 'wq': n(ks[6], (D, DQ)), 'bq': jnp.zeros((DQ,)), 'wk': n(ks[7], (D, DQ)), 'bk': jnp.zeros((DQ,)), 'wv': n(ks[8], (D, D)), 'bv': jnp.zeros((D,)), 'ln_g': jnp.ones((D,)), 'ln_b': jnp.zeros((D,)), 'wvp': n(ks[9], (D, D)), 'bvp': jnp.zeros((D,)), 'wo': n(ks[10], (D, D)), 'bo': jnp.zeros((D,))}
    _L1_ffn_all = _L1_ffn_setup()
    _L1_ffn_in = {k: v for k, v in _L1_ffn_all.items() if k in ('slot_init', 'w1', 'b1', 'w2', 'b2', 'tau', 'Wih', 'Whh', 'bih', 'bhh', 'wq', 'bq', 'wk', 'bk', 'wv', 'bv', 'ln_g', 'ln_b', 'wvp', 'bvp', 'wo', 'bo')}
    del _L1_ffn_all
    return {'x': x, 'cond_1024': cond_1024, 'L0_cond_weight': _L0_cond_in['weight'], 'L0_attn_W_qkv': _L0_attn_in['W_qkv'], 'L0_attn_W_out': _L0_attn_in['W_out'], 'L0_cond2_W_f': _L0_cond2_in['W_f'], 'L0_cond2_b_f': _L0_cond2_in['b_f'], 'L0_cond2_W_i': _L0_cond2_in['W_i'], 'L0_cond2_b_i': _L0_cond2_in['b_i'], 'L0_cond2_W_h': _L0_cond2_in['W_h'], 'L0_cond2_b_h': _L0_cond2_in['b_h'], 'L0_ffn_cn_w1': _L0_ffn_in['cn_w1'], 'L0_ffn_cn_b1': _L0_ffn_in['cn_b1'], 'L0_ffn_cn_w2': _L0_ffn_in['cn_w2'], 'L0_ffn_cn_b2': _L0_ffn_in['cn_b2'], 'L0_ffn_cn_w3': _L0_ffn_in['cn_w3'], 'L0_ffn_cn_b3': _L0_ffn_in['cn_b3'], 'L0_ffn_cn_w4': _L0_ffn_in['cn_w4'], 'L0_ffn_cn_b4': _L0_ffn_in['cn_b4'], 'L0_ffn_gc_w1': _L0_ffn_in['gc_w1'], 'L0_ffn_gc_b1': _L0_ffn_in['gc_b1'], 'L0_ffn_gc_w2': _L0_ffn_in['gc_w2'], 'L0_ffn_gc_b2': _L0_ffn_in['gc_b2'], 'L0_ffn_gc_w3': _L0_ffn_in['gc_w3'], 'L0_ffn_gc_b3': _L0_ffn_in['gc_b3'], 'L0_ffn_adaptive_range': _L0_ffn_in['adaptive_range'], 'L1_cond_gate_w': _L1_cond_in['gate_w'], 'L1_cond_gate_b': _L1_cond_in['gate_b'], 'L1_cond_time_w': _L1_cond_in['time_w'], 'L1_cond_time_b': _L1_cond_in['time_b'], 'L1_cond_ew1': _L1_cond_in['ew1'], 'L1_cond_eb1': _L1_cond_in['eb1'], 'L1_cond_ew2': _L1_cond_in['ew2'], 'L1_cond_eb2': _L1_cond_in['eb2'], 'L1_cond_sw1': _L1_cond_in['sw1'], 'L1_cond_sb1': _L1_cond_in['sb1'], 'L1_cond_sw2': _L1_cond_in['sw2'], 'L1_cond_sb2': _L1_cond_in['sb2'], 'L1_attn_Wq': _L1_attn_in['Wq'], 'L1_attn_bq': _L1_attn_in['bq'], 'L1_attn_Wk': _L1_attn_in['Wk'], 'L1_attn_bk': _L1_attn_in['bk'], 'L1_attn_Wv': _L1_attn_in['Wv'], 'L1_attn_bv': _L1_attn_in['bv'], 'L1_attn_gamma': _L1_attn_in['gamma'], 'L1_attn_beta': _L1_attn_in['beta'], 'L1_cond2_base_layer': _L1_cond2_in['base_layer'], 'L1_cond2_w1': _L1_cond2_in['w1'], 'L1_cond2_b1': _L1_cond2_in['b1'], 'L1_cond2_w2': _L1_cond2_in['w2'], 'L1_cond2_b2': _L1_cond2_in['b2'], 'L1_cond2_ln_g': _L1_cond2_in['ln_g'], 'L1_cond2_ln_b': _L1_cond2_in['ln_b'], 'L1_ffn_slot_init': _L1_ffn_in['slot_init'], 'L1_ffn_w1': _L1_ffn_in['w1'], 'L1_ffn_b1': _L1_ffn_in['b1'], 'L1_ffn_w2': _L1_ffn_in['w2'], 'L1_ffn_b2': _L1_ffn_in['b2'], 'L1_ffn_tau': _L1_ffn_in['tau'], 'L1_ffn_Wih': _L1_ffn_in['Wih'], 'L1_ffn_Whh': _L1_ffn_in['Whh'], 'L1_ffn_bih': _L1_ffn_in['bih'], 'L1_ffn_bhh': _L1_ffn_in['bhh'], 'L1_ffn_wq': _L1_ffn_in['wq'], 'L1_ffn_bq': _L1_ffn_in['bq'], 'L1_ffn_wk': _L1_ffn_in['wk'], 'L1_ffn_bk': _L1_ffn_in['bk'], 'L1_ffn_wv': _L1_ffn_in['wv'], 'L1_ffn_bv': _L1_ffn_in['bv'], 'L1_ffn_ln_g': _L1_ffn_in['ln_g'], 'L1_ffn_ln_b': _L1_ffn_in['ln_b'], 'L1_ffn_wvp': _L1_ffn_in['wvp'], 'L1_ffn_bvp': _L1_ffn_in['bvp'], 'L1_ffn_wo': _L1_ffn_in['wo'], 'L1_ffn_bo': _L1_ffn_in['bo']}

def reference(x, cond_1024, L0_cond_weight, L0_attn_W_qkv, L0_attn_W_out, L0_cond2_W_f, L0_cond2_b_f, L0_cond2_W_i, L0_cond2_b_i, L0_cond2_W_h, L0_cond2_b_h, L0_ffn_cn_w1, L0_ffn_cn_b1, L0_ffn_cn_w2, L0_ffn_cn_b2, L0_ffn_cn_w3, L0_ffn_cn_b3, L0_ffn_cn_w4, L0_ffn_cn_b4, L0_ffn_gc_w1, L0_ffn_gc_b1, L0_ffn_gc_w2, L0_ffn_gc_b2, L0_ffn_gc_w3, L0_ffn_gc_b3, L0_ffn_adaptive_range, L1_cond_gate_w, L1_cond_gate_b, L1_cond_time_w, L1_cond_time_b, L1_cond_ew1, L1_cond_eb1, L1_cond_ew2, L1_cond_eb2, L1_cond_sw1, L1_cond_sb1, L1_cond_sw2, L1_cond_sb2, L1_attn_Wq, L1_attn_bq, L1_attn_Wk, L1_attn_bk, L1_attn_Wv, L1_attn_bv, L1_attn_gamma, L1_attn_beta, L1_cond2_base_layer, L1_cond2_w1, L1_cond2_b1, L1_cond2_w2, L1_cond2_b2, L1_cond2_ln_g, L1_cond2_ln_b, L1_ffn_slot_init, L1_ffn_w1, L1_ffn_b1, L1_ffn_w2, L1_ffn_b2, L1_ffn_tau, L1_ffn_Wih, L1_ffn_Whh, L1_ffn_bih, L1_ffn_bhh, L1_ffn_wq, L1_ffn_bq, L1_ffn_wk, L1_ffn_bk, L1_ffn_wv, L1_ffn_bv, L1_ffn_ln_g, L1_ffn_ln_b, L1_ffn_wvp, L1_ffn_bvp, L1_ffn_wo, L1_ffn_bo):
    import jax
    import jax.numpy as jnp

    def _L0_cond_ref(Efou, y, weight):
        import jax, jax.numpy as jnp
        import numpy as np
        IN_FEATURES = 128
        OUT_FEATURES = 128
        BATCH = 32
        SEQ = 128
        EPS = 1e-08
        scale = 1.0 / np.sqrt(np.float32(weight.shape[0]))
        ys = y * scale
        d = jax.lax.rsqrt(jnp.einsum('bi,io->bo', ys * ys, weight * weight) + EPS)
        out = jnp.einsum('bsi,io->bso', Efou * ys[:, None, :], weight) * d[:, None, :]
        return out

    def _L0_attn_ref(inputs, W_qkv, W_out):
        import jax, jax.numpy as jnp
        import numpy as np
        B, L, IN_DIM = (4, 256, 128)
        H, D = (16, 64)
        OUT_DIM = 128
        b, l, _ = inputs.shape
        qkv = inputs @ W_qkv
        q, k, v = jnp.split(qkv, 3, axis=-1)
        q = q.reshape(b, l, H, D)
        k = k.reshape(b, l, H, D)
        v = v.reshape(b, l, H, D)
        score = jnp.einsum('bihd,bjhd->bijh', q, k) / D ** 0.5
        mask = jnp.tril(jnp.ones((l, l), dtype=score.dtype))[None, :, :, None]
        masked_score = score * mask + 1e+30 * (mask - 1.0)
        wmat = jax.nn.softmax(masked_score, axis=2)
        out = jnp.einsum('bijh,bjhd->bihd', wmat, v).reshape(b, l, H * D)
        return out @ W_out

    def _L0_cond2_ref(input_seq, initial_hidden, W_f, b_f, W_i, b_i, W_h, b_h):
        import jax, jax.numpy as jnp
        import numpy as np
        EPS = 1e-08
        forget_gate = jax.nn.sigmoid(jnp.einsum('bsd,hd->bsh', input_seq, W_f) + b_f)
        input_gate = jax.nn.sigmoid(jnp.einsum('bsd,hd->bsh', input_seq, W_i) + b_i)
        gate_sum = forget_gate + input_gate + EPS
        forget_norm = forget_gate / gate_sum
        input_norm = input_gate / gate_sum
        candidate = jnp.einsum('bsd,hd->bsh', input_seq, W_h) + b_h
        new_info = input_norm * candidate
        log_ret = jnp.log(forget_norm + EPS)
        log_cumprod = jnp.cumsum(log_ret, axis=1)
        B, _, H = log_cumprod.shape
        padded = jnp.concatenate([jnp.zeros((B, 1, H), dtype=log_cumprod.dtype), log_cumprod], axis=1)
        scaling = jnp.exp(log_cumprod[:, -1:, :] - padded[:, :-1, :])
        hidden = jnp.cumsum(scaling * new_info, axis=1)
        hidden = hidden + jnp.exp(log_cumprod) * initial_hidden[:, None, :]
        return hidden

    def _L0_ffn_ref(x, cn_w1, cn_b1, cn_w2, cn_b2, cn_w3, cn_b3, cn_w4, cn_b4, gc_w1, gc_b1, gc_w2, gc_b2, gc_w3, gc_b3, adaptive_range):
        import jax, jax.numpy as jnp
        import numpy as np
        B, S, DIM = (4, 512, 128)
        BASE_COUPLING = 0.1
        NUM_CYCLES = 3

        def _gelu(x):
            return jax.nn.gelu(x, approximate=False)

        def _coupling_net(h, w1, b1, w2, b2, w3, b3, w4, b4):
            h = _gelu(h @ w1 + b1)
            h = _gelu(h @ w2 + b2)
            h = _gelu(h @ w3 + b3)
            return jax.nn.sigmoid(h @ w4 + b4)

        def _global_net(h, w1, b1, w2, b2, w3, b3):
            h = _gelu(h @ w1 + b1)
            h = _gelu(h @ w2 + b2)
            return jax.nn.sigmoid(h @ w3 + b3)

        def _twist(x):
            o_r, o_i, p_r, p_i = jnp.split(x, 4, axis=-1)
            return jnp.concatenate([p_r, -p_i, -o_r, o_i], axis=-1)
        global_context = x.mean(axis=1, keepdims=True)
        gf = _global_net(global_context, gc_w1, gc_b1, gc_w2, gc_b2, gc_w3, gc_b3)
        out = x
        for _ in range(NUM_CYCLES):
            tf = _coupling_net(out, cn_w1, cn_b1, cn_w2, cn_b2, cn_w3, cn_b3, cn_w4, cn_b4)
            combined = 0.7 * gf + 0.3 * tf
            coupling = BASE_COUPLING + adaptive_range * (combined - 0.5) * 2.0
            out = out + coupling * _twist(out)
        return out

    def _L1_cond_ref(context_c, time_cond, gate_w, gate_b, time_w, time_b, ew1, eb1, ew2, eb2, sw1, sb1, sw2, sb2):
        import jax, jax.numpy as jnp
        import numpy as np
        NUM_EXPERTS = 4
        TOP_K = 2
        B, L, D = context_c.shape
        E, K = (NUM_EXPERTS, TOP_K)
        L_head = L_wrist = L // 3
        head = context_c[:, :L_head]
        wrist = context_c[:, L_head:L_head + L_wrist]
        proprio = context_c[:, L_head + L_wrist:]
        full_agg = context_c.mean(axis=1)
        hp_agg = jnp.concatenate([head, proprio], axis=1).mean(axis=1)
        wp_agg = jnp.concatenate([wrist, proprio], axis=1).mean(axis=1)
        gate_in = jnp.concatenate([full_agg, hp_agg, wp_agg], axis=-1)
        gate_logits = gate_in @ gate_w + gate_b
        mod = jax.nn.silu(time_cond) @ time_w + time_b
        scale, shift = jnp.split(mod, 2, axis=-1)
        gate_logits = gate_logits * (1.0 + scale) + shift
        gate_scores = jax.nn.softmax(gate_logits, axis=-1)
        topk_w, topk_i = jax.lax.top_k(gate_scores, K)
        topk_w = topk_w / (topk_w.sum(axis=-1, keepdims=True) + 1e-08)
        onehot = (topk_i[..., None] == jnp.arange(E)[None, None, :]).astype(context_c.dtype)
        w_be = jnp.sum(topk_w[..., None] * onehot, axis=1)
        mask = np.ones((E, L), dtype=np.float32)
        mask[1, L_head:L_head + L_wrist] = 0.0
        mask[2, :L_head] = 0.0
        mask = jnp.asarray(mask)
        out = jnp.zeros_like(context_c)
        for e in range(E):
            h = jax.nn.gelu(context_c @ ew1[e] + eb1[e], approximate=True)
            y = h @ ew2[e] + eb2[e]
            out = out + w_be[:, e][:, None, None] * mask[e][None, :, None] * y
        shared = jax.nn.gelu(context_c @ sw1 + sb1, approximate=True) @ sw2 + sb2
        return out + shared

    def _L1_attn_ref(x, Wq, bq, Wk, bk, Wv, bv, gamma, beta):
        import jax, jax.numpy as jnp
        import numpy as np
        NUM_HEADS = 16
        NUM_UNITS = 128
        NEG = -2.0 ** 32 + 1.0
        EPS = 1e-08

        def _attention(x, Wq, bq, Wk, bk, Wv, bv, gamma, beta):
            B, T, C = x.shape
            H = NUM_HEADS
            U = NUM_UNITS
            dh = U // H
            Q = jax.nn.relu(x @ Wq + bq)
            K = jax.nn.relu(x @ Wk + bk)
            V = jax.nn.relu(x @ Wv + bv)
            Qh = Q.reshape(B, T, H, dh)
            Kh = K.reshape(B, T, H, dh)
            Vh = V.reshape(B, T, H, dh)
            scores = jnp.einsum('bqhd,bkhd->bhqk', Qh, Kh) / np.sqrt(dh)
            key_mask = jnp.sign(jnp.abs(jnp.sum(x, axis=-1)))
            scores = jnp.where(key_mask[:, None, None, :] == 0, NEG, scores)
            tril = jnp.tril(jnp.ones((T, T), dtype=scores.dtype))
            scores = jnp.where(tril[None, None, :, :] == 0, NEG, scores)
            attn = jax.nn.softmax(scores, axis=-1)
            query_mask = jnp.sign(jnp.abs(jnp.sum(x, axis=-1)))
            attn = attn * query_mask[:, None, :, None]
            out = jnp.einsum('bhqk,bkhd->bqhd', attn, Vh).reshape(B, T, U)
            out = out + x
            mean = jnp.mean(out, axis=-1, keepdims=True)
            var = jnp.mean((out - mean) ** 2, axis=-1, keepdims=True)
            normalized = (out - mean) / jnp.sqrt(var + EPS)
            return gamma * normalized + beta
        return _attention(x, Wq, bq, Wk, bk, Wv, bv, gamma, beta)

    def _L1_cond2_ref(x, ada_emb, base_layer, w1, b1, w2, b2, ln_g, ln_b):
        import jax, jax.numpy as jnp
        import numpy as np
        B, T, D = (128, 32, 128)
        ADA, INTER, RANK = (128, 128, 8)
        LN_EPS = 1e-05

        def _layernorm(x, g, b):
            mu = jnp.mean(x, axis=-1, keepdims=True)
            var = jnp.var(x, axis=-1, keepdims=True)
            return (x - mu) * jax.lax.rsqrt(var + LN_EPS) * g + b
        b, t, d = x.shape
        ae = _layernorm(ada_emb, ln_g, ln_b)
        h = jax.nn.gelu(ae @ w1 + b1, approximate=False)
        xw = h @ w2 + b2
        x_a, x_b = jnp.split(xw, 2, axis=-1)
        x_a = x_a.reshape(b, d, RANK)
        x_b = x_b.reshape(b, d, RANK)
        layer = base_layer[None, :, :] + jnp.einsum('bdr,bkr->bdk', x_a, x_b)
        out = jnp.einsum('btc,bco->bto', x, layer)
        return x + out

    def _L1_ffn_ref(x, slot_init, w1, b1, w2, b2, tau, Wih, Whh, bih, bhh, wq, bq, wk, bk, wv, bv, ln_g, ln_b, wvp, bvp, wo, bo):
        import jax, jax.numpy as jnp
        import numpy as np
        B, T, D = (8, 512, 128)
        NUM_SLOTS = 64
        TOP_K = 8
        DQ = D // 4
        DH = D // 2

        def _forward(x, slot_init, w1, b1, w2, b2, tau, Wih, Whh, bih, bhh, wq, bq, wk, bk, wv, bv, ln_g, ln_b, wvp, bvp, wo, bo):
            Bx, Tx, Dx = x.shape
            S = jnp.broadcast_to(slot_init[None], (Bx, NUM_SLOTS, Dx)).astype(x.dtype)
            slot_mean = jnp.broadcast_to(S.mean(axis=1, keepdims=True), (Bx, Tx, Dx))
            ctx = jnp.concatenate([x, slot_mean], axis=-1)
            h = jax.nn.gelu(ctx @ w1 + b1, approximate=False)
            route_logits = (h @ w2 + b2) / (jnp.abs(tau) + 0.1)
            topk_vals, topk_idx = jax.lax.top_k(route_logits, TOP_K)
            topk_w = jax.nn.softmax(topk_vals, axis=-1)
            alpha = (jax.nn.one_hot(topk_idx, NUM_SLOTS, dtype=x.dtype) * topk_w[..., None]).sum(axis=-2)
            slot_input = jnp.einsum('bts,btd->bsd', alpha, x)
            denom = alpha.sum(axis=1) + 1e-08
            si = slot_input / denom[..., None]
            gi = si @ Wih.T + bih
            gh = S @ Whh.T + bhh
            i_r, i_z, i_n = jnp.split(gi, 3, axis=-1)
            h_r, h_z, h_n = jnp.split(gh, 3, axis=-1)
            r = jax.nn.sigmoid(i_r + h_r)
            z = jax.nn.sigmoid(i_z + h_z)
            n = jnp.tanh(i_n + r * h_n)
            S_new = (1.0 - z) * n + z * S
            q = S_new @ wq + bq
            k = S_new @ wk + bk
            v = S_new @ wv + bv
            scale = DQ ** (-0.5)
            attn = jax.nn.softmax(jnp.einsum('bsq,btq->bst', q, k) * scale, axis=-1)
            S_comm = jnp.einsum('bst,btd->bsd', attn, v)
            y = S_new + S_comm
            mu = y.mean(axis=-1, keepdims=True)
            var = y.var(axis=-1, keepdims=True)
            y = (y - mu) * jax.lax.rsqrt(var + 1e-05) * ln_g + ln_b
            slot_values = y @ wvp + bvp
            out = jnp.einsum('bts,bsd->btd', alpha, slot_values)
            return out @ wo + bo
        return _forward(x, slot_init, w1, b1, w2, b2, tau, Wih, Whh, bih, bhh, wq, bq, wk, bk, wv, bv, ln_g, ln_b, wvp, bvp, wo, bo)
    x = x + _L0_attn_ref(_L0_cond_ref(x, cond_1024, L0_cond_weight), L0_attn_W_qkv, L0_attn_W_out)
    x = x + _L0_ffn_ref(_L0_cond2_ref(x, cond_1024, L0_cond2_W_f, L0_cond2_b_f, L0_cond2_W_i, L0_cond2_b_i, L0_cond2_W_h, L0_cond2_b_h), L0_ffn_cn_w1, L0_ffn_cn_b1, L0_ffn_cn_w2, L0_ffn_cn_b2, L0_ffn_cn_w3, L0_ffn_cn_b3, L0_ffn_cn_w4, L0_ffn_cn_b4, L0_ffn_gc_w1, L0_ffn_gc_b1, L0_ffn_gc_w2, L0_ffn_gc_b2, L0_ffn_gc_w3, L0_ffn_gc_b3, L0_ffn_adaptive_range)
    x = x + _L1_attn_ref(_L1_cond_ref(x, cond_1024, L1_cond_gate_w, L1_cond_gate_b, L1_cond_time_w, L1_cond_time_b, L1_cond_ew1, L1_cond_eb1, L1_cond_ew2, L1_cond_eb2, L1_cond_sw1, L1_cond_sb1, L1_cond_sw2, L1_cond_sb2), L1_attn_Wq, L1_attn_bq, L1_attn_Wk, L1_attn_bk, L1_attn_Wv, L1_attn_bv, L1_attn_gamma, L1_attn_beta)
    x = x + _L1_ffn_ref(_L1_cond2_ref(x, cond_1024, L1_cond2_base_layer, L1_cond2_w1, L1_cond2_b1, L1_cond2_w2, L1_cond2_b2, L1_cond2_ln_g, L1_cond2_ln_b), L1_ffn_slot_init, L1_ffn_w1, L1_ffn_b1, L1_ffn_w2, L1_ffn_b2, L1_ffn_tau, L1_ffn_Wih, L1_ffn_Whh, L1_ffn_bih, L1_ffn_bhh, L1_ffn_wq, L1_ffn_bq, L1_ffn_wk, L1_ffn_bk, L1_ffn_wv, L1_ffn_bv, L1_ffn_ln_g, L1_ffn_ln_b, L1_ffn_wvp, L1_ffn_bvp, L1_ffn_wo, L1_ffn_bo)
    return x

_drawn_inputs = setup_inputs


def setup_inputs(seed=0):
    import zlib

    import numpy as np

    out = dict(_drawn_inputs(seed))
    spreads = {'L0_cond2_b_f': (0.0, 2.0),
     'L0_cond2_b_i': (0.0, 2.0),
     'L0_cond2_b_h': (0.0, 2.0),
     'L0_ffn_cn_b1': (0.0, 2.0),
     'L0_ffn_cn_b2': (0.0, 2.0),
     'L0_ffn_cn_b3': (0.0, 2.0),
     'L0_ffn_gc_b1': (0.0, 2.0),
     'L0_ffn_gc_b2': (0.0, 2.0),
     'L1_cond_gate_b': (0.0, 0.1),
     'L1_cond_time_b': (0.0, 0.1),
     'L1_cond_eb1': (0.0, 0.1),
     'L1_cond_eb2': (0.0, 0.1),
     'L1_cond_sb1': (0.0, 0.1),
     'L1_cond_sb2': (0.0, 0.1),
     'L1_attn_bq': (0.0, 2.0),
     'L1_attn_bk': (0.0, 2.0),
     'L1_attn_bv': (0.0, 0.1),
     'L1_attn_gamma': (1.0, 0.2),
     'L1_attn_beta': (0.0, 0.1),
     'L1_cond2_b1': (0.0, 0.8),
     'L1_cond2_b2': (0.0, 0.8),
     'L1_cond2_ln_g': (1.0, 0.6),
     'L1_cond2_ln_b': (0.0, 0.8),
     'L1_ffn_b1': (0.0, 2.0),
     'L1_ffn_b2': (0.0, 2.0),
     'L1_ffn_bih': (0.0, 2.0),
     'L1_ffn_bhh': (0.0, 2.0),
     'L1_ffn_bq': (0.0, 2.0),
     'L1_ffn_bk': (0.0, 2.0),
     'L1_ffn_bv': (0.0, 0.8),
     'L1_ffn_ln_g': (1.0, 0.6),
     'L1_ffn_ln_b': (0.0, 2.0),
     'L1_ffn_bvp': (0.0, 0.501),
     'L1_ffn_bo': (0.0, 0.1)}
    factors = {'L0_cond2_W_f': 3.835,
     'L0_cond2_W_i': 3.561,
     'L0_ffn_cn_w1': 8.0,
     'L0_ffn_cn_w2': 42.001,
     'L0_ffn_cn_w3': 43.413,
     'L0_ffn_cn_w4': 44.482,
     'L0_ffn_gc_w1': 64.0,
     'L0_ffn_gc_w2': 64.0,
     'L0_ffn_gc_w3': 43.541,
     'L1_attn_Wq': 31.742,
     'L1_attn_Wk': 23.273,
     'L1_cond2_w1': 8.0,
     'L1_cond2_w2': 8.0,
     'L1_ffn_slot_init': 64.0,
     'L1_ffn_w1': 8.0,
     'L1_ffn_w2': 8.0,
     'L1_ffn_Whh': 64.0,
     'L1_ffn_wq': 29.705,
     'L1_ffn_wk': 26.743,
     'L1_ffn_wv': 8.0,
     'L0_cond2_W_h': 3.071,
     'L1_cond2_base_layer': 4.925}
    for name, (base, spread) in spreads.items():
        noise = np.random.default_rng([zlib.crc32(name.encode()), seed]).standard_normal(out[name].shape)
        drawn = base * np.exp(spread * noise) if base else spread * noise
        out[name] = jnp.asarray(drawn.astype(out[name].dtype))
    for name, factor in factors.items():
        out[name] = (out[name] * factor).astype(out[name].dtype)
    return out
```

```python
from contextlib import ExitStack

import numpy as np

import concourse.bass as bass
from concourse import mybir

F32 = mybir.dt.float32
BF16 = mybir.dt.bfloat16
ALU = mybir.AluOpType
ACTF = mybir.ActivationFunctionType
AX = mybir.AxisListType

B, T, D = 32, 128, 128
N = B * T
NEG = -1e30

COLS = [
    ("condT", 32), ("w0", 128), ("ident", 128), ("mask", 512), ("wqkv", 3072), ("wout", 1024),
    ("wfT", 128), ("wiT", 128), ("whT", 128), ("bf", 1), ("bi", 1), ("bh", 1),
    ("cw1", 128), ("cw2", 64), ("cw3", 32), ("cw4", 128), ("cb1", 1), ("cb2", 1), ("cb3", 1), ("cb4", 1),
    ("gw1", 64), ("gw2", 32), ("gw3", 128), ("gb1", 1), ("gb2", 1), ("gb3", 1), ("ar", 1), ("twist", 128),
    ("gatew", 12), ("gateb", 4), ("timew", 8), ("timeb", 8), ("lower", 16),
    ("ew1", 2048), ("eb1", 16), ("ew2", 2048), ("eb2", 4), ("sw1", 512), ("sb1", 4), ("sw2", 512), ("sb2", 1),
    ("emask", 512),
    ("aq", 128), ("bq", 1), ("ak", 128), ("bk", 1), ("av", 128), ("bv", 128), ("gamma", 128), ("beta", 128),
    ("hm", 16),
    ("cond", 128), ("lng", 128), ("lnb", 128), ("lw1", 128), ("lb1", 1), ("lw2a", 1024), ("lw2b", 1024),
    ("lb2a", 8), ("lb2b", 128), ("base", 128), ("bm16", 16),
    ("fw1a", 64), ("fw1b", 64), ("fb1", 1), ("fw2", 64), ("fb2", 64), ("tau", 1), ("wihT", 384), ("whhT", 384),
    ("bih", 3), ("bhh", 3), ("slotT", 64), ("fwq", 32), ("fbq", 1), ("fwk", 32), ("fbk", 1), ("fwv", 128),
    ("fbv", 128), ("flng", 128), ("flnb", 128), ("wvp", 128), ("bvp", 1), ("wo", 128), ("bo", 128), ("pmask", 128),
]
OFF, _at = {}, 0
for _n, _c in COLS:
    OFF[_n] = (_at, _c)
    _at += _c
WIDE = _at
GROUPS = [(0, OFF["wfT"][0]), (OFF["wfT"][0], OFF["gatew"][0]), (OFF["gatew"][0], OFF["aq"][0]), (OFF["aq"][0], WIDE)]


class Queue:

    def __init__(self, eng, new_sem, name):
        self.eng, self.new_sem, self.name = eng, new_sem, name
        self.seen = {}
        self.stage("s0")

    def stage(self, label):
        self.sem = self.new_sem(f"{self.name}_{label}")
        self.n = 0

    def wait(self, toks):
        need = {}
        todo = list(toks)
        while todo:
            t = todo.pop()
            if t is None:
                continue
            if isinstance(t, list):
                todo += t
                continue
            s, v = t
            if v > need.get(id(s), (s, 0))[1]:
                need[id(s)] = (s, v)
        for k, (s, v) in need.items():
            if self.seen.get(k, 0) < v:
                self.eng.wait_ge(s, v)
                self.seen[k] = v

    def do(self, make, *toks, inc=True):
        self.wait(toks)
        ins = make(self.eng)
        if not inc:
            return None
        self.n += 1
        ins.then_inc(self.sem, 1)
        return (self.sem, self.n)

    def last(self):
        return (self.sem, self.n) if self.n else None


def build(nc, xT_d, w_d, out_d):
    ctx = ExitStack()
    with ctx:
        def sb(name, shape, dt=F32):
            return ctx.enter_context(nc.sbuf_tensor(name, shape, dt))

        def new_sem(name):
            return ctx.enter_context(nc.semaphore(name))

        PB = [ctx.enter_context(nc.psum_tensor(f"PB{i}", [128, 512], F32)) for i in range(8)]
        W = sb("W", [128, WIDE])
        XF = sb("XF", [128, N])
        HF = sb("HF", [128, N])
        XT = sb("XT", [128, N])
        AR = sb("AR", [128, 19200])
        small = sb("small", [128, 2048])
        identb = sb("identb", [128, 128], BF16)
        maskb = sb("maskb", [128, 512], BF16)

        def w(name, rows=128, a=0, b=None):
            o, c = OFF[name]
            return W[0:rows, o + a:o + (c if b is None else b)]

        used = [0]

        def sm(cols):
            a = used[0]
            used[0] += cols
            assert used[0] <= 2048
            return small[:, a:a + cols]

        arena = [0]

        def ar(cols):
            a = arena[0]
            arena[0] += cols
            assert arena[0] <= 19200, arena[0]
            return AR[:, a:a + cols]

        pe = Queue(nc.tensor, new_sem, "pe")
        act = Queue(nc.scalar, new_sem, "act")
        dve = Queue(nc.vector, new_sem, "dve")
        pool = Queue(nc.gpsimd, new_sem, "pool")
        engines = [pe, act, dve, pool]
        s_w = [new_sem(f"s_w{i}") for i in range(4)]
        s_x = [new_sem(f"s_x{i}") for i in range(4)]
        s_out = new_sem("s_out")

        def load(g):
            a, b = GROUPS[g]
            nc.sync.dma_start(W[:, a:b], w_d[:, a:b]).then_inc(s_w[g], 16)

        load(0)
        for i in range(4):
            nc.sync.dma_start(XF[:, i * 1024:(i + 1) * 1024], xT_d[:, i * 1024:(i + 1) * 1024]).then_inc(s_x[i], 16)
        for g in range(1, 4):
            load(g)
        LW = [(s, 16) for s in s_w]
        LX = [(s, 16) for s in s_x]

        def barrier(label):
            toks = [e.last() for e in engines]
            for e in engines:
                e.stage(label)
                e.wait(toks)
            arena[0] = 0

        ident = w("ident")

        pad = [(pool.do(lambda e: e.memset(small[:, 0:8], 0.0)))]
        c_eps8, c_eps5, c_zero = sm(1), sm(1), sm(1)
        used[0] = 8
        t = pool.do(lambda e: e.memset(c_eps8, 1e-8), pad)
        eps_tok = pool.do(lambda e: e.memset(c_eps5, 1e-5), t)

        tmb = [dve.do(lambda e: e.tensor_copy(identb[:, :], ident), LW[0]),
               dve.do(lambda e: e.tensor_copy(maskb[:, :], w("mask")))]

        ysT, ys2, dT = sm(32), sm(32), sm(32)
        w2 = ar(128)
        t1 = dve.do(lambda e: e.tensor_scalar(ysT, w("condT"), float(np.float32(1.0) / np.sqrt(np.float32(128))), None, ALU.mult), LW[0])
        t2 = dve.do(lambda e: e.tensor_tensor(ys2, ysT, ysT, ALU.mult), t1)
        t3 = dve.do(lambda e: e.tensor_tensor(w2, w("w0"), w("w0"), ALU.mult))
        t4 = pe.do(lambda e: e.matmul(PB[6][:, 0:32], w2, ys2, start=True, stop=True), t2, t3)
        t5 = act.do(lambda e: e.activation(dT, PB[6][:, 0:32], ACTF.Sqrt, bias=c_eps8), t4, eps_tok)
        t_d = dve.do(lambda e: e.reciprocal(dT, dT), t5)
        t_ys = t1

        NCH = 16
        xs = [ar(256) for _ in range(2)]
        uu = [ar(256) for _ in range(2)]
        QT = [ar(2048).rearrange("p (f n) -> p f n", f=8) for _ in range(2)]
        KB = [ar(4096).rearrange("p (f b s j) -> p f b s j", f=8, b=2, s=2) for _ in range(2)]
        VX = [HF[:, i * 2048:(i + 1) * 2048] for i in range(0)]
        VXW = 1104
        VX = [HF[:, 0:2 * VXW].rearrange("p (b v) -> p b v", b=2),
              XT[:, 0:2 * VXW].rearrange("p (b v) -> p b v", b=2)]
        SS = [HF[:, 2304 + i * 512:2816 + i * 512] for i in range(3)]
        PT = [XT[:, 2304 + i * 512:2816 + i * 512] for i in range(2)]
        ON = [ar(256) for _ in range(2)]
        OT = [ar(1024).rearrange("p (k t) -> p k t", k=8) for _ in range(2)]
        mx = [sm(4) for _ in range(3)]
        rc = [sm(4) for _ in range(2)]

        zk = [pool.do(lambda e, i=i: e.memset(KB[i][:, :, :, :, :].rearrange("p f b s j -> p (f b s j)"), 0.0)) for i in range(2)]
        ov = [pool.do(lambda e, i=i: e.memset(VX[i].rearrange("p b v -> p (b v)"), 1.0)) for i in range(2)]

        pj_free = [t5, None]
        pj_n = [0]

        def pj():
            i = pj_n[0] % 2
            pj_n[0] += 1
            return PB[6 + i], i

        tok_q, tok_k, tok_v = {}, {}, {}
        last_s, last_pv = {}, {}
        u_readers, xs_readers = [None, None], [None, None]

        def proj(c):
            i = c % 2
            x3 = XF[:, c * 256:(c + 1) * 256].rearrange("p (b t) -> p b t", b=2)
            ta = pool.do(lambda e: e.tensor_tensor(xs[i].rearrange("p (b t) -> p b t", b=2), x3,
                                                   ysT[:, 2 * c:2 * c + 2].unsqueeze(2).broadcast_to([128, 2, 128]), ALU.mult),
                         LX[c // 4], t_ys, xs_readers[i])
            bank, k = pj()
            tb = pe.do(lambda e: e.matmul(bank[:, 0:256], w("w0"), xs[i], start=True, stop=True), ta, pj_free[k], LW[0])
            xs_readers[i] = tb
            tu = dve.do(lambda e: e.tensor_tensor(uu[i].rearrange("p (b t) -> p b t", b=2),
                                                  bank[:, 0:256].rearrange("p (b t) -> p b t", b=2),
                                                  dT[:, 2 * c:2 * c + 2].unsqueeze(2).broadcast_to([128, 2, 128]), ALU.mult),
                        tb, t_d, u_readers[i])
            pj_free[k] = tu
            yield
            for f in range(0, 8, 2):
                bank, k = pj()
                for h in range(2):
                    tp = pe.do(lambda e: e.matmul(bank[:, h * 256:(h + 1) * 256], w("wqkv", 128, (f + h) * 128, (f + h + 1) * 128),
                                                  uu[i], start=True, stop=True), tu, pj_free[k], inc=h == 1)
                tq = act.do(lambda e: e.activation(QT[i][:, f:f + 2, :], bank[:, :].rearrange("p (f n) -> p f n", f=2),
                                                   ACTF.Copy, scale=0.125), tp, last_s.get(c - 2))
                pj_free[k] = tq
                tok_q[c] = tq
                yield
                bank, k = pj()
                for h in range(2):
                    tp = pe.do(lambda e: e.matmul(bank[:, h * 256:(h + 1) * 256], w("wqkv", 128, 1024 + (f + h) * 128, 1024 + (f + h + 1) * 128),
                                                  uu[i], start=True, stop=True), tu, pj_free[k], inc=h == 1)
                k0 = dve.do(lambda e: e.tensor_copy(KB[i][0:64, f:f + 2, :, 0, :],
                                                    bank[0:64, :].rearrange("p (f b j) -> p f b j", f=2, b=2)),
                            tp, zk[i], last_s.get(c - 2))
                k1 = act.do(lambda e: e.activation(KB[i][64:128, f:f + 2, :, 1, :],
                                                   bank[64:128, :].rearrange("p (f b j) -> p f b j", f=2, b=2), ACTF.Copy),
                            tp, zk[i], last_s.get(c - 2))
                pj_free[k] = [k0, k1]
                tok_k[c] = [k0, k1]
                yield
            for b in range(2):
                for h in range(2):
                    bank, k = pj()
                    tp = pe.do(lambda e: e.matmul(bank[:, :], uu[i][:, b * 128:(b + 1) * 128],
                                                  w("wqkv", 128, 2048 + h * 512, 2048 + (h + 1) * 512), start=True, stop=True),
                               tu, pj_free[k])
                    u_readers[i] = tp
                    tv = act.do(lambda e: e.activation(
                        VX[i][:, b, h * 520:(h + 1) * 520].rearrange("p (h v) -> p h v", v=65)[:, :, 0:64],
                        bank[:, :].rearrange("p (h v) -> p h v", v=64), ACTF.Copy), tp, ov[i], last_pv.get(c - 2))
                    pj_free[k] = tv
                    tok_v[c] = tv
                    yield

        units = [(c, b, g) for c in range(NCH) for b in range(2) for g in range(4)]
        U = len(units)
        k_sub, k_exp, k_T, k_cp, k_pv, k_nm, k_ot, k_on = ({} for _ in range(8))
        k_otc, k_y = {}, {}

        def a_S(u):
            c, b, g = units[u]
            i = c % 2
            bank = PB[u % 2]
            pe.do(lambda e: e.matmul(bank[:, :], identb[:, :], maskb[:, :], start=True, stop=False), k_sub.get(u - 2), tmb, inc=False)
            for h in range(2):
                f = 2 * g + h
                t = pe.do(lambda e: e.matmul(bank[:, h * 256:(h + 1) * 256], QT[i][:, f, b * 128:(b + 1) * 128],
                                             KB[i][:, f, b, :, :].rearrange("p s j -> p (s j)"), start=False, stop=h == 1),
                          tok_q[c], tok_k[c], inc=h == 1)
            last_s[c] = t
            m = mx[u % 3]
            b3 = bank[:, :].rearrange("p (h j) -> p h j", h=4)
            t = dve.do(lambda e: e.tensor_reduce(m, b3, AX.X, ALU.max), t)
            t = dve.do(lambda e: e.tensor_tensor(SS[u % 3].rearrange("p (h j) -> p h j", h=4), b3,
                                                 m.unsqueeze(2).broadcast_to([128, 4, 128]), ALU.subtract), t, k_T.get(u - 3))
            k_sub[u] = t
            k_exp[u] = act.do(lambda e: e.activation(SS[u % 3], SS[u % 3], ACTF.Exp), t)

        def a_T(u):
            bank = PB[2 + u % 2]
            for h in range(4):
                t = pe.do(lambda e: e.transpose(bank[:, h * 128:(h + 1) * 128], SS[u % 3][:, h * 128:(h + 1) * 128], ident),
                          k_exp[u], k_cp.get(u - 2), inc=h == 3)
            k_T[u] = t
            k_cp[u] = act.do(lambda e: e.activation(PT[u % 2], bank[:, :], ACTF.Copy), t, k_pv.get(u - 2))

        def a_PV(u):
            c, b, g = units[u]
            bank = PB[4 + u % 2]
            for h in range(4):
                o = 65 * (4 * g + h)
                t = pe.do(lambda e: e.matmul(bank[:, h * 128:(h + 1) * 128], PT[u % 2][:, h * 128:(h + 1) * 128],
                                             VX[c % 2][:, b, o:o + 128], start=True, stop=True),
                          k_cp[u], tok_v[c], k_on.get(u - 2), inc=h == 3)
            k_pv[u] = t
            last_pv[c] = t
            o3 = bank[:, :].rearrange("p (h v) -> p h v", h=4)
            t = dve.do(lambda e: e.reciprocal(rc[u % 2].unsqueeze(2), o3[:, :, 64:65]), t)
            k_on[u] = dve.do(lambda e: e.tensor_tensor(ON[u % 2].rearrange("p (h v) -> p h v", h=4), o3[:, :, 0:64],
                                                       rc[u % 2].unsqueeze(2).broadcast_to([128, 4, 64]), ALU.mult),
                             t, k_ot.get(u - 2))

        def a_OT(u):
            c, b, g = units[u]
            q = (2 * c + b)
            bank, k = pj()
            for h in range(2):
                t = pe.do(lambda e: e.transpose(bank[:, h * 128:(h + 1) * 128], ON[u % 2][:, h * 128:(h + 1) * 128], ident),
                          k_on[u], pj_free[k], inc=h == 1)
            k_ot[u] = t
            pj_free[k] = k_otc[u] = act.do(lambda e: e.activation(OT[q % 2][:, 2 * g:2 * g + 2, :],
                                                                  bank[:, 0:256].rearrange("p (k t) -> p k t", k=2), ACTF.Copy),
                                           t, k_y.get(q - 2))
            if g < 3:
                return
            bank, k = pj()
            for f in range(8):
                t = pe.do(lambda e: e.matmul(bank[:, 0:128], w("wout", 128, f * 128, (f + 1) * 128), OT[q % 2][:, f, :],
                                             start=f == 0, stop=f == 7), k_otc[u], pj_free[k], inc=f == 7)
            k_y[q] = t
            pj_free[k] = dve.do(lambda e: e.tensor_tensor(XF[:, q * 128:(q + 1) * 128], bank[:, 0:128],
                                                          XF[:, q * 128:(q + 1) * 128], ALU.add), t)

        for _ in proj(0):
            pass
        filler = iter(())
        for s in range(U + 3):
            if s < U:
                if s % 8 == 0:
                    for _ in filler:
                        pass
                    filler = proj(s // 8 + 1) if s // 8 + 1 < NCH else iter(())
                a_S(s)
            if 0 <= s - 1 < U:
                a_T(s - 1)
            if 0 <= s - 2 < U:
                a_PV(s - 2)
            if 0 <= s - 3 < U:
                a_OT(s - 3)
            for _ in range(2):
                next(filler, None)

        barrier("s2")
        FG, IG, CD = ar(4096), ar(4096), ar(4096)
        ones = ar(128)
        SM = XT[:, :]
        t_on = pool.do(lambda e: e.memset(ones, 1.0))
        tf, ti, tc, ts = {}, {}, {}, {}
        fr = [None] * 8
        CH = 8

        def cs(tile, c, n=512):
            return tile[:, c * n:(c + 1) * n]

        def v4(ap):
            return ap.rearrange("p (b t) -> p b t", b=4)

        for c in range(CH):
            for j, (wn, bn, dst) in enumerate([("wfT", "bf", FG), ("wiT", "bi", IG), ("whT", "bh", CD)]):
                k = (3 * c + j) % 8
                tp = pe.do(lambda e: e.matmul(PB[k][:, :], w(wn), cs(XF, c), start=True, stop=True), LW[1], fr[k])
                if j < 2:
                    fr[k] = act.do(lambda e: e.activation(cs(dst, c), PB[k][:, :], ACTF.Sigmoid, bias=w(bn)), tp, LW[1])
                    (tf, ti)[j][c] = fr[k]
                else:
                    fr[k] = tc[c] = dve.do(lambda e: e.tensor_scalar(cs(dst, c), PB[k][:, :], w(bn), None, ALU.add), tp, LW[1])
            ts[c] = dve.do(lambda e: e.scalar_tensor_tensor(cs(SM, c), cs(FG, c), 1e-8, cs(IG, c), ALU.add, ALU.add), tf[c], ti[c])
        d1, d2, d3, d4, d5 = {}, {}, {}, {}, {}
        for c in range(CH):
            ta = act.do(lambda e: e.activation(cs(SM, c), cs(SM, c), ACTF.Ln), ts[c])
            d1[c] = act.do(lambda e: e.activation(cs(SM, c), cs(SM, c), ACTF.Exp, scale=-1.0), ta)
        for c in range(CH):
            ta = dve.do(lambda e: e.tensor_tensor(cs(FG, c), cs(FG, c), cs(SM, c), ALU.mult), d1[c])
            d2[c] = act.do(lambda e: e.activation(cs(FG, c), cs(FG, c), ACTF.Ln, bias=c_eps8), ta)
            tb = pool.do(lambda e: e.tensor_tensor(cs(IG, c), cs(IG, c), cs(SM, c), ALU.mult), d1[c])
            d3[c] = pool.do(lambda e: e.tensor_tensor(cs(CD, c), cs(CD, c), cs(IG, c), ALU.mult), tb, tc[c])
        d6 = {}
        for c in range(CH):
            for b in range(4):
                q = slice(c * 512 + b * 128, c * 512 + (b + 1) * 128)
                ta = dve.do(lambda e: e.tensor_tensor_scan(SM[:, q], ones, FG[:, q], 0.0, ALU.mult, ALU.add), d2[c], d3[c], t_on)
            tb = dve.do(lambda e: e.tensor_tensor(cs(FG, c), cs(SM, c), cs(FG, c), ALU.subtract), ta)
            for b in range(4):
                q = slice(c * 512 + b * 128, c * 512 + (b + 1) * 128)
                tcx = act.do(lambda e: e.activation(FG[:, q], FG[:, q], ACTF.Exp, scale=-1.0, bias=SM[:, q.stop - 1:q.stop]), tb)
            d4[c] = tcx
            d5[c] = act.do(lambda e: e.activation(cs(SM, c), cs(SM, c), ACTF.Exp), tcx)
            td = pool.do(lambda e: e.tensor_tensor(cs(CD, c), cs(CD, c), cs(FG, c), ALU.mult), d4[c], d3[c])
            for b in range(4):
                q = slice(c * 512 + b * 128, c * 512 + (b + 1) * 128)
                te = dve.do(lambda e: e.tensor_tensor_scan(IG[:, q], ones, CD[:, q], 0.0, ALU.mult, ALU.add), td)
            for b in range(4):
                q = slice(c * 512 + b * 128, c * 512 + (b + 1) * 128)
                n = 4 * c + b
                tg = dve.do(lambda e: e.scalar_tensor_tensor(HF[:, q], SM[:, q], w("condT", 128, n, n + 1), IG[:, q],
                                                             ALU.mult, ALU.add), d5[c], te)
            d6[c] = tg

        barrier("s3")
        gctx, g1, g2, cB, ar14, ar06, b4h, gfT = sm(32), sm(32), sm(32), sm(32), sm(1), sm(1), sm(1), sm(32)
        t = dve.do(lambda e: e.tensor_reduce(gctx, HF[:, :].rearrange("p (b t) -> p b t", b=32), AX.X, ALU.add))
        t = dve.do(lambda e: e.tensor_scalar(gctx, gctx, 1.0 / 128, None, ALU.mult), t)
        t = pe.do(lambda e: e.matmul(PB[7][0:64, 0:32], w("gw1"), gctx, start=True, stop=True), t)
        t = act.do(lambda e: e.activation(g1[0:64, :], PB[7][0:64, 0:32], ACTF.Gelu, bias=w("gb1", 64)), t)
        t = pe.do(lambda e: e.matmul(PB[7][0:32, 32:64], w("gw2", 64), g1[0:64, :], start=True, stop=True), t)
        t = act.do(lambda e: e.activation(g2[0:32, :], PB[7][0:32, 32:64], ACTF.Gelu, bias=w("gb2", 32)), t)
        t = pe.do(lambda e: e.matmul(PB[7][:, 64:96], w("gw3", 32), g2[0:32, :], start=True, stop=True), t)
        th = dve.do(lambda e: e.tensor_scalar(b4h, w("gb3"), 0.5, None, ALU.mult))
        t = act.do(lambda e: e.activation(gfT, PB[7][:, 64:96], ACTF.Tanh, bias=b4h, scale=0.5), t, th)
        b4h2 = sm(1)
        th2 = dve.do(lambda e: e.tensor_scalar(b4h2, w("cb4"), 0.5, None, ALU.mult))
        t7 = dve.do(lambda e: e.tensor_scalar(ar14, w("ar"), 0.7, None, ALU.mult))
        t3_ = dve.do(lambda e: e.tensor_scalar(ar06, w("ar"), 0.3, None, ALU.mult))
        t_cB = dve.do(lambda e: e.tensor_scalar(cB, gfT, ar14, 0.1, ALU.mult, ALU.add), t, t7)
        h1 = [ar(512) for _ in range(3)]
        h2 = [ar(512) for _ in range(3)]
        h3 = [ar(512) for _ in range(3)]
        tt = [ar(512) for _ in range(3)]
        cp = [ar(512) for _ in range(3)]
        fr = [t_cB if i == 7 else None for i in range(8)]
        r_h1, r_h2, r_h3 = [None] * 3, [None] * 3, [None] * 3
        r_tt, r_cp = [None] * 3, [None] * 3
        upd = {c: None for c in range(CH)}
        bk = [0]

        def nb():
            k = bk[0] % 8
            bk[0] += 1
            return k

        n3 = 0

        def couple(c):
            i = n3 % 3
            k = nb()
            tp = pe.do(lambda e: e.matmul(PB[k][:, :], w("cw1"), cs(HF, c), start=True, stop=True), upd[c], fr[k])
            fr[k] = t1 = act.do(lambda e: e.activation(h1[i], PB[k][:, :], ACTF.Gelu, bias=w("cb1")), tp, r_h1[i])
            yield
            k = nb()
            r_h1[i] = tp = pe.do(lambda e: e.matmul(PB[k][0:64, :], w("cw2"), h1[i], start=True, stop=True), t1, fr[k])
            fr[k] = t1 = act.do(lambda e: e.activation(h2[i][0:64, :], PB[k][0:64, :], ACTF.Gelu, bias=w("cb2", 64)), tp, r_h2[i])
            yield
            k = nb()
            r_h2[i] = tp = pe.do(lambda e: e.matmul(PB[k][0:32, :], w("cw3", 64), h2[i][0:64, :], start=True, stop=True), t1, fr[k])
            fr[k] = t1 = act.do(lambda e: e.activation(h3[i][0:32, :], PB[k][0:32, :], ACTF.Gelu, bias=w("cb3", 32)), tp, r_h3[i])
            yield
            k = nb()
            r_h3[i] = tp = pe.do(lambda e: e.matmul(PB[k][:, :], w("cw4", 32), h3[i][0:32, :], start=True, stop=True), t1, fr[k])
            fr[k] = t1 = act.do(lambda e: e.activation(tt[i], PB[k][:, :], ACTF.Tanh, bias=b4h2, scale=0.5), tp, r_tt[i], th2)
            k2 = nb()
            tw = pe.do(lambda e: e.matmul(PB[k2][:, :], w("twist"), cs(HF, c), start=True, stop=True), upd[c], fr[k2])
            r_tt[i] = t1 = dve.do(lambda e: e.scalar_tensor_tensor(
                v4(cp[i]), v4(tt[i]), ar06, cB[:, 4 * c:4 * c + 4].unsqueeze(2).broadcast_to([128, 4, 128]), ALU.mult, ALU.add),
                t1, t_cB, t3_, r_cp[i])
            fr[k2] = t1 = dve.do(lambda e: e.tensor_tensor(cp[i], cp[i], PB[k2][:, :], ALU.mult), t1, tw)
            yield
            upd[c] = r_cp[i] = dve.do(lambda e: e.tensor_tensor(cs(HF, c), cs(HF, c), cp[i], ALU.add), t1, tp)
            yield

        live = []
        jobs = [c for _ in range(3) for c in range(CH)]
        while jobs or live:
            if jobs and len(live) < 3:
                live.append(couple(jobs.pop(0)))
                next(live[-1])
                n3 += 1
            for gnr in list(live):
                try:
                    next(gnr)
                except StopIteration:
                    live.remove(gnr)
        tx2 = {}
        for c in range(CH):
            tx2[c] = dve.do(lambda e: e.tensor_tensor(cs(XF, c), cs(XF, c), cs(HF, c), ALU.add), upd[c])

        barrier("s4")
        hs, ws, psm = sm(32), sm(32), sm(32)
        agg = sm(96)
        xb3 = XF[:, :].rearrange("p (b t) -> p b t", b=32)
        ta = dve.do(lambda e: e.tensor_reduce(hs, xb3[:, :, 0:42], AX.X, ALU.add))
        tb = dve.do(lambda e: e.tensor_reduce(ws, xb3[:, :, 42:84], AX.X, ALU.add))
        tcx = dve.do(lambda e: e.tensor_reduce(psm, xb3[:, :, 84:128], AX.X, ALU.add))
        ta = dve.do(lambda e: e.tensor_tensor(agg[:, 32:64], hs, psm, ALU.add), ta, tcx)
        tb2 = dve.do(lambda e: e.tensor_tensor(agg[:, 64:96], ws, psm, ALU.add), tb)
        tcx = dve.do(lambda e: e.tensor_tensor(agg[:, 0:32], agg[:, 32:64], ws, ALU.add), ta)
        t = dve.do(lambda e: e.tensor_scalar(agg[:, 0:32], agg[:, 0:32], 1.0 / 128, None, ALU.mult), tcx)
        t = dve.do(lambda e: e.tensor_scalar(agg[:, 32:96], agg[:, 32:96], 1.0 / 86, None, ALU.mult), t, tb2)
        for j in range(3):
            tg = pe.do(lambda e: e.matmul(PB[0][0:32, 0:4], agg[:, 32 * j:32 * j + 32], w("gatew", 128, 4 * j, 4 * j + 4),
                                          start=j == 0, stop=j == 2), t, LW[2], inc=j == 2)
        sil, tmod, lg, sc = sm(32), sm(8), sm(4), sm(4)
        t = act.do(lambda e: e.activation(sil, w("condT"), ACTF.Silu))
        tm = pe.do(lambda e: e.matmul(PB[1][0:32, 0:8], sil, w("timew"), start=True, stop=True), t)
        R = 32
        t = dve.do(lambda e: e.tensor_tensor(tmod[0:R, :], PB[1][0:R, 0:8], w("timeb", R), ALU.add), tm)
        t1 = dve.do(lambda e: e.tensor_scalar(tmod[0:R, 0:4], tmod[0:R, 0:4], 1.0, None, ALU.add), t)
        t = dve.do(lambda e: e.tensor_tensor(lg[0:R, :], PB[0][0:R, 0:4], w("gateb", R), ALU.add), tg)
        t = dve.do(lambda e: e.tensor_tensor(lg[0:R, :], lg[0:R, :], tmod[0:R, 0:4], ALU.mult), t, t1)
        t = dve.do(lambda e: e.tensor_tensor(lg[0:R, :], lg[0:R, :], tmod[0:R, 4:8], ALU.add), t)
        s1 = sm(1)
        t = dve.do(lambda e: e.tensor_reduce(s1[0:R, :], lg[0:R, :], AX.X, ALU.max), t)
        t = dve.do(lambda e: e.tensor_scalar(lg[0:R, :], lg[0:R, :], s1[0:R, :], None, ALU.subtract), t)
        t = act.do(lambda e: e.activation(sc[0:R, :], lg[0:R, :], ACTF.Exp), t)
        t = dve.do(lambda e: e.tensor_reduce(s1[0:R, :], sc[0:R, :], AX.X, ALU.add), t)
        t = dve.do(lambda e: e.reciprocal(s1[0:R, :], s1[0:R, :]), t)
        t = dve.do(lambda e: e.tensor_scalar(sc[0:R, :], sc[0:R, :], s1[0:R, :], None, ALU.mult), t)
        cmp1, cmp2, rank = sm(16), sm(16), sm(4)
        sA = sc[0:R, :].unsqueeze(1).broadcast_to([R, 4, 4])
        sB = sc[0:R, :].unsqueeze(2).broadcast_to([R, 4, 4])
        c1 = cmp1[0:R, :].rearrange("p (a b) -> p a b", a=4)
        c2 = cmp2[0:R, :].rearrange("p (a b) -> p a b", a=4)
        ta = dve.do(lambda e: e.tensor_tensor(c1, sA, sB, ALU.is_gt), t)
        tb = dve.do(lambda e: e.tensor_tensor(c2, sA, sB, ALU.is_equal), t)
        tb = dve.do(lambda e: e.tensor_tensor(cmp2[0:R, :], cmp2[0:R, :], w("lower", R), ALU.mult), tb)
        t = dve.do(lambda e: e.tensor_tensor(cmp1[0:R, :], cmp1[0:R, :], cmp2[0:R, :], ALU.add), ta, tb)
        t = dve.do(lambda e: e.tensor_reduce(rank[0:R, :], c1, AX.X, ALU.add), t)
        t = dve.do(lambda e: e.tensor_scalar(rank[0:R, :], rank[0:R, :], 1.5, None, ALU.is_lt), t)
        t = dve.do(lambda e: e.tensor_tensor(sc[0:R, :], sc[0:R, :], rank[0:R, :], ALU.mult), t)
        t = dve.do(lambda e: e.tensor_reduce(s1[0:R, :], sc[0:R, :], AX.X, ALU.add), t)
        t = dve.do(lambda e: e.tensor_scalar(s1[0:R, :], s1[0:R, :], 1e-8, None, ALU.add), t)
        t = dve.do(lambda e: e.reciprocal(s1[0:R, :], s1[0:R, :]), t)
        t = dve.do(lambda e: e.tensor_scalar(sc[0:R, :], sc[0:R, :], s1[0:R, :], None, ALU.mult), t)
        dg = sm(128)
        wbc = sm(128)
        on32 = sm(128)
        to = pool.do(lambda e: e.memset(on32, 1.0))
        t = dve.do(lambda e: e.tensor_tensor(dg[0:R, :].rearrange("p (a b) -> p a b", a=4),
                                             ident[0:R, 0:32].unsqueeze(1).broadcast_to([R, 4, 32]),
                                             sc[0:R, :].unsqueeze(2).broadcast_to([R, 4, 32]), ALU.mult), t)
        t = pe.do(lambda e: e.matmul(PB[2][:, 0:128], on32[0:R, :], dg[0:R, :], start=True, stop=True), t, to)
        t_w = dve.do(lambda e: e.tensor_copy(wbc, PB[2][:, 0:128]), t)

        HB = [ar(2048).rearrange("p (c n) -> p c n", c=4) for _ in range(2)]
        GT = [ar(512) for _ in range(2)]
        YT = [ar(512) for _ in range(2)]
        r_hb, r_gt, r_yt = [None, None], [None, None], [None, None]
        pbf = [t_w] * 8
        acc = {}
        jn = [0]

        def up(c, x):
            i = jn[0] % 2
            jn[0] += 1
            w1 = (lambda k: w("ew1", 128, x * 512 + k * 128, x * 512 + (k + 1) * 128)) if x < 4 else \
                 (lambda k: w("sw1", 128, k * 128, (k + 1) * 128))
            b1 = (lambda k: w("eb1", 128, x * 4 + k, x * 4 + k + 1)) if x < 4 else (lambda k: w("sb1", 128, k, k + 1))
            toks = []
            for k in range(4):
                p = (4 * i + k) % 6
                p = k + 0
                bank = PB[p]
                tp = pe.do(lambda e: e.matmul(bank[:, :], w1(k), cs(XF, c), start=True, stop=True), pbf[p], LW[2])
                pbf[p] = act.do(lambda e: e.activation(HB[i][:, k, :], bank[:, :], ACTF.Gelu_apprx_tanh, bias=b1(k)), tp, r_hb[i])
                toks.append(pbf[p])
            return i, toks

        def down(c, x, i, toks):
            w2_ = (lambda k: w("ew2", 128, (x * 4 + k) * 128, (x * 4 + k + 1) * 128)) if x < 4 else \
                  (lambda k: w("sw2", 128, k * 128, (k + 1) * 128))
            p = 4 + jn[0] % 4
            bank = PB[p]
            for k in range(4):
                tp = pe.do(lambda e: e.matmul(bank[:, :], w2_(k), HB[i][:, k, :], start=k == 0, stop=k == 3),
                           toks[k], pbf[p], inc=k == 3)
            r_hb[i] = tp
            if x == 4:
                pbf[p] = acc[c] = dve.do(lambda e: e.tensor_scalar(cs(HF, c), bank[:, :], w("sb2"), None, ALU.add), tp)
                return
            j = jn[0] % 2
            gt = pool.do(lambda e: e.tensor_tensor(v4(GT[j]), w("emask", 128, x * 128, (x + 1) * 128).unsqueeze(1).broadcast_to([128, 4, 128]),
                                                   wbc[:, x * 32 + 4 * c:x * 32 + 4 * c + 4].unsqueeze(2).broadcast_to([128, 4, 128]),
                                                   ALU.mult), t_w, LW[2], r_gt[j])
            pbf[p] = r_gt[j] = ty = dve.do(lambda e: e.scalar_tensor_tensor(YT[j], bank[:, :], w("eb2", 128, x, x + 1), GT[j], ALU.add, ALU.mult),
                                           tp, gt, r_yt[j])
            r_yt[j] = acc[c] = pool.do(lambda e: e.tensor_tensor(cs(HF, c), cs(HF, c), YT[j], ALU.add), ty, acc[c])

        prev = None
        for c in range(CH):
            for x in (4, 0, 1, 2, 3):
                cur = (c, x) + up(c, x)
                if prev:
                    down(*prev)
                prev = cur
        down(*prev)

        barrier("s5")
        KTC = [ar(512) for _ in range(2)]
        QTC = [ar(512) for _ in range(2)]
        KMB = [ar(512) for _ in range(2)]
        KQ = [ar(2048).rearrange("p (h j) -> p h j", h=16) for _ in range(2)]
        VXW = 272
        VY = [ar(VXW) for _ in range(3)]
        VT = [ar(128) for _ in range(2)]
        X2 = [ar(512) for _ in range(2)]
        SS = [ar(512) for _ in range(3)]
        PT = [ar(512) for _ in range(2)]
        OS = [ar(128) for _ in range(3)]
        LNB = ar(4096)
        on128 = on32
        mx = [sm(4) for _ in range(3)]
        rc = [sm(4) for _ in range(2)]
        xsum, qm, iqm = sm(32), sm(32), sm(32)
        mv = sm(64)
        bns = [sm(6) for _ in range(2)]
        ov = [pool.do(lambda e, i=i: e.memset(VY[i], 0.0)) for i in range(3)]
        pj_free = [None, None]
        pj_n[0] = 0
        tok_q, tok_k, tok_v, tok_kq, tok_x2 = {}, {}, {}, {}, {}
        last_s, last_pv, last_os, r_k, r_ktc = {}, {}, {}, {}, {}
        k_x2r = {}
        isq8 = float(1.0 / np.sqrt(8))

        def proj5(c):
            i = c % 2
            bank, k = pj()
            tp = pe.do(lambda e: e.matmul(bank[:, :], w("aq"), cs(HF, c), start=True, stop=True), pj_free[k], LW[3])
            pj_free[k] = tq = act.do(lambda e: e.activation(QTC[i], bank[:, :], ACTF.Relu, bias=w("bq")), tp, last_s.get(c - 2))
            tok_q[c] = dve.do(lambda e: e.tensor_scalar(QTC[i], QTC[i], isq8, None, ALU.mult), tq)
            yield
            bank, k = pj()
            tp = pe.do(lambda e: e.matmul(bank[:, :], on128, cs(HF, c), start=True, stop=True), pj_free[k])
            pj_free[k] = tm = dve.do(lambda e: e.tensor_scalar(KMB[i], bank[:, :], 0.0, None, ALU.not_equal), tp, r_ktc.get(c - 2))
            bank, k = pj()
            tp = pe.do(lambda e: e.matmul(bank[:, :], w("ak"), cs(HF, c), start=True, stop=True), pj_free[k])
            pj_free[k] = tk = act.do(lambda e: e.activation(KTC[i], bank[:, :], ACTF.Relu, bias=w("bk")), tp, r_k.get(c - 2))
            r_ktc[c] = tok_k[c] = pool.do(lambda e: e.tensor_tensor(KTC[i], KTC[i], KMB[i], ALU.mult), tk, tm)
            yield
            bank, k = pj()
            for b in range(4):
                tp = pe.do(lambda e: e.transpose(bank[:, b * 128:(b + 1) * 128], HF[:, c * 512 + b * 128:c * 512 + (b + 1) * 128], ident),
                           pj_free[k], inc=b == 3)
            pj_free[k] = tok_x2[c] = act.do(lambda e: e.activation(X2[i], bank[:, :], ACTF.Copy), tp, k_x2r.get(c - 2))
            t = dve.do(lambda e: e.tensor_reduce(xsum[:, 4 * c:4 * c + 4], v4(X2[i]), AX.X, ALU.add), tok_x2[c])
            ta = dve.do(lambda e: e.tensor_scalar(qm[:, 4 * c:4 * c + 4], xsum[:, 4 * c:4 * c + 4], 0.0, None, ALU.not_equal), t)
            tok_v[("m", c)] = dve.do(lambda e: e.tensor_scalar(iqm[:, 4 * c:4 * c + 4], qm[:, 4 * c:4 * c + 4], -1.0, 1.0, ALU.mult, ALU.add), ta)
            yield

        def projb(q):
            c, b = q // 4, q % 4
            i = c % 2
            sl = slice(b * 128, (b + 1) * 128)
            r_k[c] = tok_kq[q] = pool.do(lambda e: e.tensor_tensor(KQ[q % 2], KTC[i][:, sl].unsqueeze(1).broadcast_to([128, 16, 128]),
                                                          w("hm").unsqueeze(2).broadcast_to([128, 16, 128]), ALU.mult),
                                tok_k[c], last_s.get(("b", q - 2)), LW[3])
            bank, k = pj()
            tp = pe.do(lambda e: e.matmul(bank[:, 0:128], HF[:, q * 128:(q + 1) * 128], w("av"), start=True, stop=True), pj_free[k])
            pj_free[k] = t = dve.do(lambda e: e.tensor_tensor(VT[q % 2], bank[:, 0:128], w("bv"), ALU.add), tp, tok_v.get(("t", q - 2)))
            vv = VY[q % 3][:, 0:144].rearrange("p (h v) -> p h v", v=9)
            ta = dve.do(lambda e: e.tensor_scalar(vv[:, :, 0:8], VT[q % 2].rearrange("p (h v) -> p h v", v=8), 0.0,
                                                  qm[:, q:q + 1], ALU.max, ALU.mult), t, tok_v[("m", c)], ov[q % 3], last_pv.get(("b", q - 3)))
            tok_v[("t", q)] = ta
            tok_v[q] = [ta, dve.do(lambda e: e.tensor_copy(vv[:, :, 8:9], qm[:, q:q + 1].unsqueeze(1).broadcast_to([128, 16, 1])))]

        units = [(q, g) for q in range(32) for g in range(4)]
        U = len(units)
        k_sub, k_exp, k_T, k_cp, k_pv, k_on = ({} for _ in range(6))
        os_w, ln_done, bn_r = {}, {}, {}

        def b_S(u):
            q, g = units[u]
            c, b = q // 4, q % 4
            bank = PB[u % 2]
            pe.do(lambda e: e.matmul(bank[:, :], identb[:, :], maskb[:, :], start=True, stop=False), k_sub.get(u - 2), inc=False)
            t = pe.do(lambda e: e.matmul(bank[:, :], QTC[c % 2][:, b * 128:(b + 1) * 128],
                                         KQ[q % 2][:, 4 * g:4 * g + 4, :].rearrange("p h j -> p (h j)"), start=False, stop=True),
                      tok_q[c], tok_kq[q])
            last_s[c] = last_s[("b", q)] = t
            m = mx[u % 3]
            b3 = bank[:, :].rearrange("p (h j) -> p h j", h=4)
            t = dve.do(lambda e: e.tensor_reduce(m, b3, AX.X, ALU.max), t)
            t = dve.do(lambda e: e.tensor_tensor(SS[u % 3].rearrange("p (h j) -> p h j", h=4), b3,
                                                 m.unsqueeze(2).broadcast_to([128, 4, 128]), ALU.subtract), t, k_T.get(u - 3))
            k_sub[u] = t
            k_exp[u] = act.do(lambda e: e.activation(SS[u % 3], SS[u % 3], ACTF.Exp), t)

        def b_T(u):
            bank = PB[2 + u % 2]
            for h in range(4):
                t = pe.do(lambda e: e.transpose(bank[:, h * 128:(h + 1) * 128], SS[u % 3][:, h * 128:(h + 1) * 128], ident),
                          k_exp[u], k_cp.get(u - 2), inc=h == 3)
            k_T[u] = t
            k_cp[u] = act.do(lambda e: e.activation(PT[u % 2], bank[:, :], ACTF.Copy), t, k_pv.get(u - 2))

        def b_PV(u):
            q, g = units[u]
            c, b = q // 4, q % 4
            bank = PB[4 + u % 2]
            for h in range(4):
                o = 9 * (4 * g + h)
                t = pe.do(lambda e: e.matmul(bank[:, h * 128:(h + 1) * 128], PT[u % 2][:, h * 128:(h + 1) * 128],
                                             VY[q % 3][:, o:o + 128], start=True, stop=True),
                          k_cp[u], tok_v[q], k_on.get(u - 2), inc=h == 3)
            k_pv[u] = t
            last_pv[("b", q)] = t
            o3 = bank[:, :].rearrange("p (h v) -> p h v", h=4)
            t = dve.do(lambda e: e.tensor_scalar(rc[u % 2].unsqueeze(2), o3[:, :, 8:9], iqm[:, q:q + 1], None, ALU.add), t)
            t = dve.do(lambda e: e.reciprocal(rc[u % 2], rc[u % 2]), t)
            t = dve.do(lambda e: e.tensor_scalar(rc[u % 2], rc[u % 2], qm[:, q:q + 1], None, ALU.mult), t)
            k_on[u] = dve.do(lambda e: e.tensor_tensor(OS[q % 3][:, 32 * g:32 * g + 32].rearrange("p (h v) -> p h v", h=4), o3[:, :, 0:8],
                                                       rc[u % 2].unsqueeze(2).broadcast_to([128, 4, 8]), ALU.mult), t, ln_done.get(q - 3))
            if g < 3:
                return
            sl = slice(b * 128, (b + 1) * 128)
            ln_done[q] = k_x2r[c] = t = dve.do(lambda e: e.tensor_tensor(cs(LNB, q, 128), OS[q % 3], X2[c % 2][:, sl], ALU.add), k_on[u], tok_x2[c])
            t = dve.do(lambda e: e.bn_stats(bns[q % 2], cs(LNB, q, 128)), t)
            bn_r[q] = dve.do(lambda e: e.bn_aggr(mv[:, 2 * q:2 * q + 2], bns[q % 2]), t)

        for _ in proj5(0):
            pass
        projb(0)
        filler = iter(())
        for s in range(U + 2):
            if s < U:
                q, g = units[s]
                if g == 0 and q % 4 == 0:
                    for _ in filler:
                        pass
                    filler = proj5(q // 4 + 1) if q // 4 + 1 < 8 else iter(())
                if g == 2 and q % 4 != 3:
                    projb(q + 1)
                if g == 0 and q % 4 == 3:
                    for _ in filler:
                        pass
                if g == 2 and q % 4 == 3 and q + 1 < 32:
                    projb(q + 1)
                b_S(s)
            if 0 <= s - 1 < U:
                b_T(s - 1)
            if 0 <= s - 2 < U:
                b_PV(s - 2)
            if s % 4 == 1:
                next(filler, None)

        rstd = sm(32)
        m3 = mv.rearrange("p (q s) -> p q s", s=2)
        t = act.do(lambda e: e.activation(rstd.unsqueeze(2), m3[:, :, 1:2], ACTF.Sqrt, bias=c_eps8), list(bn_r.values()))
        t_r = dve.do(lambda e: e.reciprocal(rstd, rstd), t)
        tx3, tx3T = {}, {}
        for c in range(CH):
            bank, k = pj()
            for b in range(4):
                q = 4 * c + b
                tp = pe.do(lambda e: e.transpose(bank[:, b * 128:(b + 1) * 128], XF[:, q * 128:(q + 1) * 128], ident), pj_free[k], inc=b == 3)
                t = dve.do(lambda e: e.tensor_scalar(cs(LNB, q, 128), cs(LNB, q, 128), m3[:, q, 0:1], rstd[:, q:q + 1], ALU.subtract, ALU.mult), t_r, bn_r[q])
                t = pool.do(lambda e: e.tensor_tensor(cs(LNB, q, 128), cs(LNB, q, 128), w("gamma"), ALU.mult), t)
                t = pool.do(lambda e: e.tensor_tensor(cs(LNB, q, 128), cs(LNB, q, 128), w("beta"), ALU.add), t)
            pj_free[k] = tx3[c] = dve.do(lambda e: e.tensor_tensor(cs(XT, c), bank[:, :], cs(LNB, c), ALU.add), tp, t)
        for c in range(CH):
            bank, k = pj()
            for b in range(4):
                q = 4 * c + b
                tp = pe.do(lambda e: e.transpose(bank[:, b * 128:(b + 1) * 128], XT[:, q * 128:(q + 1) * 128], ident), pj_free[k], tx3[c], inc=b == 3)
            pj_free[k] = tx3T[c] = act.do(lambda e: e.activation(cs(XF, c), bank[:, :], ACTF.Copy), tp)

        barrier("s6")
        ae = ar(128)
        st6, mv6, r6 = sm(6), sm(2), sm(1)
        t = dve.do(lambda e: e.bn_stats(st6[0:R, :], w("cond", R)))
        t = dve.do(lambda e: e.bn_aggr(mv6[0:R, :], st6[0:R, :]), t)
        t = act.do(lambda e: e.activation(r6[0:R, :], mv6[0:R, 1:2], ACTF.Sqrt, bias=c_eps5[0:R, :]), t)
        t = dve.do(lambda e: e.reciprocal(r6[0:R, :], r6[0:R, :]), t)
        t = dve.do(lambda e: e.tensor_scalar(ae[0:R, :], w("cond", R), mv6[0:R, 0:1], r6[0:R, :], ALU.subtract, ALU.mult), t)
        t = dve.do(lambda e: e.tensor_tensor(ae[0:R, :], ae[0:R, :], w("lng", R), ALU.mult), t)
        t = dve.do(lambda e: e.tensor_tensor(ae[0:R, :], ae[0:R, :], w("lnb", R), ALU.add), t)
        aeT, hT = ar(32), ar(32)
        t = pe.do(lambda e: e.transpose(PB[0][:, 0:32], ae[0:R, :], ident[0:R, 0:R]), t)
        t = dve.do(lambda e: e.tensor_copy(aeT, PB[0][:, 0:32]), t)
        t = pe.do(lambda e: e.matmul(PB[1][:, 0:32], w("lw1"), aeT, start=True, stop=True), t)
        t_h = act.do(lambda e: e.activation(hT, PB[1][:, 0:32], ACTF.Gelu, bias=w("lb1")), t)
        HX = ar(2048)
        hx4 = HX.rearrange("p (r b s) -> p r b s", r=8, b=32)
        tz = pool.do(lambda e: e.memset(HX, 0.0))
        for r in range(8):
            t_hx = pool.do(lambda e: e.tensor_copy(hx4[:, r, :, r:r + 1], hT.unsqueeze(2)), tz, t_h)
        XA = ar(256).rearrange("p (b r) -> p b r", r=8)
        XBP = [ar(128) for _ in range(2)]
        for r in range(8):
            tp = pe.do(lambda e: e.matmul(PB[2][:, 32 * r:32 * r + 32], w("lw2a", 128, r * 128, (r + 1) * 128), hT, start=True, stop=True), t_h, inc=r == 7)
        for r in range(8):
            t_xa = dve.do(lambda e: e.tensor_scalar(XA[:, :, r:r + 1], PB[2][:, 32 * r:32 * r + 32].unsqueeze(2), w("lb2a", 128, r, r + 1), None, ALU.add), tp)
        t_xb = []
        for hh in range(2):
            for r in range(8):
                tp = pe.do(lambda e: e.matmul(PB[3 + hh][:, 0:128], hx4[:, r, 16 * hh:16 * hh + 16, :].rearrange("p b s -> p (b s)"),
                                              w("lw2b", 128, r * 128, (r + 1) * 128), start=r == 0, stop=r == 7), t_hx, inc=r == 7)
            t_xb.append(dve.do(lambda e: e.tensor_tensor(XBP[hh], PB[3 + hh][:, 0:128], w("lb2b"), ALU.add), tp))
        GG = [ar(512) for _ in range(2)]
        r_gg = [None, None]
        fr6 = [t_xb] * 8
        tx4 = {}
        for c in range(CH):
            hh, i = c // 4, c % 2
            k = 2 * (c % 2)
            tp = pe.do(lambda e: e.matmul(PB[k][:, :], XA[:, 16 * hh:16 * hh + 16, :].rearrange("p b r -> p (b r)"), cs(XF, c), start=True, stop=True),
                       t_xa, fr6[k])
            fr6[k] = tg = dve.do(lambda e: e.tensor_tensor(v4(GG[i]), v4(PB[k][:, :]),
                                                           w("bm16", 128, 4 * (c % 4), 4 * (c % 4) + 4).unsqueeze(2).broadcast_to([128, 4, 128]), ALU.mult),
                                 tp, r_gg[i])
            pe.do(lambda e: e.matmul(PB[k + 1][:, :], w("base"), cs(XF, c), start=True, stop=False), fr6[k + 1], inc=False)
            r_gg[i] = tp = pe.do(lambda e: e.matmul(PB[k + 1][:, :], XBP[hh], GG[i], start=False, stop=True), tg, t_xb)
            fr6[k + 1] = tx4[c] = dve.do(lambda e: e.tensor_tensor(cs(HF, c), cs(XF, c), PB[k + 1][:, :], ALU.add), tp)

        barrier("s7")
        smean, b1e, tinv, b2s = sm(1), sm(1), sm(1), sm(64)
        t = dve.do(lambda e: e.tensor_reduce(smean, w("slotT"), AX.X, ALU.add))
        t = dve.do(lambda e: e.tensor_scalar(smean, smean, 1.0 / 64, None, ALU.mult), t)
        t = pe.do(lambda e: e.matmul(PB[7][0:64, 0:1], w("fw1b"), smean, start=True, stop=True), t)
        t_b1 = dve.do(lambda e: e.tensor_tensor(b1e[0:64, :], PB[7][0:64, 0:1], w("fb1", 64), ALU.add), t)
        ta = dve.do(lambda e: e.tensor_scalar(tinv, w("tau"), -1.0, None, ALU.mult))
        ta = dve.do(lambda e: e.tensor_tensor(tinv, tinv, w("tau"), ALU.max), ta)
        ta = dve.do(lambda e: e.tensor_scalar(tinv, tinv, 0.1, None, ALU.add), ta)
        t_ti = dve.do(lambda e: e.reciprocal(tinv, tinv), ta)
        AL = ar(2048)
        XTM = ar(4096)
        H1 = [ar(512) for _ in range(2)]
        LG = [ar(256) for _ in range(2)]
        MR = [ar(256) for _ in range(2)]
        m8 = [sm(32) for _ in range(2)]
        sums = [sm(4) for _ in range(2)]
        r_h, r_lg, fr7, txm, tal = [None, None], [None, None], [t_b1] * 8, {}, {}
        for c in range(CH):
            i = c % 2
            k = 4 * i
            tp = pe.do(lambda e: e.matmul(PB[k][0:64, :], w("fw1a"), cs(HF, c), start=True, stop=True), fr7[k])
            fr7[k] = th = act.do(lambda e: e.activation(H1[i][0:64, :], PB[k][0:64, :], ACTF.Gelu, bias=b1e[0:64, :]), tp, t_b1, r_h[i])
            for b in range(4):
                r_h[i] = tp = pe.do(lambda e: e.matmul(PB[k + 1][:, b * 64:(b + 1) * 64], H1[i][0:64, b * 128:(b + 1) * 128], w("fw2", 64), start=True, stop=True),
                                    th, fr7[k + 1], inc=b == 3)
            l3 = LG[i].rearrange("p (b s) -> p b s", b=4)
            fr7[k + 1] = t = dve.do(lambda e: e.tensor_tensor(l3, PB[k + 1][:, 0:256].rearrange("p (b s) -> p b s", b=4),
                                                     w("fb2").unsqueeze(1).broadcast_to([128, 4, 64]), ALU.add), tp, r_lg[i])
            t = dve.do(lambda e: e.tensor_scalar(LG[i], LG[i], tinv, None, ALU.mult), t, t_ti)
            tq = []
            for b in range(4):
                sl = slice(b * 64, (b + 1) * 64)
                t8 = dve.do(lambda e: e.max(m8[i][:, 8 * b:8 * b + 8], LG[i][:, sl]), t, r_lg[i])
                tq.append(t8)
            for b in range(4):
                sl = slice(b * 64, (b + 1) * 64)
                tr = dve.do(lambda e: e.match_replace(out=MR[i][:, sl], in_to_replace=m8[i][:, 8 * b:8 * b + 8], in_values=LG[i][:, sl], imm_value=-3.0e38), tq[b])
            t = dve.do(lambda e: e.tensor_tensor(MR[i], MR[i], LG[i], ALU.not_equal), tr)
            t8 = m8[i].rearrange("p (b e) -> p b e", b=4)[:, :, 0:1].broadcast_to([128, 4, 64])
            t2 = dve.do(lambda e: e.tensor_tensor(l3, l3, t8, ALU.subtract), t)
            t2 = act.do(lambda e: e.activation(LG[i], LG[i], ACTF.Exp), t2)
            t = pool.do(lambda e: e.tensor_tensor(LG[i], LG[i], MR[i], ALU.mult), t2)
            t = dve.do(lambda e: e.tensor_reduce(sums[i], l3, AX.X, ALU.add), t)
            t = dve.do(lambda e: e.reciprocal(sums[i], sums[i]), t)
            r_lg[i] = tal[c] = dve.do(lambda e: e.tensor_tensor(AL[:, c * 256:(c + 1) * 256].rearrange("p (b s) -> p b s", b=4), l3,
                                                       sums[i].unsqueeze(2).broadcast_to([128, 4, 64]), ALU.mult), t)
            for b in range(4):
                q = 4 * c + b
                tp = pe.do(lambda e: e.transpose(PB[k + 2][:, b * 128:(b + 1) * 128], HF[:, q * 128:(q + 1) * 128], ident), fr7[k + 2], inc=b == 3)
            fr7[k + 2] = txm[c] = act.do(lambda e: e.activation(cs(XTM, c), PB[k + 2][:, :], ACTF.Copy), tp)

        barrier_toks = [e.last() for e in engines]
        SI, GI, SN = HF[:, 0:2048], HF[:, 2048:4096], ar(2048)
        RG = ar(2048)
        ghT = ar(192).rearrange("p (g s) -> p g s", g=3)
        on_ = on32
        k = 0
        for g in range(3):
            tp = pe.do(lambda e: e.matmul(PB[7][:, g * 64:(g + 1) * 64], w("whhT", 128, g * 128, (g + 1) * 128), w("slotT"), start=True, stop=True), fr7[7], inc=g == 2)
        for g in range(3):
            t_gh = dve.do(lambda e: e.tensor_scalar(ghT[:, g, :], PB[7][:, g * 64:(g + 1) * 64], w("bhh", 128, g, g + 1), None, ALU.add), tp)
        bih_g = w("bih")
        fr7 = [barrier_toks] * 8
        tsi = {}
        for c in range(4):
            k = 2 * (c % 2)
            for b in range(8):
                q = 8 * c + b
                tp = pe.do(lambda e: e.matmul(PB[k][:, b * 64:(b + 1) * 64], XTM[:, q * 128:(q + 1) * 128], AL[:, q * 64:(q + 1) * 64], start=True, stop=True),
                           fr7[k], inc=b == 7)
            tp2 = pe.do(lambda e: e.matmul(PB[k + 1][:, :], on_, cs(AL, c), start=True, stop=True), fr7[k + 1])
            t = act.do(lambda e: e.activation(cs(RG, c), PB[k + 1][:, :], ACTF.Ln, bias=c_eps8), tp2)
            fr7[k + 1] = t
            t = act.do(lambda e: e.activation(cs(RG, c), cs(RG, c), ACTF.Exp, scale=-1.0), t)
            fr7[k] = tsi[c] = dve.do(lambda e: e.tensor_tensor(cs(SI, c), PB[k][:, :], cs(RG, c), ALU.mult), tp, t, barrier_toks)

        def v8(ap):
            return ap.rearrange("p (b s) -> p b s", b=8)

        tsn = {}
        for c in range(4):
            def gate(g, k):
                return pe.do(lambda e: e.matmul(PB[k][:, :], w("wihT", 128, g * 128, (g + 1) * 128), cs(SI, c), start=True, stop=True), tsi[c], fr7[k])

            def ghb(g):
                return ghT[:, g, :].unsqueeze(1).broadcast_to([128, 8, 64])

            tr = gate(0, 4)
            fr7[4] = t = dve.do(lambda e: e.tensor_tensor(v8(cs(RG, c)), v8(PB[4][:, :]), ghb(0), ALU.add), tr, t_gh, tsi[c])
            t_r = act.do(lambda e: e.activation(cs(RG, c), cs(RG, c), ACTF.Sigmoid, bias=bih_g[:, 0:1]), t)
            tz = gate(1, 5)
            fr7[5] = t = dve.do(lambda e: e.tensor_tensor(v8(cs(GI, c)), v8(PB[5][:, :]), ghb(1), ALU.add), tz, barrier_toks)
            t_z = act.do(lambda e: e.activation(cs(GI, c), cs(GI, c), ACTF.Sigmoid, bias=bih_g[:, 1:2]), t)
            tn = gate(2, 6)
            t = dve.do(lambda e: e.tensor_tensor(v8(cs(RG, c)), v8(cs(RG, c)), ghb(2), ALU.mult), t_r)
            fr7[6] = t = dve.do(lambda e: e.tensor_tensor(cs(RG, c), cs(RG, c), PB[6][:, :], ALU.add), t, tn)
            t_n = act.do(lambda e: e.activation(cs(RG, c), cs(RG, c), ACTF.Tanh, bias=bih_g[:, 2:3]), t)
            t = dve.do(lambda e: e.tensor_tensor(v8(cs(SN, c)), w("slotT").unsqueeze(1).broadcast_to([128, 8, 64]), v8(cs(RG, c)), ALU.subtract), t_n)
            t = dve.do(lambda e: e.tensor_tensor(cs(SN, c), cs(SN, c), cs(GI, c), ALU.mult), t, t_z)
            tsn[c] = dve.do(lambda e: e.tensor_tensor(cs(SN, c), cs(SN, c), cs(RG, c), ALU.add), t)

        QS, KS = ar(512), ar(512)
        VS = ar(2048)
        P7 = ar(512)
        PT7 = ar(512)
        Y7 = ar(512)
        YN = SI
        SV = GI
        AT = RG
        sc7 = float(32.0 ** -0.5)
        mx7, sm7 = sm(4), sm(4)
        bn7, mv7, rs7 = sm(24), sm(8), sm(4)
        t_prev = [e.last() for e in engines]
        fr7 = [t_prev] * 8
        tyn = {}
        pm = w("pmask").unsqueeze(1).broadcast_to([128, 4, 128])
        for c in range(4):
            tp = pe.do(lambda e: e.matmul(PB[0][0:32, :], w("fwq"), cs(SN, c), start=True, stop=True), fr7[0], tsn[c])
            fr7[0] = tq = dve.do(lambda e: e.tensor_scalar(QS[0:32, :], PB[0][0:32, :], w("fbq", 32), sc7, ALU.add, ALU.mult), tp)
            tp = pe.do(lambda e: e.matmul(PB[1][0:32, :], w("fwk"), cs(SN, c), start=True, stop=True), fr7[1])
            fr7[1] = tk = dve.do(lambda e: e.tensor_scalar(KS[0:32, :], PB[1][0:32, :], w("fbk", 32), None, ALU.add), tp)
            for p in range(4):
                sl = slice(p * 128, (p + 1) * 128)
                tp = pe.do(lambda e: e.matmul(PB[2][:, sl], cs(SN, c)[:, sl], w("fwv"), start=True, stop=True), fr7[2], inc=p == 3)
            fr7[2] = tv = dve.do(lambda e: e.tensor_tensor(v4(cs(VS, c)), v4(PB[2][:, :]), w("fbv").unsqueeze(1).broadcast_to([128, 4, 128]), ALU.add), tp)
            for p in range(4):
                sl = slice(p * 128, (p + 1) * 128)
                tp = pe.do(lambda e: e.matmul(PB[3][:, sl], QS[0:32, sl], KS[0:32, sl], start=True, stop=True), fr7[3], tq, tk, inc=p == 3)
            t = fr7[3] = dve.do(lambda e: e.tensor_tensor(v4(P7), v4(PB[3][:, :]), pm, ALU.add), tp)
            t = dve.do(lambda e: e.tensor_reduce(mx7, v4(P7), AX.X, ALU.max), t)
            t = dve.do(lambda e: e.tensor_tensor(v4(P7), v4(P7), mx7.unsqueeze(2).broadcast_to([128, 4, 128]), ALU.subtract), t)
            t = act.do(lambda e: e.activation(P7, P7, ACTF.Exp), t)
            t = dve.do(lambda e: e.tensor_reduce(sm7, v4(P7), AX.X, ALU.add), t)
            t = dve.do(lambda e: e.reciprocal(sm7, sm7), t)
            t = dve.do(lambda e: e.tensor_tensor(v4(P7), v4(P7), sm7.unsqueeze(2).broadcast_to([128, 4, 128]), ALU.mult), t)
            for p in range(4):
                sl = slice(p * 128, (p + 1) * 128)
                tp = pe.do(lambda e: e.transpose(PB[4][:, sl], P7[:, sl], ident), t, fr7[4], inc=p == 3)
            fr7[4] = t = act.do(lambda e: e.activation(PT7, PB[4][:, :], ACTF.Copy), tp)
            for p in range(4):
                sl = slice(p * 128, (p + 1) * 128)
                pe.do(lambda e: e.matmul(PB[5][:, sl], cs(SN, c)[:, sl], ident, start=True, stop=False), fr7[5], inc=False)
                tp = pe.do(lambda e: e.matmul(PB[5][:, sl], PT7[:, sl], cs(VS, c)[:, sl], start=False, stop=True), t, tv, inc=p == 3)
            fr7[5] = t = dve.do(lambda e: e.tensor_copy(Y7, PB[5][:, :]), tp)
            for p in range(4):
                sl = slice(p * 128, (p + 1) * 128)
                tb = dve.do(lambda e: e.bn_stats(bn7[:, 6 * p:6 * p + 6], Y7[:, sl]), t)
                tb = dve.do(lambda e: e.bn_aggr(mv7[:, 2 * p:2 * p + 2], bn7[:, 6 * p:6 * p + 6]), tb)
            t = act.do(lambda e: e.activation(rs7.unsqueeze(2), mv7.rearrange("p (q s) -> p q s", s=2)[:, :, 1:2], ACTF.Sqrt, bias=c_eps5), tb)
            t = dve.do(lambda e: e.reciprocal(rs7, rs7), t)
            for p in range(4):
                sl = slice(p * 128, (p + 1) * 128)
                tn = dve.do(lambda e: e.tensor_scalar(Y7[:, sl], Y7[:, sl], mv7[:, 2 * p:2 * p + 1], rs7[:, p:p + 1], ALU.subtract, ALU.mult), t)
            t = dve.do(lambda e: e.tensor_tensor(v4(Y7), v4(Y7), w("flng").unsqueeze(1).broadcast_to([128, 4, 128]), ALU.mult), tn)
            t = dve.do(lambda e: e.tensor_tensor(v4(Y7), v4(Y7), w("flnb").unsqueeze(1).broadcast_to([128, 4, 128]), ALU.add), t)
            for p in range(4):
                sl = slice(p * 128, (p + 1) * 128)
                tp = pe.do(lambda e: e.transpose(PB[6][:, sl], Y7[:, sl], ident), t, fr7[6], inc=p == 3)
            fr7[6] = t = act.do(lambda e: e.activation(cs(YN, c), PB[6][:, :], ACTF.Copy), tp, tsn[c])
            tp = pe.do(lambda e: e.matmul(PB[7][:, :], w("wvp"), cs(YN, c), start=True, stop=True), t, fr7[7])
            fr7[7] = t = dve.do(lambda e: e.tensor_scalar(cs(SV, c), PB[7][:, :], w("bvp"), None, ALU.add), tp)
            for p in range(4):
                sl = slice(p * 128, (p + 1) * 128)
                tp = pe.do(lambda e: e.matmul(PB[0][:, sl], cs(SV, c)[:, sl], w("wo"), start=True, stop=True), t, fr7[0], inc=p == 3)
            fr7[0] = tyn[c] = act.do(lambda e: e.activation(cs(VS, c), PB[0][:, :], ACTF.Copy), tp)

        ATT = [ar(512) for _ in range(2)]
        r_at, fo = [None, None], [[e.last() for e in engines]] * 8
        s_toks = []
        for c in range(CH):
            i = c % 2
            k = 2 * i
            for p in range(2):
                m = 2 * c + p
                tp = pe.do(lambda e: e.transpose(PB[k][:, p * 128:(p + 1) * 128], AL[:, m * 128:(m + 1) * 128], ident), fo[k], inc=p == 1)
            fo[k] = ta = act.do(lambda e: e.activation(ATT[i][:, 0:256], PB[k][:, 0:256], ACTF.Copy), tp, r_at[i])
            for p in range(2):
                for hh in range(2):
                    m = 2 * c + p
                    r_at[i] = tp = pe.do(lambda e: e.matmul(PB[k + 1 + 4 * hh][:, p * 128:(p + 1) * 128], ATT[i][64 * hh:64 * hh + 64, p * 128:(p + 1) * 128],
                                                   VS[64 * hh:64 * hh + 64, m * 128:(m + 1) * 128], start=True, stop=True),
                                         ta, tyn[c // 2], fo[k + 1], fo[k + 5], inc=(p, hh) == (1, 1))
            x4 = cs(XT, c).rearrange("p (q hh t) -> p q hh t", q=2, hh=2)
            for hh in range(2):
                fo[k + 1 + 4 * hh] = t = dve.do(lambda e: e.tensor_tensor(x4[:, :, hh, :], x4[:, :, hh, :],
                                                            PB[k + 1 + 4 * hh][:, 0:256].rearrange("p (q t) -> p q t", q=2), ALU.add), tp)
            t = pool.do(lambda e: e.tensor_tensor(v4(cs(XT, c)), v4(cs(XT, c)), w("bo").unsqueeze(1).broadcast_to([128, 4, 128]), ALU.add), t)
            nc.sync.wait_ge(t[0], t[1])
            nc.sync.dma_start(out_d[4 * c:4 * c + 4, :, :].rearrange("b t d -> t b d"), v4(cs(XT, c))).then_inc(s_out, 16)
        nc.sync.wait_ge(s_out, 16 * CH)


def pack(inp):
    f = np.float32
    wide = np.zeros((128, WIDE), f)

    def put(name, a):
        o, c = OFF[name]
        a = np.asarray(a)
        assert a.shape[1] == c, (name, a.shape)
        wide[0:a.shape[0], o:o + c] = a

    def col(name, a):
        put(name, np.asarray(a).reshape(-1, 1))

    def row(name, a, rows=128):
        a = np.asarray(a).reshape(1, -1)
        put(name, np.broadcast_to(a, (rows, a.shape[1])))

    def blocks(a, n):
        a = np.asarray(a)
        return a.reshape(n, 128, a.shape[-1]).transpose(1, 0, 2).reshape(128, -1)

    put("condT", np.asarray(inp["cond_1024"]).T)
    put("w0", inp["L0_cond_weight"])
    put("ident", np.eye(128, dtype=f))
    i, j = np.arange(128)[:, None], np.arange(128)[None, :]
    put("mask", np.tile(np.where(j > i, f(NEG), f(0)), (1, 4)))
    put("wqkv", inp["L0_attn_W_qkv"])
    put("wout", blocks(inp["L0_attn_W_out"], 8))
    for n, k in (("f", "f"), ("i", "i"), ("h", "h")):
        put(f"w{n}T", np.asarray(inp[f"L0_cond2_W_{k}"]).T)
        col(f"b{n}", inp[f"L0_cond2_b_{k}"])
    for k in (1, 2, 3):
        put(f"cw{k}", inp[f"L0_ffn_cn_w{k}"])
        col(f"cb{k}", inp[f"L0_ffn_cn_b{k}"])
    put("cw4", np.broadcast_to(np.asarray(inp["L0_ffn_cn_w4"]), (32, 128)))
    row("cb4", inp["L0_ffn_cn_b4"])
    for k in (1, 2):
        put(f"gw{k}", inp[f"L0_ffn_gc_w{k}"])
        col(f"gb{k}", inp[f"L0_ffn_gc_b{k}"])
    put("gw3", np.broadcast_to(np.asarray(inp["L0_ffn_gc_w3"]), (32, 128)))
    row("gb3", inp["L0_ffn_gc_b3"])
    row("ar", inp["L0_ffn_adaptive_range"])
    tw = np.zeros((128, 128), f)
    r = np.arange(32)
    tw[64 + r, r] = 1
    tw[96 + r, 32 + r] = -1
    tw[r, 64 + r] = -1
    tw[32 + r, 96 + r] = 1
    put("twist", tw)
    put("gatew", blocks(inp["L1_cond_gate_w"], 3))
    row("gateb", inp["L1_cond_gate_b"], 32)
    put("timew", inp["L1_cond_time_w"])
    row("timeb", inp["L1_cond_time_b"], 32)
    lower = np.zeros((4, 4), f)
    for a in range(4):
        lower[a, :a] = 1
    row("lower", lower, 32)
    put("ew1", np.asarray(inp["L1_cond_ew1"]).transpose(1, 0, 2).reshape(128, 2048))
    put("eb1", np.asarray(inp["L1_cond_eb1"]).reshape(16, 128).T)
    put("ew2", blocks(np.asarray(inp["L1_cond_ew2"]).reshape(2048, 128), 16))
    put("eb2", np.asarray(inp["L1_cond_eb2"]).T)
    put("sw1", inp["L1_cond_sw1"])
    put("sb1", np.asarray(inp["L1_cond_sb1"]).reshape(4, 128).T)
    put("sw2", blocks(inp["L1_cond_sw2"], 4))
    col("sb2", inp["L1_cond_sb2"])
    em = np.ones((4, 128), f)
    em[1, 42:84] = 0
    em[2, 0:42] = 0
    row("emask", em)
    for n, k in (("q", "q"), ("k", "k")):
        put(f"a{n}", inp[f"L1_attn_W{k}"])
        col(f"b{n}", inp[f"L1_attn_b{k}"])
    put("av", inp["L1_attn_Wv"])
    row("bv", inp["L1_attn_bv"])
    row("gamma", inp["L1_attn_gamma"])
    row("beta", inp["L1_attn_beta"])
    put("hm", (np.arange(128)[:, None] // 8 == np.arange(16)[None, :]).astype(f))
    put("cond", inp["cond_1024"])
    row("lng", inp["L1_cond2_ln_g"], 32)
    row("lnb", inp["L1_cond2_ln_b"], 32)
    put("lw1", inp["L1_cond2_w1"])
    col("lb1", inp["L1_cond2_b1"])
    w2 = np.asarray(inp["L1_cond2_w2"]).reshape(128, 2, 128, 8).transpose(1, 0, 3, 2)
    put("lw2a", w2[0].reshape(128, 1024))
    put("lw2b", w2[1].reshape(128, 1024))
    b2 = np.asarray(inp["L1_cond2_b2"]).reshape(2, 128, 8)
    put("lb2a", b2[0])
    put("lb2b", np.tile(b2[1].T, (16, 1)))
    put("base", inp["L1_cond2_base_layer"])
    put("bm16", (np.arange(128)[:, None] // 8 == np.arange(16)[None, :]).astype(f))
    w1 = np.asarray(inp["L1_ffn_w1"])
    put("fw1a", w1[:128])
    put("fw1b", w1[128:])
    col("fb1", inp["L1_ffn_b1"])
    put("fw2", inp["L1_ffn_w2"])
    row("fb2", inp["L1_ffn_b2"])
    row("tau", inp["L1_ffn_tau"])
    put("wihT", np.asarray(inp["L1_ffn_Wih"]).T)
    put("whhT", np.asarray(inp["L1_ffn_Whh"]).T)
    put("bih", np.asarray(inp["L1_ffn_bih"]).reshape(3, 128).T)
    put("bhh", np.asarray(inp["L1_ffn_bhh"]).reshape(3, 128).T)
    put("slotT", np.asarray(inp["L1_ffn_slot_init"]).T)
    put("fwq", inp["L1_ffn_wq"])
    col("fbq", inp["L1_ffn_bq"])
    put("fwk", inp["L1_ffn_wk"])
    col("fbk", inp["L1_ffn_bk"])
    put("fwv", inp["L1_ffn_wv"])
    row("fbv", inp["L1_ffn_bv"])
    row("flng", inp["L1_ffn_ln_g"])
    row("flnb", inp["L1_ffn_ln_b"])
    put("wvp", inp["L1_ffn_wvp"])
    col("bvp", inp["L1_ffn_bvp"])
    put("wo", inp["L1_ffn_wo"])
    row("bo", inp["L1_ffn_bo"])
    put("pmask", np.where(i // 64 == j // 64, f(0), f(NEG)))
    xT = np.ascontiguousarray(np.asarray(inp["x"]).reshape(N, D).T)
    return {"in_xT": xT, "in_w": wide}


def kernel(**inputs):
    import concourse.bacc as _bacc
    from concourse.bass_utils import run_bass_kernel_spmd as _run

    nc = _bacc.Bacc("TRN2", target_bir_lowering=False, num_devices=1)
    arrays = pack(inputs)
    aps = [nc.dram_tensor(n, a.shape, F32, kind="ExternalInput").ap() for n, a in arrays.items()]
    out = nc.dram_tensor("out_0", (B, T, D), F32, kind="ExternalOutput").ap()
    build(nc, *aps, out)
    r = _run(nc, [arrays], core_ids=[0])
    return r.results[0]["out_0"]
```

```python
from contextlib import ExitStack

import numpy as np

import concourse.bass as bass
from concourse import mybir

F32 = mybir.dt.float32
F32R = mybir.dt.float32r
BF16 = mybir.dt.bfloat16
ALU = mybir.AluOpType
ACTF = mybir.ActivationFunctionType
AX = mybir.AxisListType

B, T, D = 32, 128, 128
N = B * T
NEG = -1e30

COLS = [
    ("wqT", 1024), ("wkT", 1024), ("w0", 128), ("wvT", 1024), ("wout", 1024),
    ("condT", 32), ("ident", 128), ("mask", 128),
    ("wfT", 128), ("wiT", 128), ("whT", 128), ("bf", 1), ("bi", 1), ("bh", 1),
    ("cw1", 128), ("cw2", 64), ("cw3", 64), ("cw4", 256), ("cb1", 1), ("cb2", 1), ("cb3", 1), ("cb4", 1),
    ("gw1", 64), ("gw2", 32), ("gw3", 128), ("gb1", 1), ("gb2", 1), ("gb3", 1), ("ar", 1), ("twist", 128),
    ("gatew", 12), ("gateb", 4), ("timew", 8), ("timeb", 8), ("lower", 16),
    ("ew1", 2048), ("eb1", 16), ("ew2", 2048), ("eb2", 4), ("sw1", 512), ("sb1", 4), ("sw2", 512), ("sb2", 1),
    ("aq", 128), ("bq", 1), ("ak", 128), ("bk", 1), ("av", 128), ("bv", 128), ("gamma", 1), ("beta", 1),
    ("hm", 4),
    ("cond", 128), ("lng", 128), ("lnb", 128), ("lw1", 128), ("lb1", 1), ("lw2a", 1024), ("lw2b", 1024),
    ("lb2a", 8), ("lb2b", 128), ("base", 128), ("bm16", 16),
    ("fw1a", 64), ("fw1b", 64), ("fb1", 1), ("fw2", 64), ("tau", 1), ("wihT", 384), ("whhT", 384),
    ("bih", 3), ("bhh", 3), ("slotT", 64), ("fwq", 32), ("fbq", 1), ("fwk", 32), ("fbk", 1), ("fwv", 128),
    ("fbv", 128), ("flng", 1), ("flnb", 1), ("wvpT", 128), ("bvp", 1), ("wo", 128), ("bo", 128), ("pmask", 128),
]
OFF, _at = {}, 0
for _n, _c in COLS:
    OFF[_n] = (_at, _c)
    _at += _c
WIDE = _at
FIRST = OFF["condT"][0]


class Queue:

    def __init__(self, eng, new_sem, name):
        self.eng, self.new_sem, self.name = eng, new_sem, name
        self.seen = {}
        self.stage("s0")

    def stage(self, label):
        self.sem = self.new_sem(f"{self.name}_{label}")
        self.n = 0

    def wait(self, toks):
        need = {}
        todo = list(toks)
        while todo:
            t = todo.pop()
            if t is None:
                continue
            if isinstance(t, list):
                todo += t
                continue
            s, v = t
            if v > need.get(id(s), (s, 0))[1]:
                need[id(s)] = (s, v)
        for k, (s, v) in need.items():
            if self.seen.get(k, 0) < v:
                self.eng.wait_ge(s, v)
                self.seen[k] = v

    def do(self, make, *toks, inc=True):
        self.wait(toks)
        ins = make(self.eng)
        if not inc:
            return None
        self.n += 1
        ins.then_inc(self.sem, 1)
        return (self.sem, self.n)

    def last(self):
        return (self.sem, self.n) if self.n else None


def build(nc, xT_d, w_d, out_d):
    ctx = ExitStack()
    with ctx:
        def sb(name, shape, dt=F32):
            return ctx.enter_context(nc.sbuf_tensor(name, shape, dt))

        def new_sem(name):
            return ctx.enter_context(nc.semaphore(name))

        PB = [ctx.enter_context(nc.psum_tensor(f"PB{i}", [128, 512], F32)) for i in range(8)]
        W = sb("W", [128, WIDE - FIRST])
        XF = sb("XF", [128, N])
        HF = sb("HF", [128, N])
        XT = sb("XT", [128, N])
        small = sb("small", [128, 1600])
        scope = ExitStack()
        ctx.callback(scope.close)
        W1 = scope.enter_context(nc.sbuf_tensor("W1", [128, FIRST], F32))

        def w(name, rows=128, a=0, b=None):
            o, c = OFF[name]
            b = c if b is None else b
            if o < FIRST:
                return W1[0:rows, o + a:o + b]
            return W[0:rows, o - FIRST + a:o - FIRST + b]

        used = [0]

        def sm(cols):
            a = used[0]
            used[0] += cols
            assert used[0] <= 1600
            return small[:, a:a + cols]

        area = {}

        def scratch(label, cols, rcols=0):
            area["AR"] = scope.enter_context(nc.sbuf_tensor(f"AR_{label}", [128, cols], F32))
            area["RR"] = scope.enter_context(nc.sbuf_tensor(f"RR_{label}", [128, rcols], F32R)) if rcols else None
            area["a"], area["r"], area["cols"], area["rcols"] = 0, 0, cols, rcols

        def ar(cols):
            a = area["a"]
            area["a"] += cols
            assert area["a"] <= area["cols"], area
            return area["AR"][:, a:a + cols]

        def rr(cols):
            a = area["r"]
            area["r"] += cols
            assert area["r"] <= area["rcols"], area
            return area["RR"][:, a:a + cols]

        pe = Queue(nc.tensor, new_sem, "pe")
        act = Queue(nc.scalar, new_sem, "act")
        dve = Queue(nc.vector, new_sem, "dve")
        pool = Queue(nc.gpsimd, new_sem, "pool")
        engines = [pe, act, dve, pool]
        s_w = [new_sem(f"s_w{i}") for i in range(4)]
        s_x = [new_sem(f"s_x{i}") for i in range(4)]
        s_out = new_sem("s_out")

        o_v = OFF["wvT"][0]
        o_s = OFF["wfT"][0]

        def load_x(i):
            nc.sync.dma_start(XF[:, i * 1024:(i + 1) * 1024], xT_d[:, i * 1024:(i + 1) * 1024]).then_inc(s_x[i], 16)

        nc.sync.dma_start(W[:, 0:o_s - FIRST], w_d[:, FIRST:o_s]).then_inc(s_w[1], 16)
        nc.sync.dma_start(W1[:, 0:o_v], w_d[:, 0:o_v]).then_inc(s_w[0], 16)
        load_x(0)
        nc.sync.dma_start(W1[:, o_v:FIRST], w_d[:, o_v:FIRST]).then_inc(s_w[2], 16)
        for i in range(1, 4):
            load_x(i)
        nc.sync.dma_start(W[:, o_s - FIRST:WIDE - FIRST], w_d[:, o_s:WIDE]).then_inc(s_w[3], 16)
        LQ, LC, LV, LW = [(s, 16) for s in s_w]
        LX = [(s, 16) for s in s_x]

        def barrier(label, cols, rcols=0):
            toks = [e.last() for e in engines]
            for e in engines:
                e.stage(label)
                e.wait(toks)
            scope.close()
            scratch(label, cols, rcols)

        CH = 8

        def cs(tile, c, n=512):
            return tile[:, c * n:(c + 1) * n]

        def v4(ap):
            return ap.rearrange("p (b t) -> p b t", b=4)

        ident = w("ident")

        scratch("s1", 1664, 15360)
        GS = scope.enter_context(nc.sbuf_tensor("GS", [128, 1536], F32))
        pad = pool.do(lambda e: e.memset(small[:, 0:8], 0.0))
        c_eps8, c_eps5, c_zero = sm(1), sm(1), sm(1)
        used[0] = 8
        t = pool.do(lambda e: e.memset(c_eps8, 1e-8), pad)
        eps_tok = pool.do(lambda e: e.memset(c_eps5, 1e-5), t)
        ones = sm(128)
        t_ones = pool.do(lambda e: e.memset(ones, 1.0))

        AH, AL_ = rr(2048), rr(2048)
        BH, BL = rr(2048), rr(2048)
        t_A, t_B, pb_w = [], [], [None] * 4

        def products(lhs, rhs, scale, hi, lo, toks, out):
            for s in range(2):
                for hf in range(2):
                    k = 2 * s + hf
                    for f in range(4):
                        fo = 4 * hf + f
                        tp = pe.do(lambda e: e.matmul(PB[k][:, f * 128:(f + 1) * 128], w(lhs, 128, fo * 128, (fo + 1) * 128)[64 * s:64 * s + 64, :],
                                                      w(rhs, 128, fo * 128, (fo + 1) * 128)[64 * s:64 * s + 64, :], start=True, stop=True),
                                   toks, pb_w[k], inc=f == 3)
                    h_ = hi.rearrange("p (f s j) -> p f s j", f=8, s=2)[:, 4 * hf:4 * hf + 4, s, :]
                    l_ = lo.rearrange("p (f s j) -> p f s j", f=8, s=2)[:, 4 * hf:4 * hf + 4, s, :]
                    b3 = PB[k][:, :].rearrange("p (f j) -> p f j", f=4)
                    t = act.do(lambda e: e.activation(h_, b3, ACTF.Copy, scale=scale), tp)
                    pb_w[k] = t2 = dve.do(lambda e: e.scalar_tensor_tensor(l_, b3, scale, h_, ALU.mult, ALU.subtract), t)
                    out += [t, t2]

        products("wkT", "wqT", -0.125, AH, AL_, LQ, t_A)

        ysT, ys2, dT, nbf, nbi = sm(32), sm(32), sm(32), sm(1), sm(1)
        w2 = ar(128)
        t_ys = dve.do(lambda e: e.tensor_scalar(ysT, w("condT"), float(np.float32(1.0) / np.sqrt(np.float32(128))), None, ALU.mult), LC)
        t2 = dve.do(lambda e: e.tensor_tensor(ys2, ysT, ysT, ALU.mult), t_ys)
        t3 = dve.do(lambda e: e.tensor_tensor(w2, w("w0"), w("w0"), ALU.mult), LQ)
        t4 = pe.do(lambda e: e.matmul(PB[6][:, 0:32], w2, ys2, start=True, stop=True), t2, t3)
        t5 = act.do(lambda e: e.activation(dT, PB[6][:, 0:32], ACTF.Sqrt, bias=c_eps8), t4, eps_tok)
        t_d = dve.do(lambda e: e.reciprocal(dT, dT), t5)

        NCH = 16
        xs, uf = ar(256), ar(256)
        UH, UL = [rr(256) for _ in range(2)], [rr(256) for _ in range(2)]
        KH = [rr(1024).rearrange("p (h b j) -> p h b j", h=4, b=2) for _ in range(3)]
        KL = [rr(1024).rearrange("p (h b j) -> p h b j", h=4, b=2) for _ in range(3)]
        VP = [cs(XT, i) for i in range(8)] + [ar(512) for _ in range(2)]
        wvo_raw = w("wvT", 128, 0, 512), w("wvT", 128, 512, 1024), w("wout", 128, 0, 512)
        SS = [W1[:, i * 512:(i + 1) * 512] for i in range(4)] + [wvo_raw[0]]
        PT = list(wvo_raw[1:])
        mx = [sm(4) for _ in range(5)]
        rc = [sm(4) for _ in range(5)]
        FG, IG, SM = GS[:, 0:512], GS[:, 512:1024], GS[:, 1024:1536]
        pj_free = {5: None, 6: t5, 7: None}
        pj_n = [0]

        def pj():
            k = 5 + pj_n[0] % 3
            pj_n[0] += 1
            return PB[k], k

        tok_u, tok_k, tok_v = {}, {}, {}
        last_s, u_readers = {}, {}
        xs_r, uf_r = [None], [None]
        tok_x, xs_tok = {}, {}

        def pair3(bank_ap, lh, ll, rh, rl, toks, inc=True):
            pe.do(lambda e: e.matmul(bank_ap, lh, rh, start=True, stop=False), toks, inc=False)
            pe.do(lambda e: e.matmul(bank_ap, ll, rh, start=False, stop=False), inc=False)
            return pe.do(lambda e: e.matmul(bank_ap, lh, rl, start=False, stop=True), inc=inc)

        def scaled(c):
            x3 = XF[:, c * 256:(c + 1) * 256].rearrange("p (b t) -> p b t", b=2)
            ta = pool.do(lambda e: e.tensor_tensor(xs.rearrange("p (b t) -> p b t", b=2), x3,
                                                   ysT[:, 2 * c:2 * c + 2].unsqueeze(2).broadcast_to([128, 2, 128]), ALU.mult),
                         LX[c // 4], t_ys, xs_r[0])
            xs_tok[c] = ta

        def proj_u(c):
            i = c % 2
            ta = xs_tok[c]
            bank, k = pj()
            xs_r[0] = tb = pe.do(lambda e: e.matmul(bank[:, 0:256], w("w0"), xs, start=True, stop=True), ta, pj_free[k], LQ)
            pj_free[k] = tu = dve.do(lambda e: e.tensor_tensor(uf.rearrange("p (b t) -> p b t", b=2),
                                                               bank[:, 0:256].rearrange("p (b t) -> p b t", b=2),
                                                               dT[:, 2 * c:2 * c + 2].unsqueeze(2).broadcast_to([128, 2, 128]), ALU.mult),
                                     tb, t_d, uf_r[0])
            th = act.do(lambda e: e.activation(UH[i], uf, ACTF.Copy), tu, u_readers.get(c - 2))
            uf_r[0] = tl = dve.do(lambda e: e.tensor_tensor(UL[i], uf, UH[i], ALU.subtract), th, u_readers.get(c - 2))
            tok_u[c] = [th, tl]

        def proj_v(u):
            c, g, b = units[u]
            i = c % 2
            bank, k = pj()
            sl, bl = slice(g * 512, (g + 1) * 512), slice(b * 128, (b + 1) * 128)
            u_readers[c] = tp = pair3(bank[:, :], UH[i][:, bl], UL[i][:, bl], BH[:, sl], BL[:, sl], [tok_u[c], t_B, pj_free[k]])
            pj_free[k] = tok_v[u] = act.do(lambda e: e.activation(VP[u % 10], bank[:, :], ACTF.Copy), tp, k_pv.get(u - 10))

        def proj_k(G, half):
            c, g = G // 4, G % 4
            i, ks = c % 2, G % 3
            bank, k = pj()
            for h in range(2):
                o = (4 * g + 2 * half + h) * 128
                tp = pair3(bank[:, h * 256:(h + 1) * 256], AH[:, o:o + 128], AL_[:, o:o + 128], UH[i], UL[i],
                           [tok_u[c], t_A, pj_free[k]], inc=h == 1)
            u_readers[c] = tp
            hs = slice(2 * half, 2 * half + 2)
            b4 = bank[:, :].rearrange("p (h b j) -> p h b j", h=2, b=2)
            th = act.do(lambda e: e.activation(KH[ks][:, hs, :, :], b4, ACTF.Copy), tp, last_s.get(G - 3))
            pj_free[k] = tl = dve.do(lambda e: e.tensor_tensor(KL[ks][:, hs, :, :], b4, KH[ks][:, hs, :, :], ALU.subtract), th, last_s.get(G - 3))
            tok_k[(G, half)] = [th, tl]

        units = [(c, g, b) for c in range(NCH) for g in range(4) for b in range(2)]
        U = len(units)
        k_max, k_exp, k_T, k_cp, k_pv, k_nrm, y_free = ({} for _ in range(7))

        def a_S(u):
            c, g, b = units[u]
            G, i = 4 * c + g, c % 2
            bank, r = PB[u % 2], u % 5
            bl = slice(b * 128, (b + 1) * 128)
            b3 = bank[:, :].rearrange("p (h j) -> p h j", h=4)
            t = pair3(b3, UH[i][:, bl], UL[i][:, bl], KH[G % 3][:, :, b, :], KL[G % 3][:, :, b, :],
                      [tok_u[c], tok_k[(G, 0)], tok_k[(G, 1)], k_max.get(u - 2)])
            last_s[G] = u_readers[c] = t
            tx = []
            for h in range(4):
                hl = slice(h * 128, (h + 1) * 128)
                k_max[(u, h)] = k_max[u] = dve.do(lambda e: e.tensor_tensor_reduce(SS[r][:, hl], bank[:, hl], w("mask"), 1.0, 3.0e38, ALU.add, ALU.min,
                                                                        mx[r][:, h:h + 1]), t, k_T.get(u - 5), LC, t_A, t_B)

        def a_E(u):
            r = u % 5
            for h in range(4):
                hl = slice(h * 128, (h + 1) * 128)
                k_exp[u] = act.do(lambda e: e.activation(SS[r][:, hl], SS[r][:, hl], ACTF.Exp, bias=mx[r][:, h:h + 1], scale=-1.0,
                                                         accum_out=rc[r][:, h:h + 1]), k_max[(u, h)], k_nrm.get(u - 5))

        def a_N(u):
            r = u % 5
            s3 = SS[r].rearrange("p (h j) -> p h j", h=4)
            t = dve.do(lambda e: e.reciprocal(rc[r], rc[r]), k_exp[u])
            k_nrm[u] = pool.do(lambda e: e.tensor_tensor(s3, s3, rc[r].unsqueeze(2).broadcast_to([128, 4, 128]), ALU.mult), t)

        def a_T(u):
            bank, r = PB[4], u % 5
            for h in range(4):
                t = pe.do(lambda e: e.transpose(bank[:, h * 128:(h + 1) * 128], SS[r][:, h * 128:(h + 1) * 128], ident),
                          k_nrm[u], k_cp.get(u - 1), LC, inc=h == 3)
            k_T[u] = t
            k_cp[u] = act.do(lambda e: e.activation(PT[u % 2], bank[:, :], ACTF.Copy), t, k_pv.get(u - 2))

        def a_PV(u):
            c, g, b = units[u]
            for h in range(4):
                hl = slice(h * 128, (h + 1) * 128)
                t = pe.do(lambda e: e.matmul(PB[2 + b][:, 0:128], VP[u % 10][:, hl], PT[u % 2][:, hl], start=(g, h) == (0, 0), stop=(g, h) == (3, 3)),
                          k_cp[u], tok_v[u], y_free.get((c - 1, b)), inc=h == 3)
            k_pv[u] = t
            if g == 3:
                q = slice((2 * c + b) * 128, (2 * c + b + 1) * 128)
                y_free[(c, b)] = dve.do(lambda e: e.tensor_tensor(XF[:, q], PB[2 + b][:, 0:128], XF[:, q], ALU.add), t, xs_tok[c])
                tok_x[c] = [y_free.get((c, 0)), y_free.get((c, 1))]

        s2r = [None]
        gctx, t_gc = sm(32), []

        def gated(c):
            def project(wn):
                bank, k = pj()
                return bank, k, pe.do(lambda e: e.matmul(bank[:, :], w(wn), cs(XF, c), start=True, stop=True),
                                      tok_x[2 * c], tok_x[2 * c + 1], LW, pj_free[k])

            bank, k, tp = project("wfT")
            pj_free[k] = t = act.do(lambda e: e.activation(FG, bank[:, :], ACTF.Exp, bias=nbf, scale=-1.0), tp, t_nb, s2r[0])
            yield
            bank, k, tp = project("wiT")
            pj_free[k] = ti = act.do(lambda e: e.activation(IG, bank[:, :], ACTF.Exp, bias=nbi, scale=-1.0), tp, t_nb, s2r[0])
            yield
            bank, k, tp = project("whT")
            pj_free[k] = tc = dve.do(lambda e: e.tensor_scalar(cs(HF, c), bank[:, :], w("bh"), None, ALU.add), tp)
            yield
            tA = dve.do(lambda e: e.tensor_scalar(FG, FG, 1e22, 1.0, ALU.min, ALU.add), t)
            tB = dve.do(lambda e: e.tensor_scalar(IG, IG, 1e22, 1.0, ALU.min, ALU.add), ti)
            t = dve.do(lambda e: e.scalar_tensor_tensor(SM, FG, 1e-8, IG, ALU.mult, ALU.mult), tA, tB, s2r[0])
            yield
            t = pool.do(lambda e: e.tensor_tensor(SM, SM, FG, ALU.add), t)
            t = pool.do(lambda e: e.tensor_tensor(SM, SM, IG, ALU.add), t)
            yield
            tr = []
            for b in range(4):
                bl = slice(b * 128, (b + 1) * 128)
                tr.append(dve.do(lambda e: e.reciprocal(SM[:, bl], SM[:, bl]), t))
                yield
            tf = pool.do(lambda e: e.tensor_tensor(IG, IG, SM, ALU.mult), tr)
            ti = pool.do(lambda e: e.tensor_tensor(FG, FG, SM, ALU.mult), tr)
            yield
            tn = pool.do(lambda e: e.tensor_tensor(SM, cs(HF, c), FG, ALU.mult), tc, ti, tf)
            tf = dve.do(lambda e: e.tensor_scalar(IG, IG, 1e-8, None, ALU.add), tf)
            yield
            te, td = [], []
            for b in range(4):
                q = slice(c * 512 + b * 128, c * 512 + (b + 1) * 128)
                bl = slice(b * 128, (b + 1) * 128)
                td.append(dve.do(lambda e: e.tensor_tensor_scan(FG[:, bl][:, ::-1], IG[:, bl][:, ::-1], ones, 1.0, ALU.mult, ALU.mult), tf, tn, t_ones))
            tn = pool.do(lambda e: e.tensor_tensor(SM, SM, FG, ALU.mult), td, tn)
            yield
            for b in range(4):
                q = slice(c * 512 + b * 128, c * 512 + (b + 1) * 128)
                bl = slice(b * 128, (b + 1) * 128)
                te.append(dve.do(lambda e: e.tensor_tensor_scan(HF[:, q], IG[:, bl], ones, 1.0, ALU.mult, ALU.mult), tf, tn))
            yield
            for b in range(4):
                bl = slice(b * 128, (b + 1) * 128)
                t = dve.do(lambda e: e.tensor_tensor_scan(FG[:, bl], ones, SM[:, bl], 0.0, ALU.mult, ALU.add), tn)
            yield
            for b in range(4):
                q = slice(c * 512 + b * 128, c * 512 + (b + 1) * 128)
                bl = slice(b * 128, (b + 1) * 128)
                s2r[0] = dve.do(lambda e: e.scalar_tensor_tensor(HF[:, q], HF[:, q], w("condT", 128, 4 * c + b, 4 * c + b + 1), FG[:, bl],
                                                                 ALU.mult, ALU.add), t, te)
            t_gc.append(dve.do(lambda e: e.tensor_reduce(gctx[:, 4 * c:4 * c + 4], v4(cs(HF, c)), AX.X, ALU.add), s2r[0]))
            yield

        scaled(0)
        proj_u(0)
        scaled(1)
        for n in range(3):
            proj_k(n // 2, n % 2)
        products("wvT", "wout", 1.0, BH, BL, LV, t_B)
        k_max[-2], k_max[-1] = pb_w[0:2], pb_w[0:2]
        y_free[(-1, 0)], y_free[(-1, 1)] = pb_w[2], pb_w[3]
        for u in range(4):
            proj_v(u)
        t = dve.do(lambda e: e.tensor_scalar(nbf, w("bf"), -1.0, None, ALU.mult), LW)
        t_nb = dve.do(lambda e: e.tensor_scalar(nbi, w("bi"), -1.0, None, ALU.mult), LW)
        rec = iter(())
        for s in range(U + 4):
            c, j = s // 8, s % 8
            if s < U:
                a_S(s)
            if 0 <= s - 1 < U:
                a_N(s - 1)
            if 0 <= s - 3 < U:
                a_T(s - 3)
            if s + 3 < U:
                proj_k((s + 3) // 2, (s + 3) % 2)
            if s < U:
                a_E(s)
            if j == 0 and c + 1 < NCH:
                proj_u(c + 1)
            if j == 5 and c + 2 < NCH:
                scaled(c + 2)
            if s + 4 < U:
                proj_v(s + 4)
            if 0 <= s - 4 < U:
                a_PV(s - 4)
            if j == 4 and s >= 20 and (c - 1) % 2 == 1:
                for _ in rec:
                    pass
                rec = gated((c - 1) // 2)
            if s < U + 3:
                next(rec, None)
        for _ in rec:
            pass
        rec = gated(7)

        barrier("s3", 8192, 18432)
        EH1, EL1, EH2, EL2 = rr(2048), rr(2048), rr(2048), rr(2048)
        SH1, SL1, SH2, SL2 = rr(512), rr(512), rr(512), rr(512)
        XH, XL = [rr(512) for _ in range(3)], [rr(512) for _ in range(3)]
        HH = [rr(512) for _ in range(5)]
        HL = [rr(512) for _ in range(5)]
        g1, g2, cB, ar07, ar03, b4h, b4h2, gfT, sil = sm(32), sm(32), sm(32), sm(1), sm(1), sm(1), sm(1), sm(32), sm(32)
        th = dve.do(lambda e: e.tensor_scalar(b4h, w("gb3"), 0.5, None, ALU.mult))
        th2 = dve.do(lambda e: e.tensor_scalar(b4h2, w("cb4"), 0.5, None, ALU.mult))
        t7 = dve.do(lambda e: e.tensor_scalar(ar07, w("ar"), 0.7, None, ALU.mult))
        t3_ = dve.do(lambda e: e.tensor_scalar(ar03, w("ar"), 0.3, None, ALU.mult))
        H1 = [ar(1024) for _ in range(4)]
        H2 = [ar(512) for _ in range(4)]
        H3 = [ar(512) for _ in range(4)]
        hs, ws, psm, agg = sm(32), sm(32), sm(32), sm(96)
        fr = [pj_free.get(k) for k in range(8)]
        bk = [0]

        def nb():
            k = bk[0] % 8
            bk[0] += 1
            return k

        left, fin, t_agg = [12], {}, []
        t_cB, tx2, t_w4 = {}, {}, []

        def context(a, b):
            n = b - a
            k = nb()
            t = pe.do(lambda e: e.matmul(PB[k][0:64, 0:n], w("gw1"), gctx[:, a:b], start=True, stop=True), t_gc, fr[k])
            fr[k] = t = act.do(lambda e: e.activation(g1[0:64, a:b], PB[k][0:64, 0:n], ACTF.Gelu, bias=w("gb1", 64), scale=1.0 / 128), t)
            yield
            k = nb()
            t = pe.do(lambda e: e.matmul(PB[k][0:32, 0:n], w("gw2", 64), g1[0:64, a:b], start=True, stop=True), t, fr[k])
            fr[k] = t = act.do(lambda e: e.activation(g2[0:32, a:b], PB[k][0:32, 0:n], ACTF.Gelu, bias=w("gb2", 32)), t)
            yield
            k = nb()
            t = pe.do(lambda e: e.matmul(PB[k][:, 0:n], w("gw3", 32), g2[0:32, a:b], start=True, stop=True), t, fr[k])
            fr[k] = t = act.do(lambda e: e.activation(gfT[:, a:b], PB[k][:, 0:n], ACTF.Tanh, bias=b4h, scale=0.5), t, th)
            t = dve.do(lambda e: e.tensor_scalar(cB[:, a:b], gfT[:, a:b], ar07, 0.1, ALU.mult, ALU.add), t, t7)
            for p in range(a // 8, b // 8):
                t_cB[p] = t
            if a == 0:
                t = act.do(lambda e: e.activation(sil, w("condT"), ACTF.Tanh, scale=0.5))
                t = dve.do(lambda e: e.tensor_scalar(sil, sil, 0.5, 0.5, ALU.mult, ALU.add), t)
                t_w4.append(dve.do(lambda e: e.tensor_tensor(sil, sil, w("condT"), ALU.mult), t))
            yield

        def split(hi, lo, src):
            t = act.do(lambda e: e.activation(hi, src, ACTF.Copy))
            return [t, pool.do(lambda e: e.tensor_tensor(lo, src, hi, ALU.subtract), t)]

        def couple(p):
            S, Tw = cs(HF, p, 1024), cs(XT, p, 1024)
            upS, upT, r1 = [None, None], [None, None], None
            for y in range(3):
                tg = []
                for s in range(2):
                    k = nb()
                    tp = pe.do(lambda e: e.matmul(PB[k][:, :], w("cw1"), cs(S, s), start=True, stop=True), upS[s], fr[k])
                    fr[k] = t = act.do(lambda e: e.activation(cs(H1[p], s), PB[k][:, :], ACTF.Gelu, bias=w("cb1")), tp, upS[s])
                    tg.append(t)
                    if y == 0:
                        k = nb()
                        tp = pe.do(lambda e: e.matmul(PB[k][:, :], w("twist"), cs(S, s), start=True, stop=True), fr[k])
                        fr[k] = upT[s] = act.do(lambda e: e.activation(cs(Tw, s), PB[k][:, :], ACTF.Copy), tp)
                yield
                k = nb()
                for s in range(2):
                    tp = pe.do(lambda e: e.matmul(PB[k][64 * s:64 * s + 64, :], w("cw2"), cs(H1[p], s), start=True, stop=True), tg[s], fr[k], inc=s == 1)
                fr[k] = t = act.do(lambda e: e.activation(H2[p], PB[k][:, :], ACTF.Gelu, bias=w("cb2")), tp, upS)
                yield
                k = nb()
                tp = pe.do(lambda e: e.matmul(PB[k][0:64, :], w("cw3"), H2[p], start=True, stop=True), t, fr[k])
                fr[k] = t3 = act.do(lambda e: e.activation(H3[p][0:64, :], PB[k][0:64, :], ACTF.Gelu, bias=w("cb3", 64)), tp, upS)
                yield
                tt = []
                for s in range(2):
                    k = nb()
                    t4 = pe.do(lambda e: e.matmul(PB[k][:, :], w("cw4", 64, 128 * s, 128 * s + 128), H3[p][0:64, :], start=True, stop=True), t3, fr[k])
                    fr[k] = t = act.do(lambda e: e.activation(cs(H1[p], s), PB[k][:, :], ACTF.Tanh, bias=b4h2, scale=0.5), t4, th2)
                    tt.append(t)
                left[0] -= 1
                yield
                while p not in t_cB:
                    yield
                tu = []
                for s in range(2):
                    c = 2 * p + s
                    cp = cs(H1[p], s)
                    u = (H2, H3)[s][p]
                    t = dve.do(lambda e: e.scalar_tensor_tensor(
                        v4(cp), v4(cp), ar03, cB[:, 4 * c:4 * c + 4].unsqueeze(2).broadcast_to([128, 4, 128]), ALU.mult, ALU.add),
                        tt[s], t_cB[p], t3_)
                    t = dve.do(lambda e: e.tensor_tensor(u, cp, cs(Tw, s), ALU.mult), t, upT[s], t4)
                    if y < 2:
                        tw = dve.do(lambda e: e.tensor_tensor(cp, cp, cs(S, s), ALU.mult), t, upS[s])
                        upT[s] = pool.do(lambda e: e.tensor_tensor(cs(Tw, s), cs(Tw, s), cp, ALU.subtract), tw)
                        upS[s] = [upT[s], dve.do(lambda e: e.tensor_tensor(cs(S, s), cs(S, s), u, ALU.add), t, tw)]
                    else:
                        upS[s] = tx2[c] = dve.do(lambda e: e.tensor_tensor(cs(XF, c), cs(XF, c), u, ALU.add), t, tx[s])
                yield
                if y == 1:
                    tx = [pool.do(lambda e: e.tensor_tensor(cs(XF, 2 * p + s), cs(XF, 2 * p + s), cs(S, s), ALU.add), upS[s]) for s in range(2)]
            fin[p] = upS
            for s in range(2):
                c = 2 * p + s
                xb = v4(cs(XF, c))
                for dst, a, b in ((hs, 0, 42), (ws, 42, 84), (psm, 84, 128)):
                    t_ag = dve.do(lambda e: e.tensor_reduce(dst[:, 4 * c:4 * c + 4], xb[:, :, a:b], AX.X, ALU.add), tx2[c])
                t_agg.append(t_ag)
                yield

        splits = [(EH1, EL1, w("ew1"), k) for k in range(4)] + [(EH2, EL2, w("ew2"), k) for k in range(4)] + \
                 [(SH1, SL1, w("sw1"), 0), (SH2, SL2, w("sw2"), 0)]
        t_ws = []
        for _ in range(3):
            next(rec)
        for k in range(5, 8):
            fr[k] = pj_free[k]
        G4 = [cs(H1[p], s) for p in range(2) for s in range(2)]
        YT = [cs(H1[2], s) for s in range(2)]
        sc, tmod, lg, wbc, dg = sm(4), sm(8), sm(4), sm(128), sm(128)
        R = 32
        t_w = [None]

        def gates():
            ta = dve.do(lambda e: e.tensor_tensor(agg[:, 32:64], hs, psm, ALU.add), t_agg)
            tb2 = dve.do(lambda e: e.tensor_tensor(agg[:, 64:96], ws, psm, ALU.add), t_agg)
            tcx = dve.do(lambda e: e.tensor_tensor(agg[:, 0:32], agg[:, 32:64], ws, ALU.add), ta)
            t = dve.do(lambda e: e.tensor_scalar(agg[:, 0:32], agg[:, 0:32], 1.0 / 128, None, ALU.mult), tcx)
            t = dve.do(lambda e: e.tensor_scalar(agg[:, 32:96], agg[:, 32:96], 1.0 / 86, None, ALU.mult), t, tb2)
            yield
            p = 6
            for j in range(3):
                tg = pe.do(lambda e: e.matmul(PB[p][0:32, 0:4], agg[:, 32 * j:32 * j + 32], w("gatew", 128, 4 * j, 4 * j + 4),
                                              start=j == 0, stop=j == 2), t, pbf[p], inc=j == 2)
            p = 7
            tm = pe.do(lambda e: e.matmul(PB[p][0:32, 0:8], sil, w("timew"), start=True, stop=True), pbf[p], t_w4)
            pbf[7] = t = dve.do(lambda e: e.tensor_tensor(tmod[0:R, :], PB[7][0:R, 0:8], w("timeb", R), ALU.add), tm)
            t1 = dve.do(lambda e: e.tensor_scalar(tmod[0:R, 0:4], tmod[0:R, 0:4], 1.0, None, ALU.add), t)
            pbf[6] = t = dve.do(lambda e: e.tensor_tensor(lg[0:R, :], PB[6][0:R, 0:4], w("gateb", R), ALU.add), tg)
            t = dve.do(lambda e: e.tensor_tensor(lg[0:R, :], lg[0:R, :], tmod[0:R, 0:4], ALU.mult), t, t1)
            t = dve.do(lambda e: e.tensor_tensor(lg[0:R, :], lg[0:R, :], tmod[0:R, 4:8], ALU.add), t)
            yield
            s1 = sm(1)
            t = dve.do(lambda e: e.tensor_reduce(s1[0:R, :], lg[0:R, :], AX.X, ALU.max), t)
            t = dve.do(lambda e: e.tensor_scalar(lg[0:R, :], lg[0:R, :], s1[0:R, :], None, ALU.subtract), t)
            yield
            t = act.do(lambda e: e.activation(sc[0:R, :], lg[0:R, :], ACTF.Exp), t)
            t = dve.do(lambda e: e.tensor_reduce(s1[0:R, :], sc[0:R, :], AX.X, ALU.add), t)
            t = dve.do(lambda e: e.reciprocal(s1[0:R, :], s1[0:R, :]), t)
            t = dve.do(lambda e: e.tensor_scalar(sc[0:R, :], sc[0:R, :], s1[0:R, :], None, ALU.mult), t)
            yield
            cmp1, cmp2, rank = sm(16), sm(16), sm(4)
            sA = sc[0:R, :].unsqueeze(1).broadcast_to([R, 4, 4])
            sB = sc[0:R, :].unsqueeze(2).broadcast_to([R, 4, 4])
            c1 = cmp1[0:R, :].rearrange("p (a b) -> p a b", a=4)
            c2 = cmp2[0:R, :].rearrange("p (a b) -> p a b", a=4)
            ta = dve.do(lambda e: e.tensor_tensor(c1, sA, sB, ALU.is_gt), t)
            tb = dve.do(lambda e: e.tensor_tensor(c2, sA, sB, ALU.is_equal), t)
            tb = dve.do(lambda e: e.tensor_tensor(cmp2[0:R, :], cmp2[0:R, :], w("lower", R), ALU.mult), tb)
            t = dve.do(lambda e: e.tensor_tensor(cmp1[0:R, :], cmp1[0:R, :], cmp2[0:R, :], ALU.add), ta, tb)
            t = dve.do(lambda e: e.tensor_reduce(rank[0:R, :], c1, AX.X, ALU.add), t)
            t = dve.do(lambda e: e.tensor_scalar(rank[0:R, :], rank[0:R, :], 1.5, None, ALU.is_lt), t)
            yield
            t = dve.do(lambda e: e.tensor_tensor(sc[0:R, :], sc[0:R, :], rank[0:R, :], ALU.mult), t)
            t = dve.do(lambda e: e.tensor_reduce(s1[0:R, :], sc[0:R, :], AX.X, ALU.add), t)
            t = dve.do(lambda e: e.tensor_scalar(s1[0:R, :], s1[0:R, :], 1e-8, None, ALU.add), t)
            t = dve.do(lambda e: e.reciprocal(s1[0:R, :], s1[0:R, :]), t)
            t = dve.do(lambda e: e.tensor_scalar(sc[0:R, :], sc[0:R, :], s1[0:R, :], None, ALU.mult), t)
            t = dve.do(lambda e: e.tensor_tensor(dg[0:R, :].rearrange("p (a b) -> p a b", a=4),
                                                 ident[0:R, 0:32].unsqueeze(1).broadcast_to([R, 4, 32]),
                                                 sc[0:R, :].unsqueeze(2).broadcast_to([R, 4, 32]), ALU.mult), t)
            yield
            p = 6
            t = pe.do(lambda e: e.matmul(PB[p][:, 0:128], ones[0:R, :], dg[0:R, :], start=True, stop=True), t, pbf[p])
            pbf[p] = t_w[0] = dve.do(lambda e: e.tensor_copy(wbc, PB[p][:, 0:128]), t)
            yield

        def tokens(ap, x):
            if x == 1:
                return bass.AP(tensor=ap.tensor, offset=ap.offset, ap=[list(ap.ap[0]), [128, 4], [84, 2], [1, 44]])
            return v4(ap)[:, :, 42:128] if x == 2 else ap

        LEN = {0: 512, 1: 352, 2: 344, 3: 512, 4: 512}
        tok_x, x_r = {}, {}
        r_hb, r_g, r_yt = [None] * 5, [None] * 4, [None] * 2
        pbf = fr
        acc = {}
        gn, dn = [0], [0]

        def part(c):
            i = c % 3
            t = act.do(lambda e: e.activation(XH[i], cs(XF, c), ACTF.Copy), tx2[c], x_r.get(c - 3))
            tok_x[c] = [t, dve.do(lambda e: e.tensor_tensor(XL[i], cs(XF, c), XH[i], ALU.subtract), t, x_r.get(c - 3))]

        def up(c, x, k):
            n = LEN[x]
            o = x * 512 + k * 128 if x < 4 else k * 128
            wh, wl = (EH1, EL1) if x < 4 else (SH1, SL1)
            b1 = w("eb1", 128, x * 4 + k, x * 4 + k + 1) if x < 4 else w("sb1", 128, k, k + 1)
            bank = PB[k][:, 0:n]
            x_r[c] = tp = pair3(bank, wh[:, o:o + 128], wl[:, o:o + 128], tokens(XH[c % 3], x), tokens(XL[c % 3], x),
                                [tok_x[c], t_ws, pbf[k]])
            g, i = gn[0] % 4, gn[0] % 5
            gn[0] += 1
            pbf[k] = t = act.do(lambda e: e.activation(G4[g][:, 0:n], bank, ACTF.Gelu_apprx_tanh, bias=b1), tp, r_g[g])
            th_ = dve.do(lambda e: e.tensor_copy(HH[i][:, 0:n], G4[g][:, 0:n]), t, r_hb[i])
            r_g[g] = tl = (pool if k == 2 else dve).do(
                lambda e: e.tensor_tensor(HL[i][:, 0:n], G4[g][:, 0:n], HH[i][:, 0:n], ALU.subtract), th_, r_hb[i])
            return i, [th_, tl]

        def down(c, x, k, i, toks):
            n = LEN[x]
            o = x * 512 + k * 128 if x < 4 else k * 128
            wh, wl = (EH2[:, o:o + 128], EL2[:, o:o + 128]) if x < 4 else (SH2[:, o:o + 128], SL2[:, o:o + 128])
            if k == 0:
                dn[0] += 1
            j = dn[0] % 2
            p = 4 + j
            bank = PB[p][:, 0:n]
            pe.do(lambda e: e.matmul(bank, wh, HH[i][:, 0:n], start=k == 0, stop=False), toks, t_ws, pbf[p], inc=False)
            pe.do(lambda e: e.matmul(bank, wl, HH[i][:, 0:n], start=False, stop=False), inc=False)
            r_hb[i] = tp = pe.do(lambda e: e.matmul(bank, wh, HL[i][:, 0:n], start=False, stop=k == 3))
            if k < 3:
                return
            if x == 4:
                pbf[p] = acc[c] = dve.do(lambda e: e.tensor_scalar(cs(HF, c), bank, w("sb2"), None, ALU.add), tp)
                return
            L = n // 4
            b3 = bank.rearrange("p (b t) -> p b t", b=4)
            y3 = YT[j][:, 0:n].rearrange("p (b t) -> p b t", b=4)
            h3 = v4(cs(HF, c))
            pbf[p] = ty = dve.do(lambda e: e.scalar_tensor_tensor(
                y3, b3, w("eb2", 128, x, x + 1), wbc[:, x * 32 + 4 * c:x * 32 + 4 * c + 4].unsqueeze(2).broadcast_to([128, 4, L]),
                ALU.add, ALU.mult), tp, t_w[0], r_yt[j])
            for a, b, o in {1: ((0, 42, 0), (84, 128, 44)), 2: ((42, 128, 0),)}.get(x, ((0, 128, 0),)):
                t = pool.do(lambda e: e.tensor_tensor(h3[:, :, a:b], h3[:, :, a:b], y3[:, :, o:o + b - a], ALU.add), ty, acc[c])
            r_yt[j] = acc[c] = t

        jobs = [(0, 4), (1, 4), (2, 4)] + [(c, x) for c in range(2) for x in range(4)] + [(c, x) for c in range(2, CH) for x in ((4, 0, 1, 2, 3) if c > 2 else range(4))]
        def experts():
            r_hb[:] = [s2r[0]] * 5
            r_g[:] = [fin[0], fin[0], fin[1], fin[1]]
            r_yt[:] = [fin[2], fin[2]]
            prev, gt = None, gates()
            part(0)
            yield
            part(1)
            for n, (c, x) in enumerate(jobs + [(0, 0)]):
                if c >= 2 and x == 4:
                    part(c)
                if n == 3:
                    while len(t_agg) < 8:
                        yield
                cur = []
                for k in range(4):
                    if n < len(jobs):
                        cur.append((c, x, k) + up(c, x, k))
                    if prev:
                        down(*prev[k])
                    if len(t_agg) == 8:
                        next(gt, None)
                    yield
                prev = cur

        starts = [[couple(0)], [couple(1), context(0, 24)], [couple(2)], [], [], [context(24, 32), couple(3)]]
        live = []
        moe = None
        while live or starts:
            if left[0] == 0 and moe is None:
                for e in engines:
                    e.stage("s4")
                moe = experts()
                live.append(moe)
            if starts:
                if len(starts) == 3:
                    for _ in rec:
                        pass
                live += starts.pop(0)
            for gnr in list(live):
                if next(gnr, "over") == "over":
                    live.remove(gnr)
            for _ in range(3 if left[0] < 4 else 1):
                if splits and len(starts) < 2:
                    hi, lo, src, k = splits.pop()
                    t_ws.append(split(cs(hi, k), cs(lo, k), cs(src, k)))

        barrier("s5", 11600, 12288)
        QT, KT, KMB = ar(512), ar(512), ar(512)
        X2 = [ar(512) for _ in range(2)]
        VT = [ar(128) for _ in range(2)]
        VY = [ar(272) for _ in range(3)]
        SS = [ar(512) for _ in range(4)]
        PT = [ar(512) for _ in range(2)]
        LN = [ar(512) for _ in range(2)]
        GG = [ar(512) for _ in range(2)]
        XA = ar(256).rearrange("p (b r) -> p b r", r=8)
        XBP = [ar(128) for _ in range(2)]
        HX = ar(2048)
        ae, aeT, hT = ar(128), ar(32), ar(32)
        QH, QL, KH, KL = rr(512), rr(512), rr(512), rr(512)
        QS = [rr(2048) for _ in range(2)]
        KR = [rr(2048) for _ in range(2)]
        KS = [rr(512).rearrange("p (h j) -> p h j", h=4) for _ in range(4)]
        ov = [pool.do(lambda e, i=i: e.memset(VY[i], 0.0)) for i in range(3)]
        mx = [sm(4) for _ in range(4)]
        rc = [sm(16) for _ in range(2)]
        xsum, qm, iqm, rstd = sm(32), sm(32), sm(32), sm(32)
        mv, mhalf = sm(64), sm(4)
        t_half = pool.do(lambda e: e.memset(mhalf, -0.5))
        m3 = mv.rearrange("p (q s) -> p q s", s=2)
        bns = [sm(6) for _ in range(2)]
        s_q = [new_sem(f"s_q{i}") for i in range(2)]
        s_k = [new_sem(f"s_k{i}") for i in range(2)]
        sp = Queue(nc.sync, new_sem, "sp")
        pj_free = {5: None, 6: None, 7: None}
        pj_n[0] = 0
        nisq8 = float(-1.0 / np.sqrt(8))
        tok_q, tok_k, tok_v, tok_m, tok_x2 = {}, {}, {}, {}, {}
        last_s, last_pv, last_ks, x2_r, v_r = {}, {}, {}, {}, {}
        r_parts = {"q": None, "k": None, "QT": None, "KT": None, "KMB": None}

        def spread(hi, lo, order, dst, s, toks, c):
            sp.wait([toks])
            for g in range(4):
                for rep in range(3):
                    src = (hi, lo)[order[rep]]
                    nc.sync.dma_start(dst[32 * rep:32 * rep + 32, g * 512:(g + 1) * 512].bitcast(F32), src[32 * g:32 * g + 32, :].bitcast(F32)).then_inc(s, 16)
            return (s, 16 * 12 * (c // 2 + 1))

        def proj5(c):
            i = c % 2
            bank, k = pj()
            tp = pe.do(lambda e: e.matmul(bank[:, :], w("aq"), cs(HF, c), start=True, stop=True), pj_free[k])
            pj_free[k] = t = act.do(lambda e: e.activation(QT, bank[:, :], ACTF.Relu, bias=w("bq")), tp, r_parts["QT"])
            yield
            th = dve.do(lambda e: e.tensor_scalar(QH, QT, nisq8, None, ALU.mult), t, r_parts["q"])
            r_parts["QT"] = tl = dve.do(lambda e: e.scalar_tensor_tensor(QL, QT, nisq8, QH, ALU.mult, ALU.subtract), th, r_parts["q"])
            r_parts["q"] = tok_q[c] = spread(QH, QL, (0, 0, 1), QS[i], s_q[i], [th, tl, last_s.get(c - 2)], c)
            yield
            bank, k = pj()
            tp = pe.do(lambda e: e.matmul(bank[:, :], ones, cs(HF, c), start=True, stop=True), pj_free[k])
            pj_free[k] = tm = dve.do(lambda e: e.tensor_scalar(KMB, bank[:, :], 0.0, None, ALU.not_equal), tp, r_parts["KMB"])
            bank, k = pj()
            tp = pe.do(lambda e: e.matmul(bank[:, :], w("ak"), cs(HF, c), start=True, stop=True), pj_free[k])
            pj_free[k] = t = act.do(lambda e: e.activation(KT, bank[:, :], ACTF.Relu, bias=w("bk")), tp, r_parts["KT"])
            yield
            r_parts["KMB"] = t = dve.do(lambda e: e.tensor_tensor(KT, KT, KMB, ALU.mult), t, tm)
            th = dve.do(lambda e: e.tensor_copy(KH, KT), t, r_parts["k"])
            yield
            r_parts["KT"] = tl = dve.do(lambda e: e.tensor_tensor(KL, KT, KH, ALU.subtract), th, r_parts["k"])
            r_parts["k"] = tok_k[c] = spread(KH, KL, (0, 1, 0), KR[i], s_k[i], [th, tl, last_ks.get(c - 2)], c)
            yield
            bank, k = pj()
            for b in range(4):
                tp = pe.do(lambda e: e.transpose(bank[:, b * 128:(b + 1) * 128], HF[:, c * 512 + b * 128:c * 512 + (b + 1) * 128], ident),
                           pj_free[k], inc=b == 3)
            pj_free[k] = tok_x2[c] = act.do(lambda e: e.activation(X2[i], bank[:, :], ACTF.Copy), tp, x2_r.get(c - 2))
            yield
            t = dve.do(lambda e: e.tensor_reduce(xsum[:, 4 * c:4 * c + 4], v4(X2[i]), AX.X, ALU.add), tok_x2[c])
            ta = dve.do(lambda e: e.tensor_scalar(qm[:, 4 * c:4 * c + 4], xsum[:, 4 * c:4 * c + 4], 0.0, None, ALU.not_equal), t)
            tok_m[c] = dve.do(lambda e: e.tensor_scalar(iqm[:, 4 * c:4 * c + 4], qm[:, 4 * c:4 * c + 4], -1.0, 1.0, ALU.mult, ALU.add), ta)
            yield

        def projv(q):
            c = q // 4
            bank, k = pj()
            v_r[c] = tp = pe.do(lambda e: e.matmul(bank[:, 0:128], HF[:, q * 128:(q + 1) * 128], w("av"), start=True, stop=True), pj_free[k])
            pj_free[k] = t = dve.do(lambda e: e.tensor_tensor(VT[q % 2], bank[:, 0:128], w("bv"), ALU.add), tp, tok_v.get(q - 2))
            vv = VY[q % 3][:, 0:144].rearrange("p (h v) -> p h v", v=9)
            ta = dve.do(lambda e: e.tensor_scalar(vv[:, :, 0:8], VT[q % 2].rearrange("p (h v) -> p h v", v=8), 0.0,
                                                  qm[:, q:q + 1], ALU.max, ALU.mult), t, tok_m[c], ov[q % 3], last_pv.get(q - 3))
            tok_v[q] = [ta, dve.do(lambda e: e.tensor_copy(vv[:, :, 8:9], qm[:, q:q + 1].unsqueeze(1).broadcast_to([128, 16, 1])),
                                   tok_m[c], last_pv.get(q - 3))]

        units = [(q, g) for q in range(32) for g in range(4)]
        U = len(units)
        k_max, k_exp, k_T, k_cp, k_S, k_ks = ({} for _ in range(6))
        bank_free, bn_r, ln_w, ln_free = {}, {}, {}, {}

        def b_K(u):
            q, g = units[u]
            c, b = q // 4, q % 4
            last_ks[c] = k_ks[u] = pool.do(lambda e: e.tensor_tensor(
                KS[u % 4][0:96, :, :], KR[c % 2][0:96, g * 512 + b * 128:g * 512 + (b + 1) * 128].unsqueeze(1).broadcast_to([96, 4, 128]),
                w("hm", 96).unsqueeze(2).broadcast_to([96, 4, 128]), ALU.mult), tok_k[c], k_S.get(u - 4))

        def b_S(u):
            q, g = units[u]
            c, b = q // 4, q % 4
            bank, r = PB[u % 2], u % 4
            last_s[c] = k_S[u] = t = pe.do(lambda e: e.matmul(bank[:, :].rearrange("p (h j) -> p h j", h=4),
                                                              QS[c % 2][0:96, g * 512 + b * 128:g * 512 + (b + 1) * 128], KS[r][0:96, :, :],
                                                              start=True, stop=True), tok_q[c], k_ks[u], k_max.get(u - 2))
            for h in range(4):
                hl = slice(h * 128, (h + 1) * 128)
                k_max[(u, h)] = k_max[u] = dve.do(lambda e: e.tensor_tensor_reduce(SS[r][:, hl], bank[:, hl], w("mask"), 1.0, 3.0e38, ALU.add, ALU.min,
                                                                                   mx[r][:, h:h + 1]), t, k_T.get(u - 4), k_exp.get(u - 4))

        def b_E(u):
            r = u % 4
            for h in range(4):
                hl = slice(h * 128, (h + 1) * 128)
                k_exp[u] = act.do(lambda e: e.activation(SS[r][:, hl], SS[r][:, hl], ACTF.Exp, bias=mx[r][:, h:h + 1], scale=-1.0), k_max[(u, h)])

        k_pv = {}

        def b_T(u):
            bank, r = PB[4], u % 4
            for h in range(4):
                t = pe.do(lambda e: e.transpose(bank[:, h * 128:(h + 1) * 128], SS[r][:, h * 128:(h + 1) * 128], ident),
                          k_exp[u], k_cp.get(u - 1), inc=h == 3)
            k_T[u] = t
            k_cp[u] = act.do(lambda e: e.activation(PT[u % 2], bank[:, :], ACTF.Copy), t, k_pv.get(u - 2))

        def b_PV(u):
            q, g = units[u]
            c, b = q // 4, q % 4
            bank = PB[2 + q % 2]
            for h in range(4):
                o = 9 * (4 * g + h)
                t = pe.do(lambda e: e.matmul(bank[:, o:o + 128], PT[u % 2][:, h * 128:(h + 1) * 128], VY[q % 3][:, o:o + 128], start=True, stop=True),
                          k_cp[u], tok_v[q], ov[q % 3], bank_free.get(q - 2), inc=h == 3)
            k_pv[u] = t
            last_pv[q] = t

        def b_N(q):
            c, b = q // 4, q % 4
            o3 = PB[2 + q % 2][:, 0:144].rearrange("p (h v) -> p h v", h=16)
            r = rc[q % 2]
            sl = cs(LN[c % 2], b, 128)
            t = dve.do(lambda e: e.tensor_scalar(r.unsqueeze(2), o3[:, :, 8:9], iqm[:, q:q + 1], None, ALU.add), last_pv[q], tok_m[c])
            t = dve.do(lambda e: e.reciprocal(r, r), t)
            t = dve.do(lambda e: e.tensor_scalar(r, r, qm[:, q:q + 1], None, ALU.mult), t)
            bank_free[q] = t = dve.do(lambda e: e.tensor_tensor(sl.rearrange("p (h v) -> p h v", h=16), o3[:, :, 0:8],
                                                                r.unsqueeze(2).broadcast_to([128, 16, 8]), ALU.mult), t, ln_free.get(c - 2))
            x2_r[c] = t = dve.do(lambda e: e.tensor_tensor(sl, sl, cs(X2[c % 2], b, 128), ALU.add), t, tok_x2[c])
            t = dve.do(lambda e: e.bn_stats(bns[q % 2], sl), t)
            bn_r[q] = dve.do(lambda e: e.bn_aggr(mv[:, 2 * q:2 * q + 2], bns[q % 2]), t)

        hx4 = HX.rearrange("p (r b s) -> p r b s", r=8, b=32)
        t_xa, t_xb = [], []

        def adapt():
            st6, mv6, r6 = sm(6), sm(2), sm(1)
            tz = pool.do(lambda e: e.memset(HX, 0.0))
            t = dve.do(lambda e: e.bn_stats(st6[0:R, :], w("cond", R)))
            t = dve.do(lambda e: e.bn_aggr(mv6[0:R, :], st6[0:R, :]), t)
            t = pool.do(lambda e: e.tensor_scalar(r6[0:R, :], mv6[0:R, 1:2], 1e-5, None, ALU.add), t)
            t = pool.do(lambda e: e.tensor_tensor(r6[0:R, :], r6[0:R, :], mhalf[0:R, 0:1], ALU.pow), t, t_half)
            t = dve.do(lambda e: e.tensor_scalar(ae[0:R, :], w("cond", R), mv6[0:R, 0:1], r6[0:R, :], ALU.subtract, ALU.mult), t)
            t = dve.do(lambda e: e.tensor_tensor(ae[0:R, :], ae[0:R, :], w("lng", R), ALU.mult), t)
            t = dve.do(lambda e: e.tensor_tensor(ae[0:R, :], ae[0:R, :], w("lnb", R), ALU.add), t)
            bank, k = pj()
            t = pe.do(lambda e: e.transpose(bank[:, 0:32], ae[0:R, :], ident[0:R, 0:R]), t, pj_free[k])
            t = dve.do(lambda e: e.tensor_copy(aeT, bank[:, 0:32]), t)
            t = pe.do(lambda e: e.matmul(bank[:, 32:64], w("lw1"), aeT, start=True, stop=True), t)
            pj_free[k] = t_h = act.do(lambda e: e.activation(hT, bank[:, 32:64], ACTF.Gelu, bias=w("lb1")), t)
            for r in range(8):
                t_hx = pool.do(lambda e: e.tensor_copy(hx4[:, r, :, r:r + 1], hT.unsqueeze(2)), tz, t_h)
            return t_h, t_hx

        def factors(t_h, t_hx):
            bank, k = pj()
            for r in range(8):
                tp = pe.do(lambda e: e.matmul(bank[:, 32 * r:32 * r + 32], w("lw2a", 128, r * 128, (r + 1) * 128), hT, start=True, stop=True),
                           t_h, pj_free[k], inc=r == 7)
            for r in range(8):
                pj_free[k] = t = dve.do(lambda e: e.tensor_scalar(XA[:, :, r:r + 1], bank[:, 32 * r:32 * r + 32].unsqueeze(2), w("lb2a", 128, r, r + 1), None, ALU.add), tp)
            t_xa.append(t)
            yield
            for hh in range(2):
                bank, k = pj()
                for r in range(8):
                    tp = pe.do(lambda e: e.matmul(bank[:, 0:128], hx4[:, r, 16 * hh:16 * hh + 16, :].rearrange("p b s -> p (b s)"),
                                                  w("lw2b", 128, r * 128, (r + 1) * 128), start=r == 0, stop=r == 7), t_hx, pj_free[k], inc=r == 7)
                pj_free[k] = t = dve.do(lambda e: e.tensor_tensor(XBP[hh], bank[:, 0:128], w("lb2b"), ALU.add), tp)
                t_xb.append(t)
                yield

        tx3, tx4, r_gg = {}, {}, {}

        def finish(c):
            q0 = 4 * c
            bn = [bn_r[q0 + b] for b in range(4)]
            t_r = pool.do(lambda e: e.tensor_scalar(rstd[:, q0:q0 + 4].unsqueeze(2), m3[:, q0:q0 + 4, 1:2], 1e-8, None, ALU.add), bn)
            t_r = pool.do(lambda e: e.tensor_tensor(rstd[:, q0:q0 + 4], rstd[:, q0:q0 + 4], mhalf, ALU.pow), t_r, t_half)
            t_b = pool.do(lambda e: e.tensor_scalar(cs(XF, c), cs(XF, c), w("beta"), None, ALU.add))
            yield
            for b in range(4):
                sl = cs(LN[c % 2], b, 128)
                t = dve.do(lambda e: e.tensor_scalar(sl, sl, m3[:, q0 + b, 0:1], rstd[:, q0 + b:q0 + b + 1], ALU.subtract, ALU.mult), t_r, bn)
            yield
            yield
            bank, k = pj()
            for b in range(4):
                tp = pe.do(lambda e: e.transpose(bank[:, b * 128:(b + 1) * 128], cs(LN[c % 2], b, 128), ident), t, pj_free[k], inc=b == 3)
            ln_free[c] = tp
            pj_free[k] = t = dve.do(lambda e: e.scalar_tensor_tensor(cs(XF, c), bank[:, :], w("gamma"), cs(XF, c), ALU.mult, ALU.add), tp, t_b)
            yield
            yield
            bank, k = pj()
            for b in range(4):
                tp = pe.do(lambda e: e.transpose(bank[:, b * 128:(b + 1) * 128], XF[:, (q0 + b) * 128:(q0 + b + 1) * 128], ident), t, pj_free[k], inc=b == 3)
            pj_free[k] = tx3[c] = act.do(lambda e: e.activation(cs(XT, c), bank[:, :], ACTF.Copy), tp)
            yield
            hh, i = c // 4, c % 2
            bank, k = pj()
            tp = pe.do(lambda e: e.matmul(bank[:, :], XA[:, 16 * hh:16 * hh + 16, :].rearrange("p b r -> p (b r)"), cs(XF, c), start=True, stop=True),
                       t_xa, t, pj_free[k])
            pj_free[k] = tg = dve.do(lambda e: e.tensor_tensor(v4(GG[i]), v4(bank[:, :]),
                                                               w("bm16", 128, 4 * (c % 4), 4 * (c % 4) + 4).unsqueeze(2).broadcast_to([128, 4, 128]), ALU.mult),
                                     tp, r_gg.get(c - 2))
            yield
            yield
            bank, k = pj()
            pe.do(lambda e: e.matmul(bank[:, :], w("base"), cs(XF, c), start=True, stop=False), pj_free[k], inc=False)
            r_gg[c] = tp = pe.do(lambda e: e.matmul(bank[:, :], XBP[hh], GG[i], start=False, stop=True), tg, t_xb)
            pj_free[k] = tx4[c] = dve.do(lambda e: e.tensor_tensor(cs(HF, c), cs(XF, c), bank[:, :], ALU.add), tp, v_r[c])
            yield

        th_hx = adapt()
        for _ in proj5(0):
            pass
        projv(0)
        for u in range(3):
            b_K(u)
        fill = [factors(*th_hx)]
        for s in range(U + 6):
            if s < U:
                q, g = units[s]
                b_S(s)
            if 0 <= s - 2 < U:
                b_T(s - 2)
            if s + 3 < U:
                b_K(s + 3)
            if s < U:
                b_E(s)
                if s % 16 == 1 and s // 16 < 7:
                    nxt = proj5(s // 16 + 1)
                    fill.insert(0, nxt)
                if g == 1 and q + 1 < 32:
                    if q % 4 == 3:
                        for _ in nxt:
                            pass
                    projv(q + 1)
            if 0 <= s - 3 < U:
                b_PV(s - 3)
            if s >= 7 and (s - 4) % 4 == 3 and (s - 4) // 4 < 32:
                q = (s - 4) // 4
                b_N(q)
                if q % 4 == 3:
                    fill.append(finish(q // 4))
            while fill and next(fill[0], "over") == "over":
                fill.pop(0)
        for f in fill:
            for _ in f:
                pass

        barrier("s7", 25600)
        fr = [None] * 8
        bk = [0]
        H1all = ar(4096)
        H1 = [cs(H1all, c) for c in range(8)]
        AL = ar(2048)
        ATT = ar(2048)
        XTM = ar(32 * 129).rearrange("p (q d) -> p q d", d=129)
        LG = [ar(256) for _ in range(2)]
        MR = [ar(256) for _ in range(2)]
        hn, wvo, bvo = ar(64), ar(128), ar(128)
        tiles = [[ar(512) for _ in range(5)] for _ in range(4)]
        smean, b1e, tinv, br, bz, nq = sm(1), sm(1), sm(1), sm(1), sm(1), sm(1)
        m8 = [sm(32) for _ in range(2)]
        sums = [sm(4) for _ in range(2)]
        t_h1 = pool.do(lambda e: e.memset(H1all[64:65, :], 1.0))
        t_one = pool.do(lambda e: e.memset(XTM[:, :, 128:129], 1.0), t_h1)
        t_bo = [pool.do(lambda e, c=c: e.tensor_tensor(v4(cs(XT, c)), v4(cs(XT, c)), w("bo").unsqueeze(1).broadcast_to([128, 4, 128]), ALU.add))
                for c in range(CH)]

        t = dve.do(lambda e: e.tensor_reduce(smean, w("slotT"), AX.X, ALU.add))
        t = dve.do(lambda e: e.tensor_scalar(smean, smean, 1.0 / 64, None, ALU.mult), t)
        k = nb()
        t = pe.do(lambda e: e.matmul(PB[k][0:64, 0:1], w("fw1b"), smean, start=True, stop=True), t)
        fr[k] = t_b1 = dve.do(lambda e: e.tensor_tensor(b1e[0:64, :], PB[k][0:64, 0:1], w("fb1", 64), ALU.add), t)
        th1 = []
        for c in range(CH):
            k = nb()
            tp = pe.do(lambda e: e.matmul(PB[k][0:64, :], w("fw1a"), cs(HF, c), start=True, stop=True), fr[k])
            fr[k] = t = act.do(lambda e: e.activation(H1[c][0:64, :], PB[k][0:64, :], ACTF.Gelu, bias=b1e[0:64, :]), tp, t_b1)
            th1.append(t)
        t = dve.do(lambda e: e.tensor_scalar(tinv, w("tau"), -1.0, None, ALU.mult))
        t = dve.do(lambda e: e.tensor_tensor(tinv, tinv, w("tau"), ALU.max), t)
        t = dve.do(lambda e: e.tensor_scalar(tinv, tinv, 0.1, None, ALU.add), t)
        t_ti = dve.do(lambda e: e.reciprocal(tinv, tinv), t)
        bih, bhh = w("bih"), w("bhh")
        t_bs = []
        for dst, g in ((br, 0), (bz, 1)):
            t = dve.do(lambda e: e.tensor_tensor(dst, bih[:, g:g + 1], bhh[:, g:g + 1], ALU.add))
            t_bs.append(dve.do(lambda e: e.tensor_scalar(dst, dst, 0.5, None, ALU.mult), t))
        sc7 = float(32.0 ** -0.5)
        t_nq = dve.do(lambda e: e.tensor_scalar(nq, w("fbq"), -sc7, None, ALU.mult))
        k = nb()
        tp = pe.do(lambda e: e.matmul(PB[k][:, 0:64], w("whhT", 128, 256, 384), w("slotT"), start=True, stop=True), fr[k])
        fr[k] = t_hn = dve.do(lambda e: e.tensor_scalar(hn, PB[k][:, 0:64], bhh[:, 2:3], 0.5, ALU.add, ALU.mult), tp)
        k = nb()
        tp = pe.do(lambda e: e.matmul(PB[k][:, 0:128], w("wvpT"), w("wo"), start=True, stop=True), fr[k], inc=False)
        tp = pe.do(lambda e: e.matmul(PB[k][:, 128:256], w("bvp").broadcast_to([128, 128]), w("wo"), start=True, stop=True))
        t_vo = act.do(lambda e: e.activation(wvo, PB[k][:, 0:128], ACTF.Copy), tp)
        fr[k] = t_bvo = dve.do(lambda e: e.tensor_copy(bvo, PB[k][:, 128:256]), tp, t_vo)

        txm, tal, tatt = {}, {}, {}
        r_lg, r_mr, r_m8 = [None, None], [None, None], [None, None]

        def b4(ap):
            return ap.rearrange("p (b s) -> p b s", b=4)

        def route(c):
            i = c % 2
            k = nb()
            for b in range(4):
                tl = pe.do(lambda e: e.matmul(PB[k][:, b * 64:(b + 1) * 64], H1[c][0:65, b * 128:(b + 1) * 128], w("fw2", 65), start=True, stop=True),
                           th1[c], t_h1, fr[k], inc=b == 3)
            lg = PB[k][:, 0:256]
            kx = nb()
            for b in range(4):
                q = 4 * c + b
                tp = pe.do(lambda e: e.transpose(PB[kx][:, b * 128:(b + 1) * 128], HF[:, q * 128:(q + 1) * 128], ident), fr[kx], inc=b == 3)
            fr[kx] = txm[c] = act.do(lambda e: e.activation(XTM[:, 4 * c:4 * c + 4, 0:128], v4(PB[kx][:, :]), ACTF.Copy), tp)
            tq = [dve.do(lambda e: e.max(m8[i][:, 8 * b:8 * b + 8], lg[:, b * 64:(b + 1) * 64]), tl, r_m8[i]) for b in range(4)]
            top = b4(m8[i])[:, :, 0:1].broadcast_to([128, 4, 64])
            t2 = dve.do(lambda e: e.tensor_tensor(b4(LG[i]), b4(lg), top, ALU.subtract), tq, r_lg[i])
            for b in range(4):
                sl = slice(b * 64, (b + 1) * 64)
                tr = dve.do(lambda e: e.match_replace(out=MR[i][:, sl], in_to_replace=m8[i][:, 8 * b:8 * b + 8], in_values=lg[:, sl], imm_value=-3.0e38),
                            tq[b], r_mr[i])
            r_m8[i] = [t2, tr]
            fr[k] = t = dve.do(lambda e: e.tensor_tensor(MR[i], MR[i], lg, ALU.not_equal), tr)
            t2 = act.do(lambda e: e.activation(LG[i], LG[i], ACTF.Exp, scale=tinv), t2, t_ti)
            yield
            for b in range(4):
                sl = slice(b * 64, (b + 1) * 64)
                o = c * 256 + b * 64
                ta = dve.do(lambda e: e.tensor_tensor_reduce(AL[:, o:o + 64], LG[i][:, sl], MR[i][:, sl], 1.0, 0.0, ALU.mult, ALU.add,
                                                             sums[i][:, b:b + 1]), t2, t)
            r_lg[i] = r_mr[i] = ta
            t = dve.do(lambda e: e.reciprocal(sums[i], sums[i]), ta)
            al = AL[:, c * 256:(c + 1) * 256]
            tal[c] = dve.do(lambda e: e.tensor_tensor(b4(al), b4(al), sums[i].unsqueeze(2).broadcast_to([128, 4, 64]), ALU.mult), t)
            yield
            k = nb()
            for p in range(2):
                tp = pe.do(lambda e: e.transpose(PB[k][:, p * 128:(p + 1) * 128], al[:, p * 128:(p + 1) * 128], ident), tal[c], fr[k], inc=p == 1)
            fr[k] = tatt[c] = act.do(lambda e: e.activation(ATT[:, c * 256:(c + 1) * 256], PB[k][:, 0:256], ACTF.Copy), tp)

        def v8(ap):
            return ap.rearrange("p (b s) -> p b s", b=8)

        sp.stage("s7")
        pm = w("pmask")

        def slots(n):
            ra, rb = route(2 * n), route(2 * n + 1)
            next(ra)
            yield
            next(rb)
            next(ra)
            yield
            next(rb)
            next(ra, None)
            yield
            next(rb, None)
            T2, T3, SN, VV, VS = tiles[n]
            SI, T1 = cs(HF, 2 * n), cs(HF, 2 * n + 1)
            hf_free = [txm[2 * n], txm[2 * n + 1], th1[2 * n], th1[2 * n + 1]]
            dn, mx7, sm7, rs7, bn7, mv7 = sm(4), sm(4), sm(4), sm(4), sm(24), sm(8)
            pairs = [slice(p * 128, (p + 1) * 128) for p in range(4)]
            ts = []
            for hf in range(2):
                k = nb()
                for p in range(2):
                    for hh in range(2):
                        q = 8 * n + 4 * hf + 2 * p + hh
                        tp = pe.do(lambda e: e.matmul(PB[k][64 * hh:64 * hh + 64, 129 * p:129 * p + 129], AL[:, q * 64:(q + 1) * 64], XTM[:, q, :],
                                                      start=True, stop=True), tal[q // 4], txm[q // 4], t_one, fr[k], inc=(p, hh) == (1, 1))
                b3 = PB[k][:, 0:258].rearrange("p (q d) -> p q d", d=129)
                d2 = dn[:, 2 * hf:2 * hf + 2]
                t = dve.do(lambda e: e.tensor_scalar(d2.unsqueeze(2), b3[:, :, 128:129], 1e-8, None, ALU.add), tp)
                t = dve.do(lambda e: e.reciprocal(d2, d2), t)
                fr[k] = t = dve.do(lambda e: e.tensor_tensor(T2[:, 256 * hf:256 * hf + 256].rearrange("p (q d) -> p q d", d=128), b3[:, :, 0:128],
                                                             d2.unsqueeze(2).broadcast_to([128, 2, 128]), ALU.mult), t)
                ts.append(t)
            yield
            k = nb()
            for p in range(4):
                tp = pe.do(lambda e: e.transpose(PB[k][:, pairs[p]], T2[:, pairs[p]], ident), ts[p // 2], fr[k], inc=p == 3)
            fr[k] = t = act.do(lambda e: e.activation(SI, PB[k][:, :], ACTF.Copy), tp, hf_free)
            yield
            tg = []
            sb_ = w("slotT").unsqueeze(1).broadcast_to([128, 8, 64])
            for g, dst, bias in ((0, T1, br), (1, T2, bz)):
                k = nb()
                pe.do(lambda e: e.matmul(PB[k][:, :], w("wihT", 128, g * 128, (g + 1) * 128), SI, start=True, stop=False), t, fr[k], inc=False)
                tp = pe.do(lambda e: e.matmul(v8(PB[k][:, :]), w("whhT", 128, g * 128, (g + 1) * 128), sb_, start=False, stop=True))
                fr[k] = ta = act.do(lambda e: e.activation(dst, PB[k][:, :], ACTF.Tanh, bias=bias, scale=0.5), tp, t_bs, hf_free)
                tg.append(ta)
            k = nb()
            tp = pe.do(lambda e: e.matmul(PB[k][:, :], w("wihT", 128, 256, 384), SI, start=True, stop=True), fr[k])
            yield
            t = dve.do(lambda e: e.scalar_tensor_tensor(v8(T1), v8(T1), 1.0, hn.unsqueeze(1).broadcast_to([128, 8, 64]), ALU.add, ALU.mult), tg[0], t_hn)
            fr[k] = t = dve.do(lambda e: e.tensor_tensor(T1, T1, PB[k][:, :], ALU.add), t, tp)
            tn = act.do(lambda e: e.activation(T3, T1, ACTF.Tanh, bias=bih[:, 2:3]), t)
            yield
            t = dve.do(lambda e: e.tensor_tensor(v8(SN), sb_, v8(T3), ALU.subtract), tn)
            t = dve.do(lambda e: e.scalar_tensor_tensor(SN, T2, 1.0, SN, ALU.add, ALU.mult), t, tg[1])
            tsn = dve.do(lambda e: e.scalar_tensor_tensor(SN, SN, 0.5, T3, ALU.mult, ALU.add), t)
            yield
            k = nb()
            tp = pe.do(lambda e: e.matmul(PB[k][0:32, :], w("fwq"), SN, start=True, stop=True), fr[k], tsn)
            fr[k] = tq = act.do(lambda e: e.activation(T1[0:32, :], PB[k][0:32, :], ACTF.Identity, bias=nq[0:32, :], scale=-sc7), tp, t_nq, tn)
            k = nb()
            tp = pe.do(lambda e: e.matmul(PB[k][0:32, :], w("fwk"), SN, start=True, stop=True), fr[k])
            fr[k] = tk = act.do(lambda e: e.activation(T2[0:32, :], PB[k][0:32, :], ACTF.Identity, bias=w("fbk", 32)), tp, tsn)
            kv = nb()
            for p in range(4):
                tv = pe.do(lambda e: e.matmul(PB[kv][:, pairs[p]], SN[:, pairs[p]], w("fwv"), start=True, stop=True), fr[kv], inc=p == 3)
            fr[kv] = tv = dve.do(lambda e: e.tensor_tensor(v4(VV), v4(PB[kv][:, :]), w("fbv").unsqueeze(1).broadcast_to([128, 4, 128]), ALU.add), tv)
            yield
            k = nb()
            for p in range(4):
                tp = pe.do(lambda e: e.matmul(PB[k][:, pairs[p]], T1[0:32, pairs[p]], T2[0:32, pairs[p]], start=True, stop=True), fr[k], tq, tk, inc=p == 3)
            te = []
            for p in range(4):
                fr[k] = t = dve.do(lambda e: e.tensor_tensor_reduce(T3[:, pairs[p]], PB[k][:, pairs[p]], pm, 1.0, 3.0e38, ALU.add, ALU.min, mx7[:, p:p + 1]), tp, tsn)
                te.append(act.do(lambda e: e.activation(T3[:, pairs[p]], T3[:, pairs[p]], ACTF.Exp, bias=mx7[:, p:p + 1], scale=-1.0,
                                                        accum_out=sm7[:, p:p + 1]), t))
            yield
            k = nb()
            for p in range(4):
                tp = pe.do(lambda e: e.transpose(PB[k][:, pairs[p]], T3[:, pairs[p]], ident), te, fr[k], inc=p == 3)
            fr[k] = t = act.do(lambda e: e.activation(SI, PB[k][:, :], ACTF.Copy), tp)
            k = nb()
            for p in range(4):
                ty = pe.do(lambda e: e.transpose(PB[k][:, pairs[p]], SN[:, pairs[p]], ident), fr[k], inc=p == 3)
            fr[k] = ty = act.do(lambda e: e.activation(T1, PB[k][:, :], ACTF.Copy), ty, tp)
            tr = dve.do(lambda e: e.reciprocal(sm7, sm7), te)
            yield
            k = nb()
            for p in range(4):
                tp = pe.do(lambda e: e.matmul(PB[k][:, pairs[p]], SI[:, pairs[p]], VV[:, pairs[p]], start=True, stop=True), t, tv, fr[k], inc=p == 3)
            tb = []
            for p in range(4):
                fr[k] = t = dve.do(lambda e: e.scalar_tensor_tensor(T1[:, pairs[p]], PB[k][:, pairs[p]], sm7[:, p:p + 1], T1[:, pairs[p]], ALU.mult, ALU.add), tp, tr, ty)
                t = dve.do(lambda e: e.bn_stats(bn7[:, 6 * p:6 * p + 6], T1[:, pairs[p]]), t)
                tb.append(dve.do(lambda e: e.bn_aggr(mv7[:, 2 * p:2 * p + 2], bn7[:, 6 * p:6 * p + 6]), t))
            t = pool.do(lambda e: e.tensor_scalar(rs7.unsqueeze(2), mv7.rearrange("p (q s) -> p q s", s=2)[:, :, 1:2], 1e-5, None, ALU.add), tb)
            t = pool.do(lambda e: e.tensor_tensor(rs7, rs7, mhalf, ALU.pow), t)
            yield
            for p in range(4):
                tl = dve.do(lambda e: e.tensor_scalar(T1[:, pairs[p]], T1[:, pairs[p]], mv7[:, 2 * p:2 * p + 1], rs7[:, p:p + 1], ALU.subtract, ALU.mult), t, tb)
            k = nb()
            for p in range(4):
                tp = pe.do(lambda e: e.transpose(PB[k][:, pairs[p]], T1[:, pairs[p]], ident), tl, fr[k], inc=p == 3)
            fr[k] = t = act.do(lambda e: e.activation(T2, PB[k][:, :], ACTF.Identity, bias=w("flnb"), scale=w("flng")), tp)
            yield
            k = nb()
            for p in range(4):
                tp = pe.do(lambda e: e.matmul(PB[k][:, pairs[p]], T2[:, pairs[p]], wvo, start=True, stop=True), t, t_vo, fr[k], inc=p == 3)
            fr[k] = t = dve.do(lambda e: e.tensor_tensor(v4(VS), v4(PB[k][:, :]), bvo.unsqueeze(1).broadcast_to([128, 4, 128]), ALU.add), tp, t_bvo)
            yield
            for c in (2 * n, 2 * n + 1):
                ks = [nb(), nb()]
                for p in range(2):
                    for hh in range(2):
                        m = 2 * c + p
                        ml = pairs[m % 4]
                        tp = pe.do(lambda e: e.matmul(PB[ks[hh]][:, p * 128:(p + 1) * 128], ATT[64 * hh:64 * hh + 64, m * 128:(m + 1) * 128],
                                                      VS[64 * hh:64 * hh + 64, ml], start=True, stop=True),
                                   t, tatt[c], fr[ks[0]], fr[ks[1]], inc=(p, hh) == (1, 1))
                x4 = cs(XT, c).rearrange("p (q hh t) -> p q hh t", q=2, hh=2)
                tx = []
                for hh in range(2):
                    fr[ks[hh]] = ta = dve.do(lambda e: e.tensor_tensor(x4[:, :, hh, :], x4[:, :, hh, :],
                                                                       PB[ks[hh]][:, 0:256].rearrange("p (q t) -> p q t", q=2), ALU.add), tp, t_bo[c])
                    tx.append(ta)
                sp.wait([tx])
                nc.sync.dma_start(out_d[4 * c:4 * c + 4, :, :].rearrange("b t d -> t b d"), v4(cs(XT, c))).then_inc(s_out, 16)
                yield

        starts, live = [slots(n) for n in range(4)], []
        while starts or live:
            if starts:
                live.append(starts.pop(0))
            for gnr in list(live):
                if next(gnr, "over") == "over":
                    live.remove(gnr)
        nc.sync.wait_ge(s_out, 16 * CH)


def pack(inp):
    f = np.float32
    wide = np.zeros((128, WIDE), f)

    def put(name, a):
        o, c = OFF[name]
        a = np.asarray(a)
        assert a.shape[1] == c, (name, a.shape)
        wide[0:a.shape[0], o:o + c] = a

    def col(name, a):
        put(name, np.asarray(a).reshape(-1, 1))

    def row(name, a, rows=128):
        a = np.asarray(a).reshape(1, -1)
        put(name, np.broadcast_to(a, (rows, a.shape[1])))

    def blocks(a, n):
        a = np.asarray(a)
        return a.reshape(n, 128, a.shape[-1]).transpose(1, 0, 2).reshape(128, -1)

    put("condT", np.asarray(inp["cond_1024"]).T)
    put("w0", inp["L0_cond_weight"])
    put("ident", np.eye(128, dtype=f))
    i, j = np.arange(128)[:, None], np.arange(128)[None, :]
    put("mask", np.where(j > i, f(-NEG), f(0)))
    wqkv = np.asarray(inp["L0_attn_W_qkv"])
    for n, o in (("wqT", 0), ("wkT", 1024), ("wvT", 2048)):
        put(n, wqkv[:, o:o + 1024].reshape(128, 8, 128).transpose(2, 1, 0).reshape(128, 1024))
    put("wout", blocks(inp["L0_attn_W_out"], 8))
    for n, k in (("f", "f"), ("i", "i"), ("h", "h")):
        put(f"w{n}T", np.asarray(inp[f"L0_cond2_W_{k}"]).T)
        col(f"b{n}", inp[f"L0_cond2_b_{k}"])
    for k in (1, 2):
        put(f"cw{k}", inp[f"L0_ffn_cn_w{k}"])
    w3, w4 = np.asarray(inp["L0_ffn_cn_w3"]), np.asarray(inp["L0_ffn_cn_w4"])
    both = np.zeros((128, 64), f)
    both[0:64, 0:32] = w3
    both[64:128, 32:64] = w3
    put("cw3", both)
    both = np.zeros((64, 256), f)
    both[0:32, 0:128] = w4
    both[32:64, 128:256] = w4
    put("cw4", both)
    col("cb1", inp["L0_ffn_cn_b1"])
    col("cb2", np.tile(np.asarray(inp["L0_ffn_cn_b2"]), 2))
    col("cb3", np.tile(np.asarray(inp["L0_ffn_cn_b3"]), 2))
    row("cb4", inp["L0_ffn_cn_b4"])
    for k in (1, 2):
        put(f"gw{k}", inp[f"L0_ffn_gc_w{k}"])
        col(f"gb{k}", inp[f"L0_ffn_gc_b{k}"])
    put("gw3", np.broadcast_to(np.asarray(inp["L0_ffn_gc_w3"]), (32, 128)))
    row("gb3", inp["L0_ffn_gc_b3"])
    row("ar", inp["L0_ffn_adaptive_range"])
    tw = np.zeros((128, 128), f)
    r = np.arange(32)
    tw[64 + r, r] = 1
    tw[96 + r, 32 + r] = -1
    tw[r, 64 + r] = -1
    tw[32 + r, 96 + r] = 1
    put("twist", tw)
    put("gatew", blocks(inp["L1_cond_gate_w"], 3))
    row("gateb", inp["L1_cond_gate_b"], 32)
    put("timew", inp["L1_cond_time_w"])
    row("timeb", inp["L1_cond_time_b"], 32)
    lower = np.zeros((4, 4), f)
    for a in range(4):
        lower[a, :a] = 1
    row("lower", lower, 32)
    put("ew1", np.asarray(inp["L1_cond_ew1"]).transpose(1, 0, 2).reshape(128, 2048))
    put("eb1", np.asarray(inp["L1_cond_eb1"]).reshape(16, 128).T)
    put("ew2", blocks(np.asarray(inp["L1_cond_ew2"]).reshape(2048, 128), 16))
    put("eb2", np.asarray(inp["L1_cond_eb2"]).T)
    put("sw1", inp["L1_cond_sw1"])
    put("sb1", np.asarray(inp["L1_cond_sb1"]).reshape(4, 128).T)
    put("sw2", blocks(inp["L1_cond_sw2"], 4))
    col("sb2", inp["L1_cond_sb2"])
    for n, k in (("q", "q"), ("k", "k")):
        put(f"a{n}", inp[f"L1_attn_W{k}"])
        col(f"b{n}", inp[f"L1_attn_b{k}"])
    put("av", inp["L1_attn_Wv"])
    row("bv", inp["L1_attn_bv"])
    col("gamma", inp["L1_attn_gamma"])
    col("beta", inp["L1_attn_beta"])
    put("hm", (np.arange(128)[:, None] // 8 % 4 == np.arange(4)[None, :]).astype(f))
    put("cond", inp["cond_1024"])
    row("lng", inp["L1_cond2_ln_g"], 32)
    row("lnb", inp["L1_cond2_ln_b"], 32)
    put("lw1", inp["L1_cond2_w1"])
    col("lb1", inp["L1_cond2_b1"])
    w2 = np.asarray(inp["L1_cond2_w2"]).reshape(128, 2, 128, 8).transpose(1, 0, 3, 2)
    put("lw2a", w2[0].reshape(128, 1024))
    put("lw2b", w2[1].reshape(128, 1024))
    b2 = np.asarray(inp["L1_cond2_b2"]).reshape(2, 128, 8)
    put("lb2a", b2[0])
    put("lb2b", np.tile(b2[1].T, (16, 1)))
    put("base", inp["L1_cond2_base_layer"])
    put("bm16", (np.arange(128)[:, None] // 8 == np.arange(16)[None, :]).astype(f))
    w1 = np.asarray(inp["L1_ffn_w1"])
    put("fw1a", w1[:128])
    put("fw1b", w1[128:])
    col("fb1", inp["L1_ffn_b1"])
    put("fw2", np.concatenate([np.asarray(inp["L1_ffn_w2"]), np.asarray(inp["L1_ffn_b2"]).reshape(1, 64)]))
    row("tau", inp["L1_ffn_tau"])
    put("wihT", np.asarray(inp["L1_ffn_Wih"]).T)
    put("whhT", np.asarray(inp["L1_ffn_Whh"]).T)
    put("bih", np.asarray(inp["L1_ffn_bih"]).reshape(3, 128).T)
    put("bhh", np.asarray(inp["L1_ffn_bhh"]).reshape(3, 128).T)
    put("slotT", np.asarray(inp["L1_ffn_slot_init"]).T)
    put("fwq", inp["L1_ffn_wq"])
    col("fbq", inp["L1_ffn_bq"])
    put("fwk", inp["L1_ffn_wk"])
    col("fbk", inp["L1_ffn_bk"])
    put("fwv", inp["L1_ffn_wv"])
    row("fbv", inp["L1_ffn_bv"])
    col("flng", inp["L1_ffn_ln_g"])
    col("flnb", inp["L1_ffn_ln_b"])
    put("wvpT", np.asarray(inp["L1_ffn_wvp"]).T)
    col("bvp", inp["L1_ffn_bvp"])
    put("wo", inp["L1_ffn_wo"])
    row("bo", inp["L1_ffn_bo"])
    put("pmask", np.where(i // 64 == j // 64, f(0), f(-NEG)))
    xT = np.ascontiguousarray(np.asarray(inp["x"]).reshape(N, D).T)
    return {"in_xT": xT, "in_w": wide}


def kernel(**inputs):
    import concourse.bacc as _bacc
    from concourse.bass_utils import run_bass_kernel_spmd as _run

    nc = _bacc.Bacc("TRN2", target_bir_lowering=False, num_devices=1)
    arrays = pack(inputs)
    aps = [nc.dram_tensor(n, a.shape, F32, kind="ExternalInput").ap() for n, a in arrays.items()]
    out = nc.dram_tensor("out_0", (B, T, D), F32, kind="ExternalOutput").ap()
    build(nc, *aps, out)
    r = _run(nc, [arrays], core_ids=[0])
    return r.results[0]["out_0"]
```

```python
from contextlib import ExitStack

import numpy as np

import concourse.bass as bass
from concourse import mybir

F32 = mybir.dt.float32
F32R = mybir.dt.float32r
BF16 = mybir.dt.bfloat16
ALU = mybir.AluOpType
ACTF = mybir.ActivationFunctionType
AX = mybir.AxisListType

B, T, D = 32, 128, 128
N = B * T
NEG = -1e30

COLS = [
    ("wqT", 1024), ("wkT", 1024), ("w0", 128), ("wvT", 1024), ("wout", 1024),
    ("condT", 32), ("ident", 128), ("mask", 128),
    ("wfT", 128), ("wiT", 128), ("whT", 128), ("bf", 1), ("bi", 1), ("bh", 1),
    ("cw1", 128), ("cw2", 64), ("cw3", 64), ("cw4", 256), ("cb1", 1), ("cb2", 1), ("cb3", 1), ("cb4", 1),
    ("gw1", 64), ("gw2", 32), ("gw3", 128), ("gb1", 1), ("gb2", 1), ("gb3", 1), ("ar", 1), ("twist", 128),
    ("gatew", 12), ("gateb", 4), ("timew", 8), ("timeb", 8), ("lower", 16),
    ("ew1", 2048), ("eb1", 16), ("ew2", 2048), ("eb2", 4), ("sw1", 512), ("sb1", 4), ("sw2", 512), ("sb2", 1),
    ("aq", 128), ("bq", 1), ("ak", 128), ("bk", 1), ("av", 128), ("bv", 128), ("gamma", 1), ("beta", 1),
    ("hm", 4),
    ("cond", 128), ("lng", 128), ("lnb", 128), ("lw1", 128), ("lb1", 1), ("lw2a", 1024), ("lw2b", 1024),
    ("lb2a", 8), ("lb2b", 128), ("base", 128), ("bm16", 16),
    ("fw1a", 64), ("fw1b", 64), ("fb1", 1), ("fw2", 64), ("tau", 1), ("wihT", 384), ("whhT", 384),
    ("bih", 3), ("bhh", 3), ("slotT", 64), ("fwq", 32), ("fbq", 1), ("fwk", 32), ("fbk", 1), ("fwv", 128),
    ("fbv", 128), ("flng", 1), ("flnb", 1), ("wvpT", 128), ("bvp", 1), ("wo", 128), ("bo", 128), ("pmask", 128),
]
OFF, _at = {}, 0
for _n, _c in COLS:
    OFF[_n] = (_at, _c)
    _at += _c
WIDE = _at
FIRST = OFF["condT"][0]


class Queue:

    def __init__(self, eng, new_sem, name):
        self.eng, self.new_sem, self.name = eng, new_sem, name
        self.seen = {}
        self.stage("s0")

    def stage(self, label):
        self.sem = self.new_sem(f"{self.name}_{label}")
        self.n = 0

    def wait(self, toks):
        need = {}
        todo = list(toks)
        while todo:
            t = todo.pop()
            if t is None:
                continue
            if isinstance(t, list):
                todo += t
                continue
            s, v = t
            if v > need.get(id(s), (s, 0))[1]:
                need[id(s)] = (s, v)
        for k, (s, v) in need.items():
            if self.seen.get(k, 0) < v:
                self.eng.wait_ge(s, v)
                self.seen[k] = v

    def do(self, make, *toks, inc=True):
        self.wait(toks)
        ins = make(self.eng)
        if not inc:
            return None
        self.n += 1
        ins.then_inc(self.sem, 1)
        return (self.sem, self.n)

    def last(self):
        return (self.sem, self.n) if self.n else None


def build(nc, xT_d, w_d, out_d):
    ctx = ExitStack()
    with ctx:
        def sb(name, shape, dt=F32):
            return ctx.enter_context(nc.sbuf_tensor(name, shape, dt))

        def new_sem(name):
            return ctx.enter_context(nc.semaphore(name))

        PB = [ctx.enter_context(nc.psum_tensor(f"PB{i}", [128, 512], F32)) for i in range(8)]
        W = sb("W", [128, WIDE - FIRST])
        XF = sb("XF", [128, N])
        HF = sb("HF", [128, N])
        XT = sb("XT", [128, N])
        small = sb("small", [128, 1600])
        scope = ExitStack()
        ctx.callback(scope.close)
        W1 = scope.enter_context(nc.sbuf_tensor("W1", [128, FIRST], F32))

        def w(name, rows=128, a=0, b=None):
            o, c = OFF[name]
            b = c if b is None else b
            if o < FIRST:
                return W1[0:rows, o + a:o + b]
            return W[0:rows, o - FIRST + a:o - FIRST + b]

        used = [0]

        def sm(cols):
            a = used[0]
            used[0] += cols
            assert used[0] <= 1600
            return small[:, a:a + cols]

        area = {}

        def scratch(label, cols, rcols=0):
            area["AR"] = scope.enter_context(nc.sbuf_tensor(f"AR_{label}", [128, cols], F32))
            area["RR"] = scope.enter_context(nc.sbuf_tensor(f"RR_{label}", [128, rcols], F32R)) if rcols else None
            area["a"], area["r"], area["cols"], area["rcols"] = 0, 0, cols, rcols

        def ar(cols):
            a = area["a"]
            area["a"] += cols
            assert area["a"] <= area["cols"], area
            return area["AR"][:, a:a + cols]

        def rr(cols):
            a = area["r"]
            area["r"] += cols
            assert area["r"] <= area["rcols"], area
            return area["RR"][:, a:a + cols]

        pe = Queue(nc.tensor, new_sem, "pe")
        act = Queue(nc.scalar, new_sem, "act")
        dve = Queue(nc.vector, new_sem, "dve")
        pool = Queue(nc.gpsimd, new_sem, "pool")
        engines = [pe, act, dve, pool]
        s_w = [new_sem(f"s_w{i}") for i in range(4)]
        s_x = [new_sem(f"s_x{i}") for i in range(4)]
        s_out = new_sem("s_out")

        o_v = OFF["wvT"][0]
        o_s = OFF["wfT"][0]

        def load_x(i):
            nc.sync.dma_start(XF[:, i * 1024:(i + 1) * 1024], xT_d[:, i * 1024:(i + 1) * 1024]).then_inc(s_x[i], 16)

        nc.sync.dma_start(W[:, 0:o_s - FIRST], w_d[:, FIRST:o_s]).then_inc(s_w[1], 16)
        nc.sync.dma_start(W1[:, 0:o_v], w_d[:, 0:o_v]).then_inc(s_w[0], 16)
        load_x(0)
        nc.sync.dma_start(W1[:, o_v:FIRST], w_d[:, o_v:FIRST]).then_inc(s_w[2], 16)
        for i in range(1, 4):
            load_x(i)
        nc.sync.dma_start(W[:, o_s - FIRST:WIDE - FIRST], w_d[:, o_s:WIDE]).then_inc(s_w[3], 16)
        LQ, LC, LV, LW = [(s, 16) for s in s_w]
        LX = [(s, 16) for s in s_x]

        def barrier(label, cols, rcols=0, more=()):
            toks = [e.last() for e in engines] + list(more)
            for e in engines:
                e.stage(label)
                e.wait(toks)
            scope.close()
            scratch(label, cols, rcols)

        CH = 8

        def cs(tile, c, n=512):
            return tile[:, c * n:(c + 1) * n]

        def v4(ap):
            return ap.rearrange("p (b t) -> p b t", b=4)

        ident = w("ident")

        scratch("s1", 1664, 15360)
        GS = scope.enter_context(nc.sbuf_tensor("GS", [128, 1536], F32))
        pad = pool.do(lambda e: e.memset(small[:, 0:8], 0.0))
        c_eps8, c_eps5, c_zero = sm(1), sm(1), sm(1)
        used[0] = 8
        t = pool.do(lambda e: e.memset(c_eps8, 1e-8), pad)
        eps_tok = pool.do(lambda e: e.memset(c_eps5, 1e-5), t)
        ones = sm(128)
        t_ones = pool.do(lambda e: e.memset(ones, 1.0))

        AH, AL_ = rr(2048), rr(2048)
        BH, BL = rr(2048), rr(2048)
        t_A, t_B, pb_w = [], [], [None] * 4

        def products(lhs, rhs, scale, hi, lo, toks, out):
            for s in range(2):
                for hf in range(2):
                    k = 2 * s + hf
                    for f in range(4):
                        fo = 4 * hf + f
                        tp = pe.do(lambda e: e.matmul(PB[k][:, f * 128:(f + 1) * 128], w(lhs, 128, fo * 128, (fo + 1) * 128)[64 * s:64 * s + 64, :],
                                                      w(rhs, 128, fo * 128, (fo + 1) * 128)[64 * s:64 * s + 64, :], start=True, stop=True),
                                   toks, pb_w[k], inc=f == 3)
                    h_ = hi.rearrange("p (f s j) -> p f s j", f=8, s=2)[:, 4 * hf:4 * hf + 4, s, :]
                    l_ = lo.rearrange("p (f s j) -> p f s j", f=8, s=2)[:, 4 * hf:4 * hf + 4, s, :]
                    b3 = PB[k][:, :].rearrange("p (f j) -> p f j", f=4)
                    t = act.do(lambda e: e.activation(h_, b3, ACTF.Copy, scale=scale), tp)
                    pb_w[k] = t2 = dve.do(lambda e: e.scalar_tensor_tensor(l_, b3, scale, h_, ALU.mult, ALU.subtract), t)
                    out += [t, t2]

        ysT, ys2, dT, nbf, nbi = sm(32), sm(32), sm(32), sm(1), sm(1)
        w2 = ar(128)
        t_ys = dve.do(lambda e: e.tensor_scalar(ysT, w("condT"), float(np.float32(1.0) / np.sqrt(np.float32(128))), None, ALU.mult), LC)
        t2 = dve.do(lambda e: e.tensor_tensor(ys2, ysT, ysT, ALU.mult), t_ys)
        t3 = dve.do(lambda e: e.tensor_tensor(w2, w("w0"), w("w0"), ALU.mult), LQ)
        t4 = pe.do(lambda e: e.matmul(PB[6][:, 0:32], w2, ys2, start=True, stop=True), t2, t3)
        t5 = act.do(lambda e: e.activation(dT, PB[6][:, 0:32], ACTF.Sqrt, bias=c_eps8), t4, eps_tok)
        t_d = dve.do(lambda e: e.reciprocal(dT, dT), t5)
        products("wkT", "wqT", -0.125, AH, AL_, LQ, t_A)

        NCH = 16
        xs, uf = ar(256), ar(256)
        UH, UL = [rr(256) for _ in range(2)], [rr(256) for _ in range(2)]
        KH = [rr(1024).rearrange("p (h b j) -> p h b j", h=4, b=2) for _ in range(3)]
        KL = [rr(1024).rearrange("p (h b j) -> p h b j", h=4, b=2) for _ in range(3)]
        VP = [cs(XT, i) for i in range(8)] + [ar(512) for _ in range(2)]
        wvo_raw = w("wvT", 128, 0, 512), w("wvT", 128, 512, 1024), w("wout", 128, 0, 512)
        SS = [W1[:, i * 512:(i + 1) * 512] for i in range(4)] + [wvo_raw[0]]
        PT = list(wvo_raw[1:])
        mx = [sm(4) for _ in range(5)]
        rc = [sm(4) for _ in range(5)]
        FG, IG, SM = GS[:, 0:512], GS[:, 512:1024], GS[:, 1024:1536]
        pj_free = {5: None, 6: t5, 7: None}
        pj_n = [0]

        def pj():
            k = 5 + pj_n[0] % 3
            pj_n[0] += 1
            return PB[k], k

        tok_u, tok_k, tok_v = {}, {}, {}
        last_s, u_readers = {}, {}
        xs_r, uf_r = [None], [None]
        tok_x, xs_tok = {}, {}

        def pair3(bank_ap, lh, ll, rh, rl, toks, inc=True):
            pe.do(lambda e: e.matmul(bank_ap, lh, rh, start=True, stop=False), toks, inc=False)
            pe.do(lambda e: e.matmul(bank_ap, ll, rh, start=False, stop=False), inc=False)
            return pe.do(lambda e: e.matmul(bank_ap, lh, rl, start=False, stop=True), inc=inc)

        def scaled(c):
            x3 = XF[:, c * 256:(c + 1) * 256].rearrange("p (b t) -> p b t", b=2)
            ta = pool.do(lambda e: e.tensor_tensor(xs.rearrange("p (b t) -> p b t", b=2), x3,
                                                   ysT[:, 2 * c:2 * c + 2].unsqueeze(2).broadcast_to([128, 2, 128]), ALU.mult),
                         LX[c // 4], t_ys, xs_r[0])
            xs_tok[c] = ta

        def proj_u(c):
            i = c % 2
            ta = xs_tok[c]
            bank, k = pj()
            xs_r[0] = tb = pe.do(lambda e: e.matmul(bank[:, 0:256], w("w0"), xs, start=True, stop=True), ta, pj_free[k], LQ)
            pj_free[k] = tu = dve.do(lambda e: e.tensor_tensor(uf.rearrange("p (b t) -> p b t", b=2),
                                                               bank[:, 0:256].rearrange("p (b t) -> p b t", b=2),
                                                               dT[:, 2 * c:2 * c + 2].unsqueeze(2).broadcast_to([128, 2, 128]), ALU.mult),
                                     tb, t_d, uf_r[0])
            th = act.do(lambda e: e.activation(UH[i], uf, ACTF.Copy), tu, u_readers.get(c - 2))
            uf_r[0] = tl = dve.do(lambda e: e.tensor_tensor(UL[i], uf, UH[i], ALU.subtract), th, u_readers.get(c - 2))
            tok_u[c] = [th, tl]

        def proj_v(u):
            c, g, b = units[u]
            i = c % 2
            bank, k = pj()
            sl, bl = slice(g * 512, (g + 1) * 512), slice(b * 128, (b + 1) * 128)
            u_readers[c] = tp = pair3(bank[:, :], UH[i][:, bl], UL[i][:, bl], BH[:, sl], BL[:, sl], [tok_u[c], t_B, pj_free[k]])
            pj_free[k] = tok_v[u] = act.do(lambda e: e.activation(VP[u % 10], bank[:, :], ACTF.Copy), tp, k_pv.get(u - 10))

        def proj_k(G, half):
            c, g = G // 4, G % 4
            i, ks = c % 2, G % 3
            bank, k = pj()
            for h in range(2):
                o = (4 * g + 2 * half + h) * 128
                tp = pair3(bank[:, h * 256:(h + 1) * 256], AH[:, o:o + 128], AL_[:, o:o + 128], UH[i], UL[i],
                           [tok_u[c], t_A, pj_free[k]], inc=h == 1)
            u_readers[c] = tp
            hs = slice(2 * half, 2 * half + 2)
            b4 = bank[:, :].rearrange("p (h b j) -> p h b j", h=2, b=2)
            th = act.do(lambda e: e.activation(KH[ks][:, hs, :, :], b4, ACTF.Copy), tp, last_s.get(G - 3))
            pj_free[k] = tl = dve.do(lambda e: e.tensor_tensor(KL[ks][:, hs, :, :], b4, KH[ks][:, hs, :, :], ALU.subtract), th, last_s.get(G - 3))
            tok_k[(G, half)] = [th, tl]

        units = [(c, g, b) for c in range(NCH) for g in range(4) for b in range(2)]
        U = len(units)
        k_max, k_exp, k_T, k_cp, k_pv, k_nrm, y_free = ({} for _ in range(7))

        def a_S(u):
            c, g, b = units[u]
            G, i = 4 * c + g, c % 2
            bank, r = PB[u % 2], u % 5
            bl = slice(b * 128, (b + 1) * 128)
            b3 = bank[:, :].rearrange("p (h j) -> p h j", h=4)
            t = pair3(b3, UH[i][:, bl], UL[i][:, bl], KH[G % 3][:, :, b, :], KL[G % 3][:, :, b, :],
                      [tok_u[c], tok_k[(G, 0)], tok_k[(G, 1)], k_max.get(u - 2)])
            last_s[G] = u_readers[c] = t
            tx = []
            for h in range(4):
                hl = slice(h * 128, (h + 1) * 128)
                k_max[(u, h)] = k_max[u] = dve.do(lambda e: e.tensor_tensor_reduce(SS[r][:, hl], bank[:, hl], w("mask"), 1.0, 3.0e38, ALU.add, ALU.min,
                                                                        mx[r][:, h:h + 1]), t, k_T.get(u - 5), LC, t_A, t_B)

        def a_E(u):
            r = u % 5
            for h in range(4):
                hl = slice(h * 128, (h + 1) * 128)
                k_exp[u] = act.do(lambda e: e.activation(SS[r][:, hl], SS[r][:, hl], ACTF.Exp, bias=mx[r][:, h:h + 1], scale=-1.0,
                                                         accum_out=rc[r][:, h:h + 1]), k_max[(u, h)], k_nrm.get(u - 5))

        def a_N(u):
            r = u % 5
            s3 = SS[r].rearrange("p (h j) -> p h j", h=4)
            t = dve.do(lambda e: e.reciprocal(rc[r], rc[r]), k_exp[u])
            k_nrm[u] = pool.do(lambda e: e.tensor_tensor(s3, s3, rc[r].unsqueeze(2).broadcast_to([128, 4, 128]), ALU.mult), t)

        def a_T(u):
            bank, r = PB[4], u % 5
            for h in range(4):
                t = pe.do(lambda e: e.transpose(bank[:, h * 128:(h + 1) * 128], SS[r][:, h * 128:(h + 1) * 128], ident),
                          k_nrm[u], k_cp.get(u - 1), LC, inc=h == 3)
            k_T[u] = t
            k_cp[u] = act.do(lambda e: e.activation(PT[u % 2], bank[:, :], ACTF.Copy), t, k_pv.get(u - 2))

        def a_PV(u):
            c, g, b = units[u]
            for h in range(4):
                hl = slice(h * 128, (h + 1) * 128)
                t = pe.do(lambda e: e.matmul(PB[2 + b][:, 0:128], VP[u % 10][:, hl], PT[u % 2][:, hl], start=(g, h) == (0, 0), stop=(g, h) == (3, 3)),
                          k_cp[u], tok_v[u], y_free.get((c - 1, b)), inc=h == 3)
            k_pv[u] = t
            if g == 3:
                q = slice((2 * c + b) * 128, (2 * c + b + 1) * 128)
                y_free[(c, b)] = dve.do(lambda e: e.tensor_tensor(XF[:, q], PB[2 + b][:, 0:128], XF[:, q], ALU.add), t, xs_tok[c])
                tok_x[c] = [y_free.get((c, 0)), y_free.get((c, 1))]

        s2r = [None]
        gctx, t_gc = sm(32), []

        def gated(c):
            def project(wn):
                bank, k = pj()
                return bank, k, pe.do(lambda e: e.matmul(bank[:, :], w(wn), cs(XF, c), start=True, stop=True),
                                      tok_x[2 * c], tok_x[2 * c + 1], LW, pj_free[k])

            bank, k, tp = project("wfT")
            pj_free[k] = t = act.do(lambda e: e.activation(FG, bank[:, :], ACTF.Exp, bias=nbf, scale=-1.0), tp, t_nb, s2r[0])
            yield
            bank, k, tp = project("wiT")
            pj_free[k] = ti = act.do(lambda e: e.activation(IG, bank[:, :], ACTF.Exp, bias=nbi, scale=-1.0), tp, t_nb, s2r[0])
            yield
            bank, k, tp = project("whT")
            pj_free[k] = tc = dve.do(lambda e: e.tensor_scalar(cs(HF, c), bank[:, :], w("bh"), None, ALU.add), tp)
            yield
            tA = dve.do(lambda e: e.tensor_scalar(FG, FG, 1e22, 1.0, ALU.min, ALU.add), t)
            tB = dve.do(lambda e: e.tensor_scalar(IG, IG, 1e22, 1.0, ALU.min, ALU.add), ti)
            t = dve.do(lambda e: e.scalar_tensor_tensor(SM, FG, 1e-8, IG, ALU.mult, ALU.mult), tA, tB, s2r[0])
            yield
            t = pool.do(lambda e: e.tensor_tensor(SM, SM, FG, ALU.add), t)
            t = pool.do(lambda e: e.tensor_tensor(SM, SM, IG, ALU.add), t)
            yield
            tr = []
            for b in range(4):
                bl = slice(b * 128, (b + 1) * 128)
                tr.append(dve.do(lambda e: e.reciprocal(SM[:, bl], SM[:, bl]), t))
                yield
            tf = pool.do(lambda e: e.tensor_tensor(IG, IG, SM, ALU.mult), tr)
            ti = pool.do(lambda e: e.tensor_tensor(FG, FG, SM, ALU.mult), tr)
            yield
            tn = pool.do(lambda e: e.tensor_tensor(SM, cs(HF, c), FG, ALU.mult), tc, ti, tf)
            tf = dve.do(lambda e: e.tensor_scalar(IG, IG, 1e-8, None, ALU.add), tf)
            yield
            te, td = [], []
            for b in range(4):
                q = slice(c * 512 + b * 128, c * 512 + (b + 1) * 128)
                bl = slice(b * 128, (b + 1) * 128)
                td.append(dve.do(lambda e: e.tensor_tensor_scan(FG[:, bl][:, ::-1], IG[:, bl][:, ::-1], ones, 1.0, ALU.mult, ALU.mult), tf, tn, t_ones))
            tn = pool.do(lambda e: e.tensor_tensor(SM, SM, FG, ALU.mult), td, tn)
            yield
            for b in range(4):
                q = slice(c * 512 + b * 128, c * 512 + (b + 1) * 128)
                bl = slice(b * 128, (b + 1) * 128)
                te.append(dve.do(lambda e: e.tensor_tensor_scan(HF[:, q], IG[:, bl], ones, 1.0, ALU.mult, ALU.mult), tf, tn))
            yield
            for b in range(4):
                bl = slice(b * 128, (b + 1) * 128)
                t = dve.do(lambda e: e.tensor_tensor_scan(FG[:, bl], ones, SM[:, bl], 0.0, ALU.mult, ALU.add), tn)
            yield
            for b in range(4):
                q = slice(c * 512 + b * 128, c * 512 + (b + 1) * 128)
                bl = slice(b * 128, (b + 1) * 128)
                s2r[0] = dve.do(lambda e: e.scalar_tensor_tensor(HF[:, q], HF[:, q], w("condT", 128, 4 * c + b, 4 * c + b + 1), FG[:, bl],
                                                                 ALU.mult, ALU.add), t, te)
            t_gc.append(dve.do(lambda e: e.tensor_reduce(gctx[:, 4 * c:4 * c + 4], v4(cs(HF, c)), AX.X, ALU.add), s2r[0]))
            yield

        g1, g2, cB, ar07, b4h, gfT, sil = sm(32), sm(32), sm(32), sm(1), sm(1), sm(32), sm(32)
        t_cB, t_w4 = {}, []

        def context(a, b, bank_of, free):
            n = b - a
            bank, k = bank_of()
            t = pe.do(lambda e: e.matmul(bank[0:64, 0:n], w("gw1"), gctx[:, a:b], start=True, stop=True), t_gc, free[k])
            free[k] = t = act.do(lambda e: e.activation(g1[0:64, a:b], bank[0:64, 0:n], ACTF.Gelu, bias=w("gb1", 64), scale=1.0 / 128), t)
            yield
            bank, k = bank_of()
            t = pe.do(lambda e: e.matmul(bank[0:32, 0:n], w("gw2", 64), g1[0:64, a:b], start=True, stop=True), t, free[k])
            free[k] = t = act.do(lambda e: e.activation(g2[0:32, a:b], bank[0:32, 0:n], ACTF.Gelu, bias=w("gb2", 32)), t)
            yield
            bank, k = bank_of()
            t = pe.do(lambda e: e.matmul(bank[:, 0:n], w("gw3", 32), g2[0:32, a:b], start=True, stop=True), t, free[k])
            free[k] = t = act.do(lambda e: e.activation(gfT[:, a:b], bank[:, 0:n], ACTF.Tanh, bias=b4h, scale=0.5), t, th)
            t = dve.do(lambda e: e.tensor_scalar(cB[:, a:b], gfT[:, a:b], ar07, 0.1, ALU.mult, ALU.add), t, t7)
            for p in range(a // 8, b // 8):
                t_cB[p] = t
            if a == 0:
                t = act.do(lambda e: e.activation(sil, w("condT"), ACTF.Tanh, scale=0.5))
                t = dve.do(lambda e: e.tensor_scalar(sil, sil, 0.5, 0.5, ALU.mult, ALU.add), t)
                t_w4.append(dve.do(lambda e: e.tensor_tensor(sil, sil, w("condT"), ALU.mult), t))
            yield

        scaled(0)
        proj_u(0)
        products("wvT", "wout", 1.0, BH, BL, LV, t_B)
        scaled(1)
        for n in range(3):
            proj_k(n // 2, n % 2)
        k_max[-2], k_max[-1] = pb_w[0:2], pb_w[0:2]
        y_free[(-1, 0)], y_free[(-1, 1)] = pb_w[2], pb_w[3]
        for u in range(4):
            proj_v(u)
        t = dve.do(lambda e: e.tensor_scalar(nbf, w("bf"), -1.0, None, ALU.mult), LW)
        t_nb = dve.do(lambda e: e.tensor_scalar(nbi, w("bi"), -1.0, None, ALU.mult), LW)
        th = dve.do(lambda e: e.tensor_scalar(b4h, w("gb3"), 0.5, None, ALU.mult))
        t7 = dve.do(lambda e: e.tensor_scalar(ar07, w("ar"), 0.7, None, ALU.mult))
        rec, gates24 = iter(()), context(0, 24, pj, pj_free)
        for s in range(U + 4):
            c, j = s // 8, s % 8
            if s < U:
                a_S(s)
            if 0 <= s - 1 < U:
                a_N(s - 1)
            if 0 <= s - 3 < U:
                a_T(s - 3)
            if s + 3 < U:
                proj_k((s + 3) // 2, (s + 3) % 2)
            if s < U:
                a_E(s)
            if j == 0 and c + 1 < NCH:
                proj_u(c + 1)
            if j == 5 and c + 2 < NCH:
                scaled(c + 2)
            if s + 4 < U:
                proj_v(s + 4)
            if 0 <= s - 4 < U:
                a_PV(s - 4)
            if j == 4 and s >= 20 and (c - 1) % 2 == 1:
                for _ in rec:
                    pass
                rec = gated((c - 1) // 2)
            if s < U + 3:
                next(rec, None)
            if s > U:
                next(gates24, None)
        for _ in rec:
            pass
        rec = gated(7)

        barrier("s3", 4096, 18432)
        later = ExitStack()
        ctx.callback(later.close)
        HR = later.enter_context(nc.sbuf_tensor("HR", [128, 4096], F32, side="right"))
        EH1, EL1, EH2, EL2 = rr(2048), rr(2048), rr(2048), rr(2048)
        SH1, SL1, SH2, SL2 = rr(512), rr(512), rr(512), rr(512)
        XH, XL = [rr(512) for _ in range(3)], [rr(512) for _ in range(3)]
        HH = [rr(512) for _ in range(5)]
        HL = [rr(512) for _ in range(5)]
        ar03, b4h2 = sm(1), sm(1)
        th2 = dve.do(lambda e: e.tensor_scalar(b4h2, w("cb4"), 0.5, None, ALU.mult))
        t3_ = dve.do(lambda e: e.tensor_scalar(ar03, w("ar"), 0.3, None, ALU.mult))
        H1 = [ar(1024) for _ in range(4)]
        H2 = [HR[:, i * 512:(i + 1) * 512] for i in range(4)]
        H3 = [HR[:, i * 512:(i + 1) * 512] for i in range(4, 8)]
        hs, ws, psm, agg = sm(32), sm(32), sm(32), sm(96)
        fr = [pj_free.get(k) for k in range(8)]
        bk = [0]

        def nb():
            k = bk[0] % 8
            bk[0] += 1
            return k

        def nbp():
            k = nb()
            return PB[k], k

        left, fin, t_agg = [12], {}, []
        tx2 = {}

        def split(hi, lo, src):
            t = act.do(lambda e: e.activation(hi, src, ACTF.Copy))
            return [t, pool.do(lambda e: e.tensor_tensor(lo, src, hi, ALU.subtract), t)]

        def couple(p):
            S, Tw = cs(HF, p, 1024), cs(XT, p, 1024)
            upS, upT, r1 = [None, None], [None, None], None
            for y in range(3):
                tg = []
                for s in range(2):
                    k = nb()
                    tp = pe.do(lambda e: e.matmul(PB[k][:, :], w("cw1"), cs(S, s), start=True, stop=True), upS[s], fr[k])
                    fr[k] = t = act.do(lambda e: e.activation(cs(H1[p], s), PB[k][:, :], ACTF.Gelu, bias=w("cb1")), tp, upS[s])
                    tg.append(t)
                    if y == 0:
                        k = nb()
                        tp = pe.do(lambda e: e.matmul(PB[k][:, :], w("twist"), cs(S, s), start=True, stop=True), fr[k])
                        fr[k] = upT[s] = act.do(lambda e: e.activation(cs(Tw, s), PB[k][:, :], ACTF.Copy), tp)
                yield
                k = nb()
                for s in range(2):
                    tp = pe.do(lambda e: e.matmul(PB[k][64 * s:64 * s + 64, :], w("cw2"), cs(H1[p], s), start=True, stop=True), tg[s], fr[k], inc=s == 1)
                fr[k] = t = act.do(lambda e: e.activation(H2[p], PB[k][:, :], ACTF.Gelu, bias=w("cb2")), tp, upS)
                yield
                k = nb()
                tp = pe.do(lambda e: e.matmul(PB[k][0:64, :], w("cw3"), H2[p], start=True, stop=True), t, fr[k])
                fr[k] = t3 = act.do(lambda e: e.activation(H3[p][0:64, :], PB[k][0:64, :], ACTF.Gelu, bias=w("cb3", 64)), tp, upS)
                yield
                tt = []
                for s in range(2):
                    k = nb()
                    t4 = pe.do(lambda e: e.matmul(PB[k][:, :], w("cw4", 64, 128 * s, 128 * s + 128), H3[p][0:64, :], start=True, stop=True), t3, fr[k])
                    fr[k] = t = act.do(lambda e: e.activation(cs(H1[p], s), PB[k][:, :], ACTF.Tanh, bias=b4h2, scale=0.5), t4, th2)
                    tt.append(t)
                left[0] -= 1
                yield
                while p not in t_cB:
                    yield
                tu = []
                for s in range(2):
                    c = 2 * p + s
                    cp = cs(H1[p], s)
                    u = (H2, H3)[s][p]
                    t = dve.do(lambda e: e.scalar_tensor_tensor(
                        v4(cp), v4(cp), ar03, cB[:, 4 * c:4 * c + 4].unsqueeze(2).broadcast_to([128, 4, 128]), ALU.mult, ALU.add),
                        tt[s], t_cB[p], t3_)
                    t = dve.do(lambda e: e.tensor_tensor(u, cp, cs(Tw, s), ALU.mult), t, upT[s], t4)
                    if y < 2:
                        tw = dve.do(lambda e: e.tensor_tensor(cp, cp, cs(S, s), ALU.mult), t, upS[s])
                        upT[s] = pool.do(lambda e: e.tensor_tensor(cs(Tw, s), cs(Tw, s), cp, ALU.subtract), tw)
                        upS[s] = [upT[s], dve.do(lambda e: e.tensor_tensor(cs(S, s), cs(S, s), u, ALU.add), t, tw)]
                    else:
                        upS[s] = tx2[c] = dve.do(lambda e: e.tensor_tensor(cs(XF, c), cs(XF, c), u, ALU.add), t, tx[s])
                yield
                if y == 1:
                    tx = [pool.do(lambda e: e.tensor_tensor(cs(XF, 2 * p + s), cs(XF, 2 * p + s), cs(S, s), ALU.add), upS[s]) for s in range(2)]
            fin[p] = upS
            for s in range(2):
                c = 2 * p + s
                xb = v4(cs(XF, c))
                for dst, a, b in ((hs, 0, 42), (ws, 42, 84), (psm, 84, 128)):
                    t_ag = dve.do(lambda e: e.tensor_reduce(dst[:, 4 * c:4 * c + 4], xb[:, :, a:b], AX.X, ALU.add), tx2[c])
                t_agg.append(t_ag)
                yield

        R = 32
        aeT, hT, mhalf = sm(32), sm(32), sm(4)
        dg, t_hid = sm(128), []
        t_half = pool.do(lambda e: e.memset(mhalf, -0.5))

        def adapt():
            ae = dg
            st6, mv6, r6 = sm(6), sm(2), sm(1)
            t = dve.do(lambda e: e.bn_stats(st6[0:R, :], w("cond", R)), LW)
            t = dve.do(lambda e: e.bn_aggr(mv6[0:R, :], st6[0:R, :]), t)
            t = pool.do(lambda e: e.tensor_scalar(r6[0:R, :], mv6[0:R, 1:2], 1e-5, None, ALU.add), t)
            t = pool.do(lambda e: e.tensor_tensor(r6[0:R, :], r6[0:R, :], mhalf[0:R, 0:1], ALU.pow), t, t_half)
            yield
            t = dve.do(lambda e: e.tensor_scalar(ae[0:R, :], w("cond", R), mv6[0:R, 0:1], r6[0:R, :], ALU.subtract, ALU.mult), t)
            t = dve.do(lambda e: e.tensor_tensor(ae[0:R, :], ae[0:R, :], w("lng", R), ALU.mult), t)
            t = dve.do(lambda e: e.tensor_tensor(ae[0:R, :], ae[0:R, :], w("lnb", R), ALU.add), t)
            yield
            k = nb()
            t = pe.do(lambda e: e.transpose(PB[k][:, 0:32], ae[0:R, :], ident[0:R, 0:R]), t, fr[k])
            fr[k] = t = dve.do(lambda e: e.tensor_copy(aeT, PB[k][:, 0:32]), t)
            yield
            k = nb()
            t = pe.do(lambda e: e.matmul(PB[k][:, 0:32], w("lw1"), aeT, start=True, stop=True), t, fr[k])
            fr[k] = t = act.do(lambda e: e.activation(hT, PB[k][:, 0:32], ACTF.Gelu, bias=w("lb1")), t)
            t_hid.append(t)
            yield

        splits = [(EH1, EL1, w("ew1"), k) for k in range(4)] + [(EH2, EL2, w("ew2"), k) for k in range(4)] + \
                 [(SH1, SL1, w("sw1"), 0), (SH2, SL2, w("sw2"), 0)]
        t_ws = []
        for _ in range(3):
            next(rec)
        for k in range(5, 8):
            fr[k] = pj_free[k]
        G4 = [cs(H1[p], s) for p in range(2) for s in range(2)]
        YT = [cs(H1[2], s) for s in range(2)]
        sc, tmod, lg, wbc = sm(4), sm(8), sm(4), sm(128)
        t_w = [None]

        def gates():
            ta = dve.do(lambda e: e.tensor_tensor(agg[:, 32:64], hs, psm, ALU.add), t_agg)
            tb2 = dve.do(lambda e: e.tensor_tensor(agg[:, 64:96], ws, psm, ALU.add), t_agg)
            tcx = dve.do(lambda e: e.tensor_tensor(agg[:, 0:32], agg[:, 32:64], ws, ALU.add), ta)
            t = dve.do(lambda e: e.tensor_scalar(agg[:, 0:32], agg[:, 0:32], 1.0 / 128, None, ALU.mult), tcx)
            t = dve.do(lambda e: e.tensor_scalar(agg[:, 32:96], agg[:, 32:96], 1.0 / 86, None, ALU.mult), t, tb2)
            yield
            p = 6
            for j in range(3):
                tg = pe.do(lambda e: e.matmul(PB[p][0:32, 0:4], agg[:, 32 * j:32 * j + 32], w("gatew", 128, 4 * j, 4 * j + 4),
                                              start=j == 0, stop=j == 2), t, pbf[p], inc=j == 2)
            p = 7
            tm = pe.do(lambda e: e.matmul(PB[p][0:32, 0:8], sil, w("timew"), start=True, stop=True), pbf[p], t_w4)
            pbf[7] = t = dve.do(lambda e: e.tensor_tensor(tmod[0:R, :], PB[7][0:R, 0:8], w("timeb", R), ALU.add), tm)
            t1 = dve.do(lambda e: e.tensor_scalar(tmod[0:R, 0:4], tmod[0:R, 0:4], 1.0, None, ALU.add), t)
            pbf[6] = t = dve.do(lambda e: e.tensor_tensor(lg[0:R, :], PB[6][0:R, 0:4], w("gateb", R), ALU.add), tg)
            t = dve.do(lambda e: e.tensor_tensor(lg[0:R, :], lg[0:R, :], tmod[0:R, 0:4], ALU.mult), t, t1)
            t = dve.do(lambda e: e.tensor_tensor(lg[0:R, :], lg[0:R, :], tmod[0:R, 4:8], ALU.add), t)
            yield
            s1 = sm(1)
            t = dve.do(lambda e: e.tensor_reduce(s1[0:R, :], lg[0:R, :], AX.X, ALU.max), t)
            t = dve.do(lambda e: e.tensor_scalar(lg[0:R, :], lg[0:R, :], s1[0:R, :], None, ALU.subtract), t)
            yield
            t = act.do(lambda e: e.activation(sc[0:R, :], lg[0:R, :], ACTF.Exp), t)
            t = dve.do(lambda e: e.tensor_reduce(s1[0:R, :], sc[0:R, :], AX.X, ALU.add), t)
            t = dve.do(lambda e: e.reciprocal(s1[0:R, :], s1[0:R, :]), t)
            t = dve.do(lambda e: e.tensor_scalar(sc[0:R, :], sc[0:R, :], s1[0:R, :], None, ALU.mult), t)
            yield
            cmp1, cmp2, rank = sm(16), sm(16), sm(4)
            sA = sc[0:R, :].unsqueeze(1).broadcast_to([R, 4, 4])
            sB = sc[0:R, :].unsqueeze(2).broadcast_to([R, 4, 4])
            c1 = cmp1[0:R, :].rearrange("p (a b) -> p a b", a=4)
            c2 = cmp2[0:R, :].rearrange("p (a b) -> p a b", a=4)
            ta = dve.do(lambda e: e.tensor_tensor(c1, sA, sB, ALU.is_gt), t)
            tb = dve.do(lambda e: e.tensor_tensor(c2, sA, sB, ALU.is_equal), t)
            tb = dve.do(lambda e: e.tensor_tensor(cmp2[0:R, :], cmp2[0:R, :], w("lower", R), ALU.mult), tb)
            t = dve.do(lambda e: e.tensor_tensor(cmp1[0:R, :], cmp1[0:R, :], cmp2[0:R, :], ALU.add), ta, tb)
            t = dve.do(lambda e: e.tensor_reduce(rank[0:R, :], c1, AX.X, ALU.add), t)
            t = dve.do(lambda e: e.tensor_scalar(rank[0:R, :], rank[0:R, :], 1.5, None, ALU.is_lt), t)
            yield
            t = dve.do(lambda e: e.tensor_tensor(sc[0:R, :], sc[0:R, :], rank[0:R, :], ALU.mult), t)
            t = dve.do(lambda e: e.tensor_reduce(s1[0:R, :], sc[0:R, :], AX.X, ALU.add), t)
            t = dve.do(lambda e: e.tensor_scalar(s1[0:R, :], s1[0:R, :], 1e-8, None, ALU.add), t)
            t = dve.do(lambda e: e.reciprocal(s1[0:R, :], s1[0:R, :]), t)
            t = dve.do(lambda e: e.tensor_scalar(sc[0:R, :], sc[0:R, :], s1[0:R, :], None, ALU.mult), t)
            t = dve.do(lambda e: e.tensor_tensor(dg[0:R, :].rearrange("p (a b) -> p a b", a=4),
                                                 ident[0:R, 0:32].unsqueeze(1).broadcast_to([R, 4, 32]),
                                                 sc[0:R, :].unsqueeze(2).broadcast_to([R, 4, 32]), ALU.mult), t)
            yield
            p = 6
            t = pe.do(lambda e: e.matmul(PB[p][:, 0:128], ones[0:R, :], dg[0:R, :], start=True, stop=True), t, pbf[p])
            pbf[p] = t_w[0] = dve.do(lambda e: e.tensor_copy(wbc, PB[p][:, 0:128]), t)
            yield

        def tokens(ap, x):
            if x == 1:
                return bass.AP(tensor=ap.tensor, offset=ap.offset, ap=[list(ap.ap[0]), [128, 4], [84, 2], [1, 44]])
            return v4(ap)[:, :, 42:128] if x == 2 else ap

        LEN = {0: 512, 1: 352, 2: 344, 3: 512, 4: 512}
        tok_x, x_r = {}, {}
        r_hb, r_g, r_yt = [None] * 5, [None] * 4, [None] * 2
        pbf = fr
        acc = {}
        gn, dn = [0], [0]

        def part(c):
            i = c % 3
            t = act.do(lambda e: e.activation(XH[i], cs(XF, c), ACTF.Copy), tx2[c], x_r.get(c - 3))
            tok_x[c] = [t, dve.do(lambda e: e.tensor_tensor(XL[i], cs(XF, c), XH[i], ALU.subtract), t, x_r.get(c - 3))]

        def up(c, x, k):
            n = LEN[x]
            o = x * 512 + k * 128 if x < 4 else k * 128
            wh, wl = (EH1, EL1) if x < 4 else (SH1, SL1)
            b1 = w("eb1", 128, x * 4 + k, x * 4 + k + 1) if x < 4 else w("sb1", 128, k, k + 1)
            bank = PB[k][:, 0:n]
            x_r[c] = tp = pair3(bank, wh[:, o:o + 128], wl[:, o:o + 128], tokens(XH[c % 3], x), tokens(XL[c % 3], x),
                                [tok_x[c], t_ws, pbf[k]])
            g, i = gn[0] % 4, gn[0] % 5
            gn[0] += 1
            pbf[k] = t = act.do(lambda e: e.activation(G4[g][:, 0:n], bank, ACTF.Gelu_apprx_tanh, bias=b1), tp, r_g[g])
            first = gn[0] <= 16
            if first:
                th_ = act.do(lambda e: e.activation(HH[i][:, 0:n], G4[g][:, 0:n], ACTF.Copy), t, r_hb[i])
            else:
                th_ = dve.do(lambda e: e.tensor_copy(HH[i][:, 0:n], G4[g][:, 0:n]), t, r_hb[i])
            r_g[g] = tl = (pool if k == 2 or first and k == 0 else dve).do(
                lambda e: e.tensor_tensor(HL[i][:, 0:n], G4[g][:, 0:n], HH[i][:, 0:n], ALU.subtract), th_, r_hb[i])
            return i, [th_, tl]

        def down(c, x, k, i, toks):
            n = LEN[x]
            o = x * 512 + k * 128 if x < 4 else k * 128
            wh, wl = (EH2[:, o:o + 128], EL2[:, o:o + 128]) if x < 4 else (SH2[:, o:o + 128], SL2[:, o:o + 128])
            if k == 0:
                dn[0] += 1
            j = dn[0] % 2
            p = 4 + j
            bank = PB[p][:, 0:n]
            pe.do(lambda e: e.matmul(bank, wh, HH[i][:, 0:n], start=k == 0, stop=False), toks, t_ws, pbf[p], inc=False)
            pe.do(lambda e: e.matmul(bank, wl, HH[i][:, 0:n], start=False, stop=False), inc=False)
            r_hb[i] = tp = pe.do(lambda e: e.matmul(bank, wh, HL[i][:, 0:n], start=False, stop=k == 3))
            if k < 3:
                return
            if x == 4:
                pbf[p] = acc[c] = dve.do(lambda e: e.tensor_scalar(cs(HF, c), bank, w("sb2"), None, ALU.add), tp)
                return
            L = n // 4
            b3 = bank.rearrange("p (b t) -> p b t", b=4)
            y3 = YT[j][:, 0:n].rearrange("p (b t) -> p b t", b=4)
            h3 = v4(cs(HF, c))
            pbf[p] = ty = dve.do(lambda e: e.scalar_tensor_tensor(
                y3, b3, w("eb2", 128, x, x + 1), wbc[:, x * 32 + 4 * c:x * 32 + 4 * c + 4].unsqueeze(2).broadcast_to([128, 4, L]),
                ALU.add, ALU.mult), tp, t_w[0], r_yt[j])
            for a, b, o in {1: ((0, 42, 0), (84, 128, 44)), 2: ((42, 128, 0),)}.get(x, ((0, 128, 0),)):
                t = pool.do(lambda e: e.tensor_tensor(h3[:, :, a:b], h3[:, :, a:b], y3[:, :, o:o + b - a], ALU.add), ty, acc[c])
            r_yt[j] = acc[c] = t

        s_q = [new_sem(f"s_q{i}") for i in range(2)]
        s_k = [new_sem(f"s_k{i}") for i in range(2)]
        sp = Queue(nc.sync, new_sem, "sp")
        nisq8 = float(-1.0 / np.sqrt(8))
        tok_q, tok_k, last_s, last_ks = {}, {}, {}, {}
        r_parts = {}
        QS, KR = [None, None], [None, None]

        def spread(hi, lo, order, dst, s, toks, c):
            sp.wait([toks])
            for g in range(4):
                for rep in range(3):
                    src = (hi, lo)[order[rep]]
                    nc.sync.dma_start(dst[32 * rep:32 * rep + 32, g * 512:(g + 1) * 512].bitcast(F32), src[32 * g:32 * g + 32, :].bitcast(F32)).then_inc(s, 16)
            return (s, 16 * 12 * (c // 2 + 1))

        def queries(c, bank_of, free, QT, QH, QL, *toks):
            bank, k = bank_of()
            tp = pe.do(lambda e: e.matmul(bank[:, :], w("aq"), cs(HF, c), start=True, stop=True), free[k], *toks)
            free[k] = t = act.do(lambda e: e.activation(QT, bank[:, :], ACTF.Relu, bias=w("bq")), tp, r_parts.get("QT"))
            yield
            th = dve.do(lambda e: e.tensor_scalar(QH, QT, nisq8, None, ALU.mult), t, r_parts.get("q"))
            r_parts["QT"] = tl = dve.do(lambda e: e.scalar_tensor_tensor(QL, QT, nisq8, QH, ALU.mult, ALU.subtract), th, r_parts.get("q"))
            r_parts["q"] = tok_q[c] = spread(QH, QL, (0, 0, 1), QS[c % 2], s_q[c % 2], [th, tl, last_s.get(c - 2)], c)
            yield

        def keys(c, bank_of, free, KT, KMB, KH, KL, *toks):
            bank, k = bank_of()
            tp = pe.do(lambda e: e.matmul(bank[:, :], ones, cs(HF, c), start=True, stop=True), free[k], *toks)
            free[k] = tm = dve.do(lambda e: e.tensor_scalar(KMB, bank[:, :], 0.0, None, ALU.not_equal), tp, r_parts.get("KMB"))
            bank, k = bank_of()
            tp = pe.do(lambda e: e.matmul(bank[:, :], w("ak"), cs(HF, c), start=True, stop=True), free[k])
            free[k] = t = act.do(lambda e: e.activation(KT, bank[:, :], ACTF.Relu, bias=w("bk")), tp, r_parts.get("KT"))
            yield
            r_parts["KMB"] = t = dve.do(lambda e: e.tensor_tensor(KT, KT, KMB, ALU.mult), t, tm)
            th = dve.do(lambda e: e.tensor_copy(KH, KT), t, r_parts.get("k"))
            yield
            r_parts["KT"] = tl = dve.do(lambda e: e.tensor_tensor(KL, KT, KH, ALU.subtract), th, r_parts.get("k"))
            r_parts["k"] = tok_k[c] = spread(KH, KL, (0, 1, 0), KR[c % 2], s_k[c % 2], [th, tl, last_ks.get(c - 2)], c)
            yield

        ahead = [0]

        def bank67():
            k = 6 + ahead[0] % 2
            ahead[0] += 1
            return PB[k], k

        def ahead_of_attention():
            later.close()
            QS[0] = later.enter_context(nc.sbuf_tensor("QS0", [128, 2048], F32R, side="right"))
            KR[0] = later.enter_context(nc.sbuf_tensor("KR0", [128, 2048], F32R, side="right"))
            raw = [w("ew1", 128, i * 512, (i + 1) * 512) for i in range(3)]
            yield from queries(0, bank67, pbf, raw[0], XH[2], XL[2], acc[0], x_r[5], t_ws, [fin[p] for p in range(4)])
            while 7 not in x_r:
                yield
            yield from keys(0, bank67, pbf, raw[1], raw[2], XH[0], XL[0], x_r[6])

        jobs = [(0, 4), (1, 4), (2, 4)] + [(c, x) for c in range(2) for x in range(4)] + [(c, x) for c in range(2, CH) for x in ((4, 0, 1, 2, 3) if c > 2 else range(4))]
        def experts():
            part(0)
            part(1)
            yield
            r_hb[:] = [s2r[0]] * 5
            r_g[:] = [fin[0], fin[0], fin[1], fin[1]]
            r_yt[:] = [fin[2], fin[2]]
            prev, gt = None, gates()
            for n, (c, x) in enumerate(jobs + [(0, 0)]):
                if n == 1:
                    part(2)
                if 2 <= c < CH - 1 and x == 2 and n < len(jobs):
                    part(c + 1)
                if n == 3:
                    while len(t_agg) < 8:
                        yield
                if (c, x) == (6, 4):
                    qk = ahead_of_attention()
                cur = []
                for k in range(4):
                    if k % 2 == 1 and c >= 6:
                        next(qk, None)
                    if n < len(jobs):
                        cur.append((c, x, k) + up(c, x, k))
                    if prev:
                        down(*prev[k])
                    if len(t_agg) == 8 and k % 2 == 0:
                        next(gt, None)
                    yield
                prev = cur

        starts = [[couple(0)], [couple(1)], [couple(2)], [adapt()]]
        live = []
        moe, ran, turn = None, [], 0
        while live or starts or rec:
            if 0 in fin and left[0] <= 3 and moe is None:
                moe = experts()
                next(moe)
            if left[0] == 0 and all(p in fin for p in range(3)) and not ran:
                ran.append(1)
                for e in engines:
                    e.stage("s4")
                live.append(moe)
            if starts:
                live += starts.pop(0)
            for _ in range(4):
                if rec and next(rec, "over") == "over":
                    rec = None
                    live += [context(24, 32, nbp, fr), couple(3)]
            turn += 1
            for gnr in list(live):
                if (gnr is moe or not ran or turn % 2 == 0) and next(gnr, "over") == "over":
                    live.remove(gnr)
            for _ in range(3 if left[0] < 4 else 1):
                if splits and rec is None:
                    hi, lo, src, k = splits.pop()
                    t_ws.append(split(cs(hi, k), cs(lo, k), cs(src, k)))

        barrier("s5", 12432, 9216, [tok_q[0], tok_k[0]])
        QT, KT, KMB = ar(512), ar(512), ar(512)
        X2 = [ar(512) for _ in range(2)]
        VT = [ar(128) for _ in range(2)]
        VY = [ar(272) for _ in range(3)]
        SS = [ar(512) for _ in range(6)]
        PT = [ar(512) for _ in range(2)]
        LN = [ar(512) for _ in range(2)]
        GG = [ar(512) for _ in range(2)]
        XA = ar(256).rearrange("p (b r) -> p b r", r=8)
        XBP = [ar(128) for _ in range(2)]
        HX = ar(2048)
        QH, QL, KH, KL = rr(512), rr(512), rr(512), rr(512)
        QS[1], KR[1] = rr(2048), rr(2048)
        KS = [rr(512).rearrange("p (h j) -> p h j", h=4) for _ in range(6)]
        mx = [sm(4) for _ in range(6)]
        rc = [sm(16) for _ in range(2)]
        xsum, qm, iqm, rstd = sm(32), sm(32), sm(32), sm(32)
        mv = sm(64)
        m3 = mv.rearrange("p (q s) -> p q s", s=2)
        bns = [sm(6) for _ in range(2)]
        pj_free = {5: None, 6: None, 7: None}
        pj_n[0] = 0
        tok_v, tok_m, tok_x2 = {}, {}, {}
        last_pv, x2_r, v_r = {}, {}, {}

        def proj5(c):
            i = c % 2
            if c:
                yield from queries(c, pj, pj_free, QT, QH, QL)
                yield from keys(c, pj, pj_free, KT, KMB, KH, KL)
            bank, k = pj()
            for b in range(4):
                tp = pe.do(lambda e: e.transpose(bank[:, b * 128:(b + 1) * 128], HF[:, c * 512 + b * 128:c * 512 + (b + 1) * 128], ident),
                           pj_free[k], inc=b == 3)
            pj_free[k] = tok_x2[c] = act.do(lambda e: e.activation(X2[i], bank[:, :], ACTF.Copy), tp, x2_r.get(c - 2))
            yield
            t = dve.do(lambda e: e.tensor_reduce(xsum[:, 4 * c:4 * c + 4], v4(X2[i]), AX.X, ALU.add), tok_x2[c])
            ta = dve.do(lambda e: e.tensor_scalar(qm[:, 4 * c:4 * c + 4], xsum[:, 4 * c:4 * c + 4], 0.0, None, ALU.not_equal), t)
            tok_m[c] = dve.do(lambda e: e.tensor_scalar(iqm[:, 4 * c:4 * c + 4], qm[:, 4 * c:4 * c + 4], -1.0, 1.0, ALU.mult, ALU.add), ta)
            yield

        def projv(q):
            c = q // 4
            bank, k = pj()
            v_r[c] = tp = pe.do(lambda e: e.matmul(bank[:, 0:128], HF[:, q * 128:(q + 1) * 128], w("av"), start=True, stop=True), pj_free[k])
            pj_free[k] = t = dve.do(lambda e: e.tensor_tensor(VT[q % 2], bank[:, 0:128], w("bv"), ALU.add), tp, tok_v.get(q - 2))
            vv = VY[q % 3][:, 0:144].rearrange("p (h v) -> p h v", v=9)
            ta = dve.do(lambda e: e.tensor_scalar(vv[:, :, 0:8], VT[q % 2].rearrange("p (h v) -> p h v", v=8), 0.0,
                                                  qm[:, q:q + 1], ALU.max, ALU.mult), t, tok_m[c], ov[q % 3], last_pv.get(q - 3))
            tok_v[q] = [ta, dve.do(lambda e: e.tensor_copy(vv[:, :, 8:9], qm[:, q:q + 1].unsqueeze(1).broadcast_to([128, 16, 1])),
                                   tok_m[c], last_pv.get(q - 3))]

        units = [(q, g) for q in range(32) for g in range(4)]
        U = len(units)
        k_max, k_exp, k_T, k_cp, k_S, k_ks = ({} for _ in range(6))
        bank_free, bn_r, ln_w, ln_free = {}, {}, {}, {}

        def b_K(u):
            q, g = units[u]
            c, b = q // 4, q % 4
            last_ks[c] = k_ks[u] = pool.do(lambda e: e.tensor_tensor(
                KS[u % 6][0:96, :, :], KR[c % 2][0:96, g * 512 + b * 128:g * 512 + (b + 1) * 128].unsqueeze(1).broadcast_to([96, 4, 128]),
                w("hm", 96).unsqueeze(2).broadcast_to([96, 4, 128]), ALU.mult), tok_k[c], k_S.get(u - 6))

        def b_S(u):
            q, g = units[u]
            c, b = q // 4, q % 4
            bank, r = PB[u % 2], u % 6
            last_s[c] = k_S[u] = t = pe.do(lambda e: e.matmul(bank[:, :].rearrange("p (h j) -> p h j", h=4),
                                                              QS[c % 2][0:96, g * 512 + b * 128:g * 512 + (b + 1) * 128], KS[r][0:96, :, :],
                                                              start=True, stop=True), tok_q[c], k_ks[u], k_max.get(u - 2))
            for h in range(4):
                hl = slice(h * 128, (h + 1) * 128)
                k_max[(u, h)] = k_max[u] = dve.do(lambda e: e.tensor_tensor_reduce(SS[r][:, hl], bank[:, hl], w("mask"), 1.0, 3.0e38, ALU.add, ALU.min,
                                                                                   mx[r][:, h:h + 1]), t, k_T.get(u - 6))

        def b_E(u):
            r = u % 6
            for h in range(4):
                hl = slice(h * 128, (h + 1) * 128)
                k_exp[u] = act.do(lambda e: e.activation(SS[r][:, hl], SS[r][:, hl], ACTF.Exp, bias=mx[r][:, h:h + 1], scale=-1.0), k_max[(u, h)])

        k_pv = {}

        def b_T(u):
            bank, r = PB[4], u % 6
            for h in range(4):
                t = pe.do(lambda e: e.transpose(bank[:, h * 128:(h + 1) * 128], SS[r][:, h * 128:(h + 1) * 128], ident),
                          k_exp[u], k_cp.get(u - 1), inc=h == 3)
            k_T[u] = t
            k_cp[u] = act.do(lambda e: e.activation(PT[u % 2], bank[:, :], ACTF.Copy), t, k_pv.get(u - 2))

        def b_PV(u):
            q, g = units[u]
            c, b = q // 4, q % 4
            bank = PB[2 + q % 2]
            for h in range(4):
                o = 9 * (4 * g + h)
                t = pe.do(lambda e: e.matmul(bank[:, o:o + 96], PT[u % 2][:, h * 128:(h + 1) * 128], VY[q % 3][:, o:o + 96], start=True, stop=True),
                          k_cp[u], tok_v[q], ov[q % 3], bank_free.get(q - 2), inc=h == 3)
            k_pv[u] = t
            last_pv[q] = t

        def b_N(q):
            c, b = q // 4, q % 4
            o3 = PB[2 + q % 2][:, 0:144].rearrange("p (h v) -> p h v", h=16)
            r = rc[q % 2]
            sl = cs(LN[c % 2], b, 128)
            t = dve.do(lambda e: e.tensor_scalar(r.unsqueeze(2), o3[:, :, 8:9], iqm[:, q:q + 1], None, ALU.add), last_pv[q], tok_m[c])
            t = dve.do(lambda e: e.reciprocal(r, r), t)
            t = dve.do(lambda e: e.tensor_scalar(r, r, qm[:, q:q + 1], None, ALU.mult), t)
            bank_free[q] = t = dve.do(lambda e: e.tensor_tensor(sl.rearrange("p (h v) -> p h v", h=16), o3[:, :, 0:8],
                                                                r.unsqueeze(2).broadcast_to([128, 16, 8]), ALU.mult), t, ln_free.get(c - 2))
            x2_r[c] = t = dve.do(lambda e: e.tensor_tensor(sl, sl, cs(X2[c % 2], b, 128), ALU.add), t, tok_x2[c])
            t = dve.do(lambda e: e.bn_stats(bns[q % 2], sl), t)
            bn_r[q] = dve.do(lambda e: e.bn_aggr(mv[:, 2 * q:2 * q + 2], bns[q % 2]), t)

        hx4 = HX.rearrange("p (r b s) -> p r b s", r=8, b=32)
        t_xa, t_xb = [], []

        def spread_hidden():
            t = pool.do(lambda e: e.memset(HX, 0.0))
            for r in range(8):
                t_hx = pool.do(lambda e: e.tensor_copy(hx4[:, r, :, r:r + 1], hT.unsqueeze(2)), t, t_hid)
            return t_hid, t_hx

        def factors(t_h, t_hx):
            bank, k = pj()
            for r in range(8):
                tp = pe.do(lambda e: e.matmul(bank[:, 32 * r:32 * r + 32], w("lw2a", 128, r * 128, (r + 1) * 128), hT, start=True, stop=True),
                           t_h, pj_free[k], inc=r == 7)
            for r in range(8):
                pj_free[k] = t = dve.do(lambda e: e.tensor_scalar(XA[:, :, r:r + 1], bank[:, 32 * r:32 * r + 32].unsqueeze(2), w("lb2a", 128, r, r + 1), None, ALU.add), tp)
            t_xa.append(t)
            yield
            for hh in range(2):
                bank, k = pj()
                for r in range(8):
                    tp = pe.do(lambda e: e.matmul(bank[:, 0:128], hx4[:, r, 16 * hh:16 * hh + 16, :].rearrange("p b s -> p (b s)"),
                                                  w("lw2b", 128, r * 128, (r + 1) * 128), start=r == 0, stop=r == 7), t_hx, pj_free[k], inc=r == 7)
                pj_free[k] = t = dve.do(lambda e: e.tensor_tensor(XBP[hh], bank[:, 0:128], w("lb2b"), ALU.add), tp)
                t_xb.append(t)
                yield

        tx3, tx4, r_gg = {}, {}, {}

        def finish(c):
            q0 = 4 * c
            bn = [bn_r[q0 + b] for b in range(4)]
            t_b = pool.do(lambda e: e.tensor_tensor(cs(XF, c), cs(XF, c), w("beta").broadcast_to([128, 512]), ALU.add))
            t_r = pool.do(lambda e: e.tensor_scalar(rstd[:, q0:q0 + 4].unsqueeze(2), m3[:, q0:q0 + 4, 1:2], 1e-8, None, ALU.add), bn)
            t_r = pool.do(lambda e: e.tensor_tensor(rstd[:, q0:q0 + 4], rstd[:, q0:q0 + 4], mhalf, ALU.pow), t_r, t_half)
            yield
            for b in range(4):
                sl = cs(LN[c % 2], b, 128)
                t = dve.do(lambda e: e.tensor_scalar(sl, sl, m3[:, q0 + b, 0:1], rstd[:, q0 + b:q0 + b + 1], ALU.subtract, ALU.mult), t_r, bn)
            yield
            yield
            bank, k = pj()
            for b in range(4):
                tp = pe.do(lambda e: e.transpose(bank[:, b * 128:(b + 1) * 128], cs(LN[c % 2], b, 128), ident), t, pj_free[k], inc=b == 3)
            ln_free[c] = tp
            pj_free[k] = t = dve.do(lambda e: e.scalar_tensor_tensor(cs(XF, c), bank[:, :], w("gamma"), cs(XF, c), ALU.mult, ALU.add), tp, t_b)
            yield
            yield
            bank, k = pj()
            for b in range(4):
                tp = pe.do(lambda e: e.transpose(bank[:, b * 128:(b + 1) * 128], XF[:, (q0 + b) * 128:(q0 + b + 1) * 128], ident), t, pj_free[k], inc=b == 3)
            pj_free[k] = tx3[c] = act.do(lambda e: e.activation(cs(XT, c), bank[:, :], ACTF.Copy), tp)
            yield
            hh, i = c // 4, c % 2
            bank, k = pj()
            tp = pe.do(lambda e: e.matmul(bank[:, :], XA[:, 16 * hh:16 * hh + 16, :].rearrange("p b r -> p (b r)"), cs(XF, c), start=True, stop=True),
                       t_xa, t, pj_free[k])
            pj_free[k] = tg = dve.do(lambda e: e.tensor_tensor(v4(GG[i]), v4(bank[:, :]),
                                                               w("bm16", 128, 4 * (c % 4), 4 * (c % 4) + 4).unsqueeze(2).broadcast_to([128, 4, 128]), ALU.mult),
                                     tp, r_gg.get(c - 2))
            yield
            yield
            bank, k = pj()
            pe.do(lambda e: e.matmul(bank[:, :], w("base"), cs(XF, c), start=True, stop=False), pj_free[k], inc=False)
            r_gg[c] = tp = pe.do(lambda e: e.matmul(bank[:, :], XBP[hh], GG[i], start=False, stop=True), tg, t_xb)
            pj_free[k] = tx4[c] = dve.do(lambda e: e.tensor_tensor(cs(HF, c), cs(XF, c), bank[:, :], ALU.add), tp, v_r[c])
            yield

        for u in range(3):
            b_K(u)
        ov = [pool.do(lambda e, i=i: e.memset(VY[i], 0.0)) for i in range(3)]
        for u in range(3, 5):
            b_K(u)
        b_S(0)
        for _ in proj5(0):
            pass
        projv(0)
        fill = [factors(*spread_hidden())]
        smean, b1e = sm(1), sm(1)
        t = dve.do(lambda e: e.tensor_reduce(smean, w("slotT"), AX.X, ALU.add))
        t = dve.do(lambda e: e.tensor_scalar(smean, smean, 1.0 / 64, None, ALU.mult), t)
        bank, k = pj()
        t = pe.do(lambda e: e.matmul(bank[0:64, 0:1], w("fw1b"), smean, start=True, stop=True), t, pj_free[k])
        pj_free[k] = t_b1 = dve.do(lambda e: e.tensor_tensor(b1e[0:64, :], bank[0:64, 0:1], w("fb1", 64), ALU.add), t)
        for s in range(U + 7):
            if s < U:
                q, g = units[s]
                if s:
                    b_S(s)
            if 0 <= s - 3 < U:
                b_T(s - 3)
            if s + 5 < U:
                b_K(s + 5)
            if 0 <= s - 1 < U:
                b_E(s - 1)
            if s < U:
                if s % 16 == 1 and s // 16 < 7:
                    nxt = proj5(s // 16 + 1)
                    fill.insert(0, nxt)
                if g == 1 and q + 1 < 32:
                    if q % 4 == 3:
                        for _ in nxt:
                            pass
                    projv(q + 1)
            if 0 <= s - 4 < U:
                b_PV(s - 4)
            if s >= 8 and (s - 5) % 4 == 3 and (s - 5) // 4 < 32:
                q = (s - 5) // 4
                b_N(q)
                if q % 4 == 3:
                    fill.append(finish(q // 4))
            while fill and next(fill[0], "over") == "over":
                fill.pop(0)
        later.close()
        H1all = later.enter_context(nc.sbuf_tensor("H1", [128, 4096], F32, side="right"))
        H1 = [cs(H1all, c) for c in range(8)]
        t_h1 = pool.do(lambda e: e.memset(H1all[64:65, :], 1.0), last_s[6], pool.last())
        th1 = []

        def hidden():
            free = [k_max[U - 2], k_max[U - 1]]
            for c in range(CH):
                while c not in tx4:
                    yield
                k = c % 2
                tp = pe.do(lambda e: e.matmul(PB[k][0:64, :], w("fw1a"), cs(HF, c), start=True, stop=True), free[k], tx4[c])
                free[k] = t = act.do(lambda e: e.activation(H1[c][0:64, :], PB[k][0:64, :], ACTF.Gelu, bias=b1e[0:64, :]), tp, t_b1)
                th1.append(t)
                yield

        rest = hidden()
        for _ in range(5):
            next(rest, None)
        for f in fill:
            for _ in f:
                next(rest, None)
        for _ in rest:
            pass

        barrier("s7", 21504)
        fr = [None] * 8
        bk = [0]
        AL = ar(2048)
        ATT = ar(2048)
        XTM = ar(32 * 129).rearrange("p (q d) -> p q d", d=129)
        LG = [ar(256) for _ in range(2)]
        MR = [ar(256) for _ in range(2)]
        hn, wvo, bvo = ar(64), ar(128), ar(128)
        tiles = [[ar(512) for _ in range(5)] for _ in range(4)]
        tinv, br, bz, nq = sm(1), sm(1), sm(1), sm(1)
        m8 = [sm(32) for _ in range(2)]
        sums = [sm(4) for _ in range(2)]
        t_one = pool.do(lambda e: e.memset(XTM[:, :, 128:129], 1.0))
        t_bo = [pool.do(lambda e, c=c: e.tensor_tensor(v4(cs(XT, c)), v4(cs(XT, c)), w("bo").unsqueeze(1).broadcast_to([128, 4, 128]), ALU.add))
                for c in range(CH)]

        t = dve.do(lambda e: e.tensor_scalar(tinv, w("tau"), -1.0, None, ALU.mult))
        t = dve.do(lambda e: e.tensor_tensor(tinv, tinv, w("tau"), ALU.max), t)
        t = dve.do(lambda e: e.tensor_scalar(tinv, tinv, 0.1, None, ALU.add), t)
        t_ti = dve.do(lambda e: e.reciprocal(tinv, tinv), t)
        bih, bhh = w("bih"), w("bhh")
        t_bs = []
        for dst, g in ((br, 0), (bz, 1)):
            t = dve.do(lambda e: e.tensor_tensor(dst, bih[:, g:g + 1], bhh[:, g:g + 1], ALU.add))
            t_bs.append(dve.do(lambda e: e.tensor_scalar(dst, dst, 0.5, None, ALU.mult), t))
        sc7 = float(32.0 ** -0.5)
        t_nq = dve.do(lambda e: e.tensor_scalar(nq, w("fbq"), -sc7, None, ALU.mult))
        k = nb()
        tp = pe.do(lambda e: e.matmul(PB[k][:, 0:64], w("whhT", 128, 256, 384), w("slotT"), start=True, stop=True), fr[k])
        fr[k] = t_hn = dve.do(lambda e: e.tensor_scalar(hn, PB[k][:, 0:64], bhh[:, 2:3], 0.5, ALU.add, ALU.mult), tp)
        k = nb()
        tp = pe.do(lambda e: e.matmul(PB[k][:, 0:128], w("wvpT"), w("wo"), start=True, stop=True), fr[k], inc=False)
        tp = pe.do(lambda e: e.matmul(PB[k][:, 128:256], w("bvp").broadcast_to([128, 128]), w("wo"), start=True, stop=True))
        t_vo = act.do(lambda e: e.activation(wvo, PB[k][:, 0:128], ACTF.Copy), tp)
        fr[k] = t_bvo = dve.do(lambda e: e.tensor_copy(bvo, PB[k][:, 128:256]), tp, t_vo)

        txm, tal, tatt = {}, {}, {}
        r_lg, r_mr, r_m8 = [None, None], [None, None], [None, None]

        def b4(ap):
            return ap.rearrange("p (b s) -> p b s", b=4)

        def route(c):
            i = c % 2
            k = nb()
            for b in range(4):
                tl = pe.do(lambda e: e.matmul(PB[k][:, b * 64:(b + 1) * 64], H1[c][0:65, b * 128:(b + 1) * 128], w("fw2", 65), start=True, stop=True),
                           th1[c], t_h1, fr[k], inc=b == 3)
            lg = PB[k][:, 0:256]
            kx = nb()
            for b in range(4):
                q = 4 * c + b
                tp = pe.do(lambda e: e.transpose(PB[kx][:, b * 128:(b + 1) * 128], HF[:, q * 128:(q + 1) * 128], ident), fr[kx], inc=b == 3)
            fr[kx] = txm[c] = act.do(lambda e: e.activation(XTM[:, 4 * c:4 * c + 4, 0:128], v4(PB[kx][:, :]), ACTF.Copy), tp)
            tq = [dve.do(lambda e: e.max(m8[i][:, 8 * b:8 * b + 8], lg[:, b * 64:(b + 1) * 64]), tl, r_m8[i]) for b in range(4)]
            top = b4(m8[i])[:, :, 0:1].broadcast_to([128, 4, 64])
            t2 = dve.do(lambda e: e.tensor_tensor(b4(LG[i]), b4(lg), top, ALU.subtract), tq, r_lg[i])
            for b in range(4):
                sl = slice(b * 64, (b + 1) * 64)
                tr = dve.do(lambda e: e.match_replace(out=MR[i][:, sl], in_to_replace=m8[i][:, 8 * b:8 * b + 8], in_values=lg[:, sl], imm_value=-3.0e38),
                            tq[b], r_mr[i])
            r_m8[i] = [t2, tr]
            fr[k] = t = dve.do(lambda e: e.tensor_tensor(MR[i], MR[i], lg, ALU.not_equal), tr)
            t2 = act.do(lambda e: e.activation(LG[i], LG[i], ACTF.Exp, scale=tinv), t2, t_ti)
            yield
            for b in range(4):
                sl = slice(b * 64, (b + 1) * 64)
                o = c * 256 + b * 64
                ta = dve.do(lambda e: e.tensor_tensor_reduce(AL[:, o:o + 64], LG[i][:, sl], MR[i][:, sl], 1.0, 0.0, ALU.mult, ALU.add,
                                                             sums[i][:, b:b + 1]), t2, t)
            r_lg[i] = r_mr[i] = ta
            t = dve.do(lambda e: e.reciprocal(sums[i], sums[i]), ta)
            al = AL[:, c * 256:(c + 1) * 256]
            tal[c] = dve.do(lambda e: e.tensor_tensor(b4(al), b4(al), sums[i].unsqueeze(2).broadcast_to([128, 4, 64]), ALU.mult), t)
            yield
            k = nb()
            for p in range(2):
                tp = pe.do(lambda e: e.transpose(PB[k][:, p * 128:(p + 1) * 128], al[:, p * 128:(p + 1) * 128], ident), tal[c], fr[k], inc=p == 1)
            fr[k] = tatt[c] = act.do(lambda e: e.activation(ATT[:, c * 256:(c + 1) * 256], PB[k][:, 0:256], ACTF.Copy), tp)

        def v8(ap):
            return ap.rearrange("p (b s) -> p b s", b=8)

        sp.stage("s7")
        pm = w("pmask")

        def slots(n):
            ra, rb = route(2 * n), route(2 * n + 1)
            next(ra)
            yield
            next(rb)
            next(ra)
            yield
            next(rb)
            next(ra, None)
            yield
            next(rb, None)
            T2, T3, SN, VV, VS = tiles[n]
            SI, T1 = cs(HF, 2 * n), cs(HF, 2 * n + 1)
            hf_free = [txm[2 * n], txm[2 * n + 1], th1[2 * n], th1[2 * n + 1]]
            dn, mx7, sm7, rs7, bn7, mv7 = sm(4), sm(4), sm(4), sm(4), sm(24), sm(8)
            pairs = [slice(p * 128, (p + 1) * 128) for p in range(4)]
            ts = []
            for hf in range(2):
                k = nb()
                for p in range(2):
                    for hh in range(2):
                        q = 8 * n + 4 * hf + 2 * p + hh
                        tp = pe.do(lambda e: e.matmul(PB[k][64 * hh:64 * hh + 64, 129 * p:129 * p + 129], AL[:, q * 64:(q + 1) * 64], XTM[:, q, :],
                                                      start=True, stop=True), tal[q // 4], txm[q // 4], t_one, fr[k], inc=(p, hh) == (1, 1))
                b3 = PB[k][:, 0:258].rearrange("p (q d) -> p q d", d=129)
                d2 = dn[:, 2 * hf:2 * hf + 2]
                t = dve.do(lambda e: e.tensor_scalar(d2.unsqueeze(2), b3[:, :, 128:129], 1e-8, None, ALU.add), tp)
                t = dve.do(lambda e: e.reciprocal(d2, d2), t)
                fr[k] = t = dve.do(lambda e: e.tensor_tensor(T2[:, 256 * hf:256 * hf + 256].rearrange("p (q d) -> p q d", d=128), b3[:, :, 0:128],
                                                             d2.unsqueeze(2).broadcast_to([128, 2, 128]), ALU.mult), t)
                ts.append(t)
            yield
            k = nb()
            for p in range(4):
                tp = pe.do(lambda e: e.transpose(PB[k][:, pairs[p]], T2[:, pairs[p]], ident), ts[p // 2], fr[k], inc=p == 3)
            fr[k] = t = act.do(lambda e: e.activation(SI, PB[k][:, :], ACTF.Copy), tp, hf_free)
            yield
            tg = []
            sb_ = w("slotT").unsqueeze(1).broadcast_to([128, 8, 64])
            for g, dst, bias in ((0, T1, br), (1, T2, bz)):
                k = nb()
                pe.do(lambda e: e.matmul(PB[k][:, :], w("wihT", 128, g * 128, (g + 1) * 128), SI, start=True, stop=False), t, fr[k], inc=False)
                tp = pe.do(lambda e: e.matmul(v8(PB[k][:, :]), w("whhT", 128, g * 128, (g + 1) * 128), sb_, start=False, stop=True))
                fr[k] = ta = act.do(lambda e: e.activation(dst, PB[k][:, :], ACTF.Tanh, bias=bias, scale=0.5), tp, t_bs, hf_free)
                tg.append(ta)
            k = nb()
            tp = pe.do(lambda e: e.matmul(PB[k][:, :], w("wihT", 128, 256, 384), SI, start=True, stop=True), fr[k])
            yield
            t = dve.do(lambda e: e.scalar_tensor_tensor(v8(T1), v8(T1), 1.0, hn.unsqueeze(1).broadcast_to([128, 8, 64]), ALU.add, ALU.mult), tg[0], t_hn)
            fr[k] = t = dve.do(lambda e: e.tensor_tensor(T1, T1, PB[k][:, :], ALU.add), t, tp)
            tn = act.do(lambda e: e.activation(T3, T1, ACTF.Tanh, bias=bih[:, 2:3]), t)
            yield
            t = dve.do(lambda e: e.tensor_tensor(v8(SN), sb_, v8(T3), ALU.subtract), tn)
            t = dve.do(lambda e: e.scalar_tensor_tensor(SN, T2, 1.0, SN, ALU.add, ALU.mult), t, tg[1])
            tsn = dve.do(lambda e: e.scalar_tensor_tensor(SN, SN, 0.5, T3, ALU.mult, ALU.add), t)
            yield
            k = nb()
            tp = pe.do(lambda e: e.matmul(PB[k][0:32, :], w("fwq"), SN, start=True, stop=True), fr[k], tsn)
            fr[k] = tq = act.do(lambda e: e.activation(T1[0:32, :], PB[k][0:32, :], ACTF.Identity, bias=nq[0:32, :], scale=-sc7), tp, t_nq, tn)
            k = nb()
            tp = pe.do(lambda e: e.matmul(PB[k][0:32, :], w("fwk"), SN, start=True, stop=True), fr[k])
            fr[k] = tk = act.do(lambda e: e.activation(T2[0:32, :], PB[k][0:32, :], ACTF.Identity, bias=w("fbk", 32)), tp, tsn)
            kv = nb()
            for p in range(4):
                tv = pe.do(lambda e: e.matmul(PB[kv][:, pairs[p]], SN[:, pairs[p]], w("fwv"), start=True, stop=True), fr[kv], inc=p == 3)
            fr[kv] = tv = dve.do(lambda e: e.tensor_tensor(v4(VV), v4(PB[kv][:, :]), w("fbv").unsqueeze(1).broadcast_to([128, 4, 128]), ALU.add), tv)
            yield
            k = nb()
            for p in range(4):
                tp = pe.do(lambda e: e.matmul(PB[k][:, pairs[p]], T1[0:32, pairs[p]], T2[0:32, pairs[p]], start=True, stop=True), fr[k], tq, tk, inc=p == 3)
            te = []
            for p in range(4):
                fr[k] = t = dve.do(lambda e: e.tensor_tensor_reduce(T3[:, pairs[p]], PB[k][:, pairs[p]], pm, 1.0, 3.0e38, ALU.add, ALU.min, mx7[:, p:p + 1]), tp, tsn)
                te.append(act.do(lambda e: e.activation(T3[:, pairs[p]], T3[:, pairs[p]], ACTF.Exp, bias=mx7[:, p:p + 1], scale=-1.0,
                                                        accum_out=sm7[:, p:p + 1]), t))
            yield
            k = nb()
            for p in range(4):
                tp = pe.do(lambda e: e.transpose(PB[k][:, pairs[p]], T3[:, pairs[p]], ident), te, fr[k], inc=p == 3)
            fr[k] = t = act.do(lambda e: e.activation(SI, PB[k][:, :], ACTF.Copy), tp)
            k = nb()
            for p in range(4):
                ty = pe.do(lambda e: e.transpose(PB[k][:, pairs[p]], SN[:, pairs[p]], ident), fr[k], inc=p == 3)
            fr[k] = ty = act.do(lambda e: e.activation(T1, PB[k][:, :], ACTF.Copy), ty, tp)
            tr = dve.do(lambda e: e.reciprocal(sm7, sm7), te)
            yield
            k = nb()
            for p in range(4):
                tp = pe.do(lambda e: e.matmul(PB[k][:, pairs[p]], SI[:, pairs[p]], VV[:, pairs[p]], start=True, stop=True), t, tv, fr[k], inc=p == 3)
            ta, tb = [], []
            for p in range(4):
                fr[k] = t = dve.do(lambda e: e.scalar_tensor_tensor(T1[:, pairs[p]], PB[k][:, pairs[p]], sm7[:, p:p + 1], T1[:, pairs[p]], ALU.mult, ALU.add), tp, tr, ty)
                ta.append(t)
            ta = [dve.do(lambda e, p=p: e.bn_stats(bn7[:, 6 * p:6 * p + 6], T1[:, pairs[p]]), ta[p]) for p in range(4)]
            for p in range(4):
                tb.append(dve.do(lambda e: e.bn_aggr(mv7[:, 2 * p:2 * p + 2], bn7[:, 6 * p:6 * p + 6]), ta[p]))
            t = pool.do(lambda e: e.tensor_scalar(rs7.unsqueeze(2), mv7.rearrange("p (q s) -> p q s", s=2)[:, :, 1:2], 1e-5, None, ALU.add), tb)
            t = pool.do(lambda e: e.tensor_tensor(rs7, rs7, mhalf, ALU.pow), t)
            yield
            for p in range(4):
                tl = dve.do(lambda e: e.tensor_scalar(T1[:, pairs[p]], T1[:, pairs[p]], mv7[:, 2 * p:2 * p + 1], rs7[:, p:p + 1], ALU.subtract, ALU.mult), t, tb)
            yield
            k = nb()
            for p in range(4):
                tp = pe.do(lambda e: e.transpose(PB[k][:, pairs[p]], T1[:, pairs[p]], ident), tl, fr[k], inc=p == 3)
            fr[k] = t = act.do(lambda e: e.activation(T2, PB[k][:, :], ACTF.Identity, bias=w("flnb"), scale=w("flng")), tp)
            yield
            k = nb()
            for p in range(4):
                tp = pe.do(lambda e: e.matmul(PB[k][:, pairs[p]], T2[:, pairs[p]], wvo, start=True, stop=True), t, t_vo, fr[k], inc=p == 3)
            fr[k] = t = dve.do(lambda e: e.tensor_tensor(v4(VS), v4(PB[k][:, :]), bvo.unsqueeze(1).broadcast_to([128, 4, 128]), ALU.add), tp, t_bvo)
            yield
            for c in (2 * n, 2 * n + 1):
                ks = [nb(), nb()]
                for p in range(2):
                    for hh in range(2):
                        m = 2 * c + p
                        ml = pairs[m % 4]
                        tp = pe.do(lambda e: e.matmul(PB[ks[hh]][:, p * 128:(p + 1) * 128], ATT[64 * hh:64 * hh + 64, m * 128:(m + 1) * 128],
                                                      VS[64 * hh:64 * hh + 64, ml], start=True, stop=True),
                                   t, tatt[c], fr[ks[0]], fr[ks[1]], inc=(p, hh) == (1, 1))
                x4 = cs(XT, c).rearrange("p (q hh t) -> p q hh t", q=2, hh=2)
                tx = []
                for hh in range(2):
                    fr[ks[hh]] = ta = dve.do(lambda e: e.tensor_tensor(x4[:, :, hh, :], x4[:, :, hh, :],
                                                                       PB[ks[hh]][:, 0:256].rearrange("p (q t) -> p q t", q=2), ALU.add), tp, t_bo[c])
                    tx.append(ta)
                sp.wait([tx])
                nc.sync.dma_start(out_d[4 * c:4 * c + 4, :, :].rearrange("b t d -> t b d"), v4(cs(XT, c))).then_inc(s_out, 16)
                yield

        starts, live = [slots(n) for n in range(4)], []
        while starts or live:
            if starts:
                live.append(starts.pop(0))
            for gnr in list(live):
                if next(gnr, "over") == "over":
                    live.remove(gnr)
        nc.sync.wait_ge(s_out, 16 * CH)


def pack(inp):
    f = np.float32
    wide = np.zeros((128, WIDE), f)

    def put(name, a):
        o, c = OFF[name]
        a = np.asarray(a)
        assert a.shape[1] == c, (name, a.shape)
        wide[0:a.shape[0], o:o + c] = a

    def col(name, a):
        put(name, np.asarray(a).reshape(-1, 1))

    def row(name, a, rows=128):
        a = np.asarray(a).reshape(1, -1)
        put(name, np.broadcast_to(a, (rows, a.shape[1])))

    def blocks(a, n):
        a = np.asarray(a)
        return a.reshape(n, 128, a.shape[-1]).transpose(1, 0, 2).reshape(128, -1)

    put("condT", np.asarray(inp["cond_1024"]).T)
    put("w0", inp["L0_cond_weight"])
    put("ident", np.eye(128, dtype=f))
    i, j = np.arange(128)[:, None], np.arange(128)[None, :]
    put("mask", np.where(j > i, f(-NEG), f(0)))
    wqkv = np.asarray(inp["L0_attn_W_qkv"])
    for n, o in (("wqT", 0), ("wkT", 1024), ("wvT", 2048)):
        put(n, wqkv[:, o:o + 1024].reshape(128, 8, 128).transpose(2, 1, 0).reshape(128, 1024))
    put("wout", blocks(inp["L0_attn_W_out"], 8))
    for n, k in (("f", "f"), ("i", "i"), ("h", "h")):
        put(f"w{n}T", np.asarray(inp[f"L0_cond2_W_{k}"]).T)
        col(f"b{n}", inp[f"L0_cond2_b_{k}"])
    for k in (1, 2):
        put(f"cw{k}", inp[f"L0_ffn_cn_w{k}"])
    w3, w4 = np.asarray(inp["L0_ffn_cn_w3"]), np.asarray(inp["L0_ffn_cn_w4"])
    both = np.zeros((128, 64), f)
    both[0:64, 0:32] = w3
    both[64:128, 32:64] = w3
    put("cw3", both)
    both = np.zeros((64, 256), f)
    both[0:32, 0:128] = w4
    both[32:64, 128:256] = w4
    put("cw4", both)
    col("cb1", inp["L0_ffn_cn_b1"])
    col("cb2", np.tile(np.asarray(inp["L0_ffn_cn_b2"]), 2))
    col("cb3", np.tile(np.asarray(inp["L0_ffn_cn_b3"]), 2))
    row("cb4", inp["L0_ffn_cn_b4"])
    for k in (1, 2):
        put(f"gw{k}", inp[f"L0_ffn_gc_w{k}"])
        col(f"gb{k}", inp[f"L0_ffn_gc_b{k}"])
    put("gw3", np.broadcast_to(np.asarray(inp["L0_ffn_gc_w3"]), (32, 128)))
    row("gb3", inp["L0_ffn_gc_b3"])
    row("ar", inp["L0_ffn_adaptive_range"])
    tw = np.zeros((128, 128), f)
    r = np.arange(32)
    tw[64 + r, r] = 1
    tw[96 + r, 32 + r] = -1
    tw[r, 64 + r] = -1
    tw[32 + r, 96 + r] = 1
    put("twist", tw)
    put("gatew", blocks(inp["L1_cond_gate_w"], 3))
    row("gateb", inp["L1_cond_gate_b"], 32)
    put("timew", inp["L1_cond_time_w"])
    row("timeb", inp["L1_cond_time_b"], 32)
    lower = np.zeros((4, 4), f)
    for a in range(4):
        lower[a, :a] = 1
    row("lower", lower, 32)
    put("ew1", np.asarray(inp["L1_cond_ew1"]).transpose(1, 0, 2).reshape(128, 2048))
    put("eb1", np.asarray(inp["L1_cond_eb1"]).reshape(16, 128).T)
    put("ew2", blocks(np.asarray(inp["L1_cond_ew2"]).reshape(2048, 128), 16))
    put("eb2", np.asarray(inp["L1_cond_eb2"]).T)
    put("sw1", inp["L1_cond_sw1"])
    put("sb1", np.asarray(inp["L1_cond_sb1"]).reshape(4, 128).T)
    put("sw2", blocks(inp["L1_cond_sw2"], 4))
    col("sb2", inp["L1_cond_sb2"])
    for n, k in (("q", "q"), ("k", "k")):
        put(f"a{n}", inp[f"L1_attn_W{k}"])
        col(f"b{n}", inp[f"L1_attn_b{k}"])
    put("av", inp["L1_attn_Wv"])
    row("bv", inp["L1_attn_bv"])
    col("gamma", inp["L1_attn_gamma"])
    col("beta", inp["L1_attn_beta"])
    put("hm", (np.arange(128)[:, None] // 8 % 4 == np.arange(4)[None, :]).astype(f))
    put("cond", inp["cond_1024"])
    row("lng", inp["L1_cond2_ln_g"], 32)
    row("lnb", inp["L1_cond2_ln_b"], 32)
    put("lw1", inp["L1_cond2_w1"])
    col("lb1", inp["L1_cond2_b1"])
    w2 = np.asarray(inp["L1_cond2_w2"]).reshape(128, 2, 128, 8).transpose(1, 0, 3, 2)
    put("lw2a", w2[0].reshape(128, 1024))
    put("lw2b", w2[1].reshape(128, 1024))
    b2 = np.asarray(inp["L1_cond2_b2"]).reshape(2, 128, 8)
    put("lb2a", b2[0])
    put("lb2b", np.tile(b2[1].T, (16, 1)))
    put("base", inp["L1_cond2_base_layer"])
    put("bm16", (np.arange(128)[:, None] // 8 == np.arange(16)[None, :]).astype(f))
    w1 = np.asarray(inp["L1_ffn_w1"])
    put("fw1a", w1[:128])
    put("fw1b", w1[128:])
    col("fb1", inp["L1_ffn_b1"])
    put("fw2", np.concatenate([np.asarray(inp["L1_ffn_w2"]), np.asarray(inp["L1_ffn_b2"]).reshape(1, 64)]))
    row("tau", inp["L1_ffn_tau"])
    put("wihT", np.asarray(inp["L1_ffn_Wih"]).T)
    put("whhT", np.asarray(inp["L1_ffn_Whh"]).T)
    put("bih", np.asarray(inp["L1_ffn_bih"]).reshape(3, 128).T)
    put("bhh", np.asarray(inp["L1_ffn_bhh"]).reshape(3, 128).T)
    put("slotT", np.asarray(inp["L1_ffn_slot_init"]).T)
    put("fwq", inp["L1_ffn_wq"])
    col("fbq", inp["L1_ffn_bq"])
    put("fwk", inp["L1_ffn_wk"])
    col("fbk", inp["L1_ffn_bk"])
    put("fwv", inp["L1_ffn_wv"])
    row("fbv", inp["L1_ffn_bv"])
    col("flng", inp["L1_ffn_ln_g"])
    col("flnb", inp["L1_ffn_ln_b"])
    put("wvpT", np.asarray(inp["L1_ffn_wvp"]).T)
    col("bvp", inp["L1_ffn_bvp"])
    put("wo", inp["L1_ffn_wo"])
    row("bo", inp["L1_ffn_bo"])
    put("pmask", np.where(i // 64 == j // 64, f(0), f(-NEG)))
    xT = np.ascontiguousarray(np.asarray(inp["x"]).reshape(N, D).T)
    return {"in_xT": xT, "in_w": wide}


def kernel(**inputs):
    import concourse.bacc as _bacc
    from concourse.bass_utils import run_bass_kernel_spmd as _run

    nc = _bacc.Bacc("TRN2", target_bir_lowering=False, num_devices=1)
    arrays = pack(inputs)
    aps = [nc.dram_tensor(n, a.shape, F32, kind="ExternalInput").ap() for n, a in arrays.items()]
    out = nc.dram_tensor("out_0", (B, T, D), F32, kind="ExternalOutput").ap()
    build(nc, *aps, out)
    r = _run(nc, [arrays], core_ids=[0])
    return r.results[0]["out_0"]
```
